# Optimizing a Trainium2 kernel written in Bass

```python
import numpy as np
import jax
import jax.numpy as jnp

def _softmax(x, axis=-1):
    return jax.nn.softmax(x, axis=axis)

def _gelu(x):
    return jax.nn.gelu(x, approximate=True)

def _silu(x):
    return jax.nn.silu(x)

def _sigmoid(x):
    return jax.nn.sigmoid(x)

def _layernorm(x, axis=-1, eps=1e-05):
    m = jnp.mean(x, axis=axis, keepdims=True)
    v = jnp.var(x, axis=axis, keepdims=True)
    return (x - m) / jnp.sqrt(v + eps)

def _scatter_add(tgt, idx, src, axis=0):
    return tgt.at[idx].add(src)

def _segment_sum(src, seg, n):
    return jax.ops.segment_sum(src, seg, n)
kernel_name = 'mk_adj_preln_d4_adj_r2_9c8d6e'

def setup_inputs(seed: int=0):
    np.random.seed(seed)
    _w = jnp.asarray

    def _rec_inputs():
        import jax
        import jax.numpy as jnp
        _gk = jax.random.key(seed)
        x = -0.0002928 + 1 * jax.random.normal(jax.random.fold_in(_gk, 1), (16, 512, 256), jnp.float32)
        _w = (1.0 + jnp.arange(512, dtype=jnp.float32)) ** (-0.5)
        _w = _w / _w.mean()
        _pij = jnp.clip(0.00390625 * _w[:, None] * _w[None, :], 0.0, 1.0)
        _a = jax.random.uniform(jax.random.fold_in(_gk, 2), (16, 512, 512)) < _pij
        _a = jnp.logical_or(_a, jnp.eye(512, dtype=bool))
        adj = _a.astype(jnp.int32)
        return (x, adj)
    x, adj = _rec_inputs()

    def _L0_gnn_setup():
        import jax, jax.numpy as jnp
        import numpy as np
        B, N, D = (8, 512, 256)
        NH = 8
        DK = D // NH
        key = jax.random.key(seed)
        ks = jax.random.split(key, 6)
        x = jax.random.normal(ks[0], (B, N, D), dtype=jnp.float32)
        adj = jax.random.randint(ks[1], (B, N, N), 0, 2, dtype=jnp.int32)
        adj = jnp.maximum(adj, jnp.eye(N, dtype=jnp.int32)[None])
        s = 1.0 / np.sqrt(D)
        Wq = jax.random.normal(ks[2], (D, D), dtype=jnp.float32) * s
        Wk = jax.random.normal(ks[3], (D, D), dtype=jnp.float32) * s
        Wv = jax.random.normal(ks[4], (D, D), dtype=jnp.float32) * s
        Wo = jax.random.normal(ks[5], (D, D), dtype=jnp.float32) * s
        return {'x': x, 'adj': adj, 'Wq': Wq, 'Wk': Wk, 'Wv': Wv, 'Wo': Wo}
    _L0_gnn_all = _L0_gnn_setup()
    _L0_gnn_in = {k: v for k, v in _L0_gnn_all.items() if k in ('Wq', 'Wk', 'Wv', 'Wo')}
    del _L0_gnn_all

    def _L1_gnn_setup():
        import jax, jax.numpy as jnp
        import numpy as np
        B, N, DIN, DOUT = (8, 1024, 256, 256)
        key = jax.random.key(seed)
        kx, ka, kw, kb, kattn = jax.random.split(key, 5)
        x = jax.random.normal(kx, (B, N, DIN), dtype=jnp.float32)
        adjacency_matrix = jax.random.randint(ka, (B, N, N), 0, 2, dtype=jnp.int32)
        lim_w = float(np.sqrt(1.0 / DIN))
        W = jax.random.uniform(kw, (DOUT, DIN), minval=-lim_w, maxval=lim_w, dtype=jnp.float32)
        b = jax.random.uniform(kb, (DOUT,), minval=-lim_w, maxval=lim_w, dtype=jnp.float32)
        lim_a = float(np.sqrt(6.0 / (DOUT + DOUT)))
        attn = jax.random.uniform(kattn, (DOUT, DOUT), minval=-lim_a, maxval=lim_a, dtype=jnp.float32)
        return {'x': x, 'adjacency_matrix': adjacency_matrix, 'W': W, 'b': b, 'attn': attn}
    _L1_gnn_all = _L1_gnn_setup()
    _L1_gnn_in = {k: v for k, v in _L1_gnn_all.items() if k in ('W', 'b', 'attn')}
    del _L1_gnn_all

    def _L2_gnn_setup():
        import jax, jax.numpy as jnp
        import numpy as np
        B, N, IN_DIM, OUT_DIM, H = (512, 128, 256, 256, 8)
        D = OUT_DIM // H
        key = jax.random.key(seed)
        k1, k2, k3, k4 = jax.random.split(key, 4)
        x = jax.random.normal(k1, (B, N, IN_DIM), dtype=jnp.float32)
        adj = jax.random.randint(k2, (B, N, N), 0, 2, dtype=jnp.int32)
        W = jax.random.normal(k3, (IN_DIM, OUT_DIM), dtype=jnp.float32) / np.sqrt(IN_DIM).astype(np.float32)
        a = jax.random.normal(k4, (H, 2 * D), dtype=jnp.float32) * 0.1
        return {'x': x, 'adj': adj, 'W': W, 'a': a}
    _L2_gnn_all = _L2_gnn_setup()
    _L2_gnn_in = {k: v for k, v in _L2_gnn_all.items() if k in ('W', 'a')}
    del _L2_gnn_all

    def _L3_gnn_setup():
        import jax, jax.numpy as jnp
        import numpy as np
        ALPHA = 0.2

        def _leaky(x):
            return jnp.where(x >= 0, x, ALPHA * x)
        key = jax.random.key(seed)
        k1, k2, k3, k4 = jax.random.split(key, 4)
        B, N, F_in, F_out = (4, 1024, 256, 256)
        h = jax.random.normal(k1, (B, N, F_in), dtype=jnp.float32)
        W = jax.random.normal(k2, (F_in, F_out), dtype=jnp.float32) * 0.05
        a = jax.random.normal(k3, (2 * F_out, 1), dtype=jnp.float32) * 0.05
        adj = jax.random.randint(k4, (B, N, N), 0, 2, dtype=jnp.int32)
        return {'h': h, 'W': W, 'a': a, 'adj': adj}
    _L3_gnn_all = _L3_gnn_setup()
    _L3_gnn_in = {k: v for k, v in _L3_gnn_all.items() if k in ('W', 'a')}
    del _L3_gnn_all
    return {'x': x, 'adj': adj, 'L0_gnn_Wq': _L0_gnn_in['Wq'], 'L0_gnn_Wk': _L0_gnn_in['Wk'], 'L0_gnn_Wv': _L0_gnn_in['Wv'], 'L0_gnn_Wo': _L0_gnn_in['Wo'], 'L1_gnn_W': _L1_gnn_in['W'], 'L1_gnn_b': _L1_gnn_in['b'], 'L1_gnn_attn': _L1_gnn_in['attn'], 'L2_gnn_W': _L2_gnn_in['W'], 'L2_gnn_a': _L2_gnn_in['a'], 'L3_gnn_W': _L3_gnn_in['W'], 'L3_gnn_a': _L3_gnn_in['a']}

def reference(x, adj, L0_gnn_Wq, L0_gnn_Wk, L0_gnn_Wv, L0_gnn_Wo, L1_gnn_W, L1_gnn_b, L1_gnn_attn, L2_gnn_W, L2_gnn_a, L3_gnn_W, L3_gnn_a):
    import jax
    import jax.numpy as jnp

    def _L0_gnn_ref(x, adj, Wq, Wk, Wv, Wo):
        import jax, jax.numpy as jnp
        import numpy as np
        B, N, D = (8, 512, 256)
        NH = 8
        DK = D // NH
        b, n, d = x.shape
        sqrt_dk = jnp.asarray(np.sqrt(DK), dtype=x.dtype)

        def heads(t):
            return t.reshape(b, n, NH, DK).transpose(0, 2, 1, 3)
        q = heads(x @ Wq)
        k = heads(x @ Wk)
        v = heads(x @ Wv)
        scores = jnp.einsum('bhnd,bhmd->bhnm', q, k) / sqrt_dk
        mask = adj.astype(bool)[:, None]
        scores = jnp.where(mask, scores, -jnp.inf)
        attn = jax.nn.softmax(scores, axis=-1)
        out = jnp.einsum('bhnm,bhmd->bhnd', attn, v)
        out = out.transpose(0, 2, 1, 3).reshape(b, n, d)
        return jax.nn.relu(out) @ Wo

    def _L1_gnn_ref(x, adjacency_matrix, W, b, attn):
        import jax, jax.numpy as jnp
        import numpy as np
        B, N, DIN, DOUT = (8, 1024, 256, 256)
        h = jnp.einsum('bni,oi->bno', x, W) + b
        ha = jnp.einsum('bmi,ij->bmj', h, attn)
        scores = jnp.einsum('bmj,bnj->bmn', ha, h)
        scores = jnp.where(adjacency_matrix == 0, -jnp.inf, scores)
        attn_weights = jax.nn.softmax(scores, axis=-1)
        x_out = jnp.einsum('bmn,bnd->bmd', attn_weights, h)
        return jax.nn.elu(x_out)

    def _L2_gnn_ref(x, adj, W, a):
        import jax, jax.numpy as jnp
        import numpy as np
        B, N, IN_DIM, OUT_DIM, H = (512, 128, 256, 256, 8)
        D = OUT_DIM // H
        b, n, _ = x.shape
        h = (x @ W).reshape(b, n, H, D)
        a1, a2 = (a[:, :D], a[:, D:])
        s_i = jnp.einsum('bnhd,hd->bnh', h, a1)
        s_j = jnp.einsum('bnhd,hd->bnh', h, a2)
        e = s_i[:, :, None, :] + s_j[:, None, :, :]
        e = jax.nn.leaky_relu(e, negative_slope=0.2)
        mask = (adj != 0)[..., None]
        e = jnp.where(mask, e, -jnp.inf)
        alpha = jax.nn.softmax(e, axis=2)
        alpha = jnp.nan_to_num(alpha, nan=0.0)
        out = jnp.einsum('bijh,bjhd->bihd', alpha, h).reshape(b, n, OUT_DIM)
        return jax.nn.elu(out)

    def _L3_gnn_ref(h, W, a, adj):
        import jax, jax.numpy as jnp
        import numpy as np
        ALPHA = 0.2

        def _leaky(x):
            return jnp.where(x >= 0, x, ALPHA * x)
        F_out = W.shape[1]
        Wh = jnp.matmul(h, W)
        Wh_sg = jax.lax.stop_gradient(Wh)
        a1 = a[:F_out, 0]
        a2 = a[F_out:, 0]
        s_i = Wh_sg @ a1
        s_j = Wh_sg @ a2
        e = _leaky(s_i[:, :, None] + s_j[:, None, :])
        e = jnp.where(adj > 0, e, jnp.float32(-9000000000000000.0))
        attention = jax.nn.softmax(e, axis=1)
        h_prime = jnp.einsum('bij,bjf->bif', attention, Wh)
        return _leaky(h_prime)
    h = jnp.maximum(_layernorm(x, axis=-1), 0.0)
    x = x + _L0_gnn_ref(h, adj, L0_gnn_Wq, L0_gnn_Wk, L0_gnn_Wv, L0_gnn_Wo)
    h = jnp.maximum(_layernorm(x, axis=-1), 0.0)
    x = x + _L1_gnn_ref(h, adj, L1_gnn_W, L1_gnn_b, L1_gnn_attn)
    h = jnp.maximum(_layernorm(x, axis=-1), 0.0)
    x = x + _L2_gnn_ref(h, adj, L2_gnn_W, L2_gnn_a)
    h = jnp.maximum(_layernorm(x, axis=-1), 0.0)
    x = x + _L3_gnn_ref(h, L3_gnn_W, L3_gnn_a, adj)
    return x

_drawn_inputs = setup_inputs


def setup_inputs(seed=0):
    import zlib

    import numpy as np

    out = dict(_drawn_inputs(seed))
    spreads = {}
    factors = {}
    for name, (base, spread) in spreads.items():
        noise = np.random.default_rng([zlib.crc32(name.encode()), seed]).standard_normal(out[name].shape)
        drawn = base * np.exp(spread * noise) if base else spread * noise
        out[name] = jnp.asarray(drawn.astype(out[name].dtype))
    for name, factor in factors.items():
        out[name] = (out[name] * factor).astype(out[name].dtype)
    return out
```

```python
import math
from contextlib import ExitStack

import numpy as np

import concourse.bass as bass
from concourse import mybir

F32 = mybir.dt.float32
F32R = mybir.dt.float32r
BF16 = mybir.dt.bfloat16
I32 = mybir.dt.int32
ALU = mybir.AluOpType
ACT = mybir.ActivationFunctionType
AX = mybir.AxisListType

P = 128
BATCH = 16
N = 512
D = 256
H = 8
DK = D // H
NT = N // P
C = D // P
G = P // DK
MASKED = 1e30
EPS = 1e-5
SLOPE = 0.2
L0_BLOCKS = H * NT
BLOCKS = L0_BLOCKS + NT
STACK = 16 * 4 * G
CONSTS = 11
LAG = 2
MATRICES = ["Wq", "Wk", "Wv", "Wo", "W1T", "attn", "W2", "W3"]


class Signal:

    def __init__(self, sem, per):
        self.sem, self.per = sem, per

    def at(self, b, k):
        return b * self.per + k


def later(b, n):
    return not isinstance(b, int) or b >= n


class Stream:
    pass


def interleave(first, second):
    out, done = [], [0, 0]
    streams = [list(first), list(second)]
    total = [max(1e-9, sum(w for *_, w in s)) for s in streams]
    while streams[0] or streams[1]:
        s = 0 if streams[0] and (not streams[1] or done[0] / total[0] <= done[1] / total[1]) else 1
        *step, w = streams[s].pop(0)
        done[s] += w
        out.append(tuple(step))
    return out


def steps_a():
    yield ("A", "load", 0, 0)
    yield ("A", "norm", 0, 1)
    for j in range(2 * C):
        yield ("A", "qk", j, 1.3)
    yield ("A", "v", 0, 2.6)
    for k in range(L0_BLOCKS + LAG):
        if k < L0_BLOCKS:
            yield ("A", "score0", k, 0.45)
        if k >= LAG:
            yield ("A", "turn", k - LAG, 0.5)
            if (k - LAG) % G == G - 1:
                yield ("A", "pv0", (k - LAG) // G, 1)
            if (k - LAG) % (G * NT) == G * NT - 1:
                yield ("A", "out0", (k - LAG) // (G * NT), 0.5)
    yield ("A", "wo", 0, 4)
    yield ("A", "norm", 1, 2)
    yield ("A", "h1", 0, 2.6)
    for j in range(2 * C):
        yield ("A", "proj1", j, 1.3)
    for m in range(NT + LAG):
        if m < NT:
            yield ("A", "score1", m, 2.8)
        if m >= LAG:
            yield ("A", "turn", L0_BLOCKS + m - LAG, 0.5)
    yield ("A", "pv1", 0, 7)


def steps_b():
    yield ("B", "masks", 0, 1)
    yield ("B", "norm", 0, 1)
    yield ("B", "sums2", 0, 1.5)
    yield ("B", "v2", 0, 2.6)
    yield ("B", "factors", 0, 2)
    for u in range(C * NT):
        if u % NT == 0:
            for g in range(G):
                yield ("B", "spread", u // NT * G + g, 0.5)
            if u:
                yield ("B", "out2", 0, 1)
        yield ("B", "weights2", u, 0.5)
        yield ("B", "pv2", u, 2)
    yield ("B", "out2", C - 1, 1)
    yield ("B", "elu2", 0, 1)
    yield ("B", "norm", 1, 2)
    yield ("B", "sums3", 0, 3)
    yield ("B", "v3", 0, 2.6)
    for j in range(NT):
        yield ("B", "edges3", j, 1)
    yield ("B", "pv3", 0, 7)
    yield ("B", "store", 0, 0)


def build(nc, x, adj, Wq, Wk, Wv, Wo, W1, b1, attn, W2, a2, W3, a3, out):
    x_dram = x.rearrange("b (t p) d -> b p t d", p=P)
    adj_dram = adj.rearrange("b (t p) m -> b p t m", p=P)
    out_dram = out.rearrange("b (t p) d -> b p t d", p=P)

    ctx = ExitStack()
    with ctx:
        def sb(name, shape, dt=F32):
            return ctx.enter_context(nc.sbuf_tensor(name, shape, dt))

        def signal(name, per=1):
            return Signal(ctx.enter_context(nc.semaphore(name)), per)

        ident = sb("ident", [P, P])
        ident_bf = sb("ident_bf", [P, P], BF16)
        pick = sb("pick", [2 * DK, H, P], F32R)
        halves = sb("halves", [P, NT])
        pool_tick = sb("pool_tick", [P, 1])
        dve_tick = sb("dve_tick", [P, 1])
        coef = sb("coef", [P, 1])
        w_hi = {m: sb(f"{m}_hi", [P, C, D], F32R) for m in MATRICES}
        w_lo = {m: sb(f"{m}_lo", [P, C, D], F32R) for m in MATRICES}
        wa2_hi = sb("wa2_hi", [P, C, P], F32R)
        wa2_lo = sb("wa2_lo", [P, C, P], F32R)
        wi3_hi = sb("wi3_hi", [P, C, P], F32R)
        wi3_lo = sb("wi3_lo", [P, C, P], F32R)
        wj3_hi = sb("wj3_hi", [P, C, 2], F32R)
        wj3_lo = sb("wj3_lo", [P, C, 2], F32R)
        b1_row = sb("b1_row", [P, D])
        b1_col = sb("b1_col", [P, C])

        x_in = sb("x_in", [P, NT, D])
        adj_in = sb("adj_in", [P, NT // 2, N], I32)
        mask = [sb(f"mask{s}", [P, NT, N], BF16) for s in range(2)]
        x_mid = [sb(f"x_mid{s}", [P, NT, D]) for s in range(2)]

        A, B = Stream(), Stream()
        for S, name in ((A, "A"), (B, "B")):
            S.name = name
            S.stats = sb(f"{name}_stats", [P, NT, 6])
            S.meanvar = sb(f"{name}_meanvar", [P, NT, 2])
            S.vareps = sb(f"{name}_vareps", [P, NT])
            S.rstd = sb(f"{name}_rstd", [P, NT])
            S.xn = sb(f"{name}_xn", [P, NT, D])
            S.hT_hi = sb(f"{name}_hT_hi", [P, C, N], F32R)
            S.hT_lo = sb(f"{name}_hT_lo", [P, C, N], F32R)
            S.val = sb(f"{name}_val", [P, NT, D])
            S.probsT = sb(f"{name}_probsT", [P, 2 * G, N])
            S.oT = sb(f"{name}_oT", [P, N])
            S.e = S.xn
            S.pair = ctx.enter_context(nc.psum_tensor(f"{name}_pair", [P, 2 * N], F32))
            S.bank = [ctx.enter_context(nc.psum_tensor(f"{name}_bank{i}", [P, N], F32)) for i in range(2)]
        B.y = sb("B_y", [P, NT, D])
        qk_hi = sb("qk_hi", [P, 2, N], F32R)
        qk_lo = sb("qk_lo", [P, 2, N], F32R)
        q_stack = sb("q_stack", [P, H, N], F32R)
        k_stack = sb("k_stack", [P, H, N], F32R)
        h1_hi, h1_lo = q_stack, k_stack
        probs = sb("probs", [P, 3, N])
        A.y = probs[:, 0:2, :].rearrange("p a (t d) -> p (a t) d", d=D)
        neg_max = sb("neg_max", [P, BLOCKS])
        den = sb("den", [P, BLOCKS])
        rden = sb("rden", [P, BLOCKS])
        adjT = sb("adjT", [P, NT, N], BF16)
        maskT = adjT
        cmax = sb("cmax", [P, 1])
        cbias = sb("cbias", [P, 1])
        rgf = sb("rgf", [3 * DK, N])
        r_split = sb("r_split", [2 * DK, N], F32R)
        r_all = sb("r_all", [P, G, N])
        gf = sb("gf", [P, NT, 2 * DK])
        dT = sb("dT", [P, N])
        rden2 = sb("rden2", [P, C, NT * G])
        sj3 = sb("sj3", [P, NT * 2])
        max3 = sb("max3", [P, NT])
        neg3 = sb("neg3", [P, NT])
        den3 = sb("den3", [P, NT])
        rden3 = sb("rden3", [P, NT])

        weights_in = signal("weights_in")
        consts = signal("consts")
        set_v = signal("set_v")
        w1_turned = signal("w1_turned")
        ready = signal("ready")
        x_loaded = signal("x_loaded", 16)
        adj_loaded = signal("adj_loaded", 32)
        mask_ready = signal("mask_ready", 2)
        stacked = [signal(f"{n}_stacked", C * STACK) for n in "qk"]
        stored = signal("stored", 16)
        for S, norms, turns in ((A, 2, 3), (B, 2, 2)):
            n = S.name
            S.stat = signal(f"{n}_stat", norms)
            S.aggr = signal(f"{n}_aggr", norms)
            S.eps_in = signal(f"{n}_eps_in", norms)
            S.rstd_ok = signal(f"{n}_rstd_ok", norms)
            S.normed = signal(f"{n}_normed", norms)
            S.hT_psum = signal(f"{n}_hT_psum", turns)
            S.hT_hi_ok = signal(f"{n}_hT_hi_ok", turns)
            S.hT_lo_ok = signal(f"{n}_hT_lo_ok", turns)
            S.v_psum = signal(f"{n}_v_psum")
            S.v_ok = signal(f"{n}_v_ok")
            S.pv = signal(f"{n}_pv", C)
            S.oT_ok = signal(f"{n}_oT_ok", C)
            S.o_psum = signal(f"{n}_o_psum", C)
            S.rd = signal(f"{n}_rd", C)
            S.o_ok = signal(f"{n}_o_ok", C)
            S.clip = signal(f"{n}_clip")
            S.exped = signal(f"{n}_exped")
            S.elu = signal(f"{n}_elu")
            S.x_ok = signal(f"{n}_x_ok")
        qk_psum = signal("qk_psum", 2 * C)
        qk_hi_ok = signal("qk_hi_ok", 2 * C)
        qk_lo_ok = signal("qk_lo_ok", 2 * C)
        scored = signal("scored", BLOCKS)
        maxed = signal("maxed", BLOCKS)
        exps = signal("exps", BLOCKS)
        turned = signal("turned", BLOCKS)
        kept = signal("kept", BLOCKS)
        wo_psum = signal("wo_psum")
        res0 = signal("res0")
        h1_psum = signal("h1_psum")
        h1_ok = signal("h1_ok")
        p1_psum = signal("p1_psum", 2 * C)
        p1_hi_ok = signal("p1_hi_ok", 2 * C)
        p1_lo_ok = signal("p1_lo_ok", 2 * C)
        o1_psum = signal("o1_psum")
        rd1 = signal("rd1")
        y1_ok = signal("y1_ok")
        mT_psum = signal("mT_psum", NT)
        maskT_ok = signal("maskT_ok")
        adjT_ok = signal("adjT_ok", NT)
        s2_psum = signal("s2_psum")
        cmax_part = signal("cmax_part", 2)
        cbias_ok = signal("cbias_ok")
        rgf_ok = signal("rgf_ok")
        r_hi = signal("r_hi")
        r_ok = signal("r_ok")
        gf_psum = signal("gf_psum")
        gf_ok = signal("gf_ok")
        r_psum = signal("r_psum", H)
        r_all_ok = signal("r_all_ok", H)
        w2_ok = signal("w2_ok", C * NT)
        w2_used = signal("w2_used", C * NT)
        s3_psum = signal("s3_psum")
        sj3_ok = signal("sj3_ok")
        v3_psum = signal("v3_psum")
        v3_ok = signal("v3_ok")
        u3 = signal("u3", NT)
        leaky3 = signal("leaky3", NT)
        masked3 = signal("masked3", NT)
        neg3_ok = signal("neg3_ok", NT)
        att3 = signal("att3", NT)
        rd3 = signal("rd3")
        val3_ok = signal("val3_ok")
        o3_psum = signal("o3_psum")
        y3_ok = signal("y3_ok")
        leaky_out = signal("leaky_out")
        final_ok = signal("final_ok")

        raw = A.probsT[:, :, :].rearrange("p w (c d) -> p w c d", c=C)
        raw2 = B.probsT[:, :, :].rearrange("p w n -> p (w n)")
        a2_bc = raw2[:, 0:2 * D].rearrange("p (h s d) -> p h s d", h=H, s=2)
        a3_bc = raw2[:, 2 * D:4 * D].rearrange("p (s d) -> p s d", s=2)
        prod = raw2[:, 4 * D:6 * D].rearrange("p (c d) -> p c d", c=C)
        wa2 = raw2[:, 2048:2048 + C * P].rearrange("p (c m) -> p c m", c=C)
        wi3 = raw2[:, 2304:2304 + C * P].rearrange("p (c m) -> p c m", c=C)
        wj3 = raw2[:, 2560:2560 + C * 2].rearrange("p (c m) -> p c m", c=C)
        pick_f = raw2[0:2 * DK, 3072:3072 + H * P].rearrange("p (h m) -> p h m", h=H)
        n_raw = len(MATRICES)

        def batches(engine, steps):
            def both(b, s):
                for stream, name, k in interleave(steps_a(), steps_b()):
                    if (stream, name) in steps:
                        if stream == "A":
                            steps[stream, name](b, s, k)
                        else:
                            steps[stream, name](b - 1, 1 - s, k)
            for stream, name, k in interleave(steps_a(), []):
                if (stream, name) in steps:
                    steps[stream, name](0, 0, k)
            both(1, 1)
            with engine.Fori(1, BATCH // 2) as i:
                both(2 * i, 0)
                both(2 * i + 1, 1)
            for stream, name, k in interleave([], steps_b()):
                if (stream, name) in steps:
                    steps[stream, name](BATCH - 1, (BATCH - 1) % 2, k)

        def hold_dve(dve):
            dve.memset(dve_tick[:, :], 0.0)

        def hold_pool(pool):
            pool.tensor_tensor(pool_tick[:, :], halves[:, 0:1], halves[:, 0:1], ALU.add)

        block = ctx.enter_context(nc.Block())

        @block.sync
        def _(sp):
            for i, w in enumerate([Wq, Wk, Wv, Wo, W1, attn, W2, W3]):
                sp.dma_start(raw[:, i, :, :], w.rearrange("(c p) d -> p c d", p=P)).then_inc(weights_in.sem, 16)
            sp.dma_start(b1_col[:, :], b1.rearrange("(c p) -> p c", p=P), allow_slow_non_contiguous=True
                         ).then_inc(weights_in.sem, 16)
            sp.dma_start(b1_row[:, :], b1.rearrange("(o d) -> o d", o=1).broadcast_to([P, D])).then_inc(weights_in.sem, 16)
            sp.dma_start(raw2[:, 0:2 * D], a2.rearrange("h d -> (h d)").rearrange("(o d) -> o d", o=1).broadcast_to([P, 2 * D])).then_inc(weights_in.sem, 16)
            sp.dma_start(raw2[:, 2 * D:4 * D], a3.rearrange("d o -> o d").broadcast_to([P, 2 * D])).then_inc(weights_in.sem, 16)

            def load(b, s, k):
                if later(b, 1):
                    sp.wait_ge(res0.sem, res0.at(b, 0))
                sp.dma_start(x_in[:, :, :], x_dram[b]).then_inc(x_loaded.sem, 16)
                for half in range(2):
                    if later(b, 1) or half:
                        sp.wait_ge(mask_ready.sem, mask_ready.at(b, half))
                    sp.dma_start(adj_in[:, :, :], adj_dram[b, :, half * 2:half * 2 + 2, :]).then_inc(adj_loaded.sem, 16)

            def stack(b, s, j):
                c, which = j // 2, j % 2
                hi, lo = qk_hi[:, which, :], qk_lo[:, which, :]
                dst, parts = ((q_stack, (hi, hi, lo, lo)), (k_stack, (hi, lo, hi, lo)))[which]
                if j == 0:
                    if later(b, 1):
                        sp.wait_ge(scored.sem, scored.at(b - 1, BLOCKS))
                sp.wait_ge(qk_hi_ok.sem, qk_hi_ok.at(b, j + 1))
                sp.wait_ge(qk_lo_ok.sem, qk_lo_ok.at(b, j + 1))
                for r, part in enumerate(parts):
                    for g in range(G):
                        sp.dma_start(dst[DK * r:DK * (r + 1), G * c + g, :].bitcast(F32),
                                     part[DK * g:DK * (g + 1), :].bitcast(F32)).then_inc(stacked[which].sem, 16)

            batches(sp, {("A", "load"): load, ("A", "qk"): stack})

        @block.gpsimd
        def _(pool):
            pool.memset(ident[:, :], 0.0).then_inc(consts.sem, 1)
            pool.memset(pick_f, 0.0).then_inc(consts.sem, 1)
            pool.memset(wa2, 0.0).then_inc(consts.sem, 1)
            pool.memset(halves[:, :], -0.5).then_inc(consts.sem, 1)
            for q, exponent in enumerate((SLOPE - 1, 1 - SLOPE, SLOPE)):
                pool.wait_ge(consts.sem, 4 + q)
                pool.memset(coef[q * DK:(q + 1) * DK, :], exponent).then_inc(consts.sem, 1)
            pool.wait_ge(consts.sem, 7)
            pool.affine_select(out=ident[:, :], in_=ident[:, :], compare_op=ALU.not_equal, fill=1.0,
                               base=0, pattern=[[-1, P]], channel_multiplier=1).then_inc(consts.sem, 1)
            pool.affine_select(out=pick_f, in_=pick_f, compare_op=ALU.not_equal, fill=1.0,
                               base=0, pattern=[[-1, H], [0, P]], channel_multiplier=1).then_inc(consts.sem, 1)
            pool.wait_ge(consts.sem, 9)
            pool.affine_select(out=pick_f, in_=pick_f, compare_op=ALU.not_equal, fill=1.0,
                               base=-DK, pattern=[[-1, H], [0, P]], channel_multiplier=1).then_inc(consts.sem, 1)
            pool.tensor_copy(ident_bf[:, :], ident[:, :]).then_inc(consts.sem, 1)

            def load(b, s, k):
                if later(b, 2):
                    pool.wait_ge(mT_psum.sem, mT_psum.at(b - 2, NT))
                for half in range(2):
                    pool.wait_ge(adj_loaded.sem, adj_loaded.at(b, 16 * (half + 1)))
                    hold_pool(pool)
                    pool.tensor_scalar(mask[s][:, half * 2:half * 2 + 2, :], adj_in[:, :, :], -1.0, MASKED,
                                       ALU.add, ALU.mult).then_inc(mask_ready.sem, 1)

            def rstd(S):
                def norm(b, s, k):
                    pool.wait_ge(S.eps_in.sem, S.eps_in.at(b, k + 1))
                    pool.tensor_tensor(S.rstd[:, :], S.vareps[:, :], halves[:, :], ALU.pow).then_inc(S.rstd_ok.sem, 1)
                return norm

            def edge_mask(b, s, k):
                pool.wait_ge(w2_ok.sem, w2_ok.at(b, C * NT))
                hold_pool(pool)
                pool.tensor_scalar(maskT[:, :, :], adjT[:, :, :], -1.0, MASKED,
                                   ALU.add, ALU.mult).then_inc(maskT_ok.sem, 1)

            def store(b, s, k):
                pool.wait_ge(final_ok.sem, final_ok.at(b, 1))
                pool.dma_start(out_dram[b], x_mid[s][:, :, :]).then_inc(stored.sem, 16)

            batches(pool, {("A", "load"): load, ("A", "norm"): rstd(A), ("B", "norm"): rstd(B),
                           ("B", "elu2"): edge_mask, ("B", "store"): store})
            pool.wait_ge(stored.sem, stored.at(BATCH - 1, 16))

        @block.tensor
        def _(pe):
            def three(psum, lhs, rhs, first=True, last=True):
                n = len(lhs)
                for c in range(n):
                    (lh, ll), (rh, rl) = lhs[c], rhs[c]
                    for i, (l, r) in enumerate(((lh, rh), (lh, rl), (ll, rh))):
                        mm = pe.matmul(psum, l, r, start=first and c == 0 and i == 0,
                                       stop=last and c == n - 1 and i == 2)
                return mm

            def cols(hi, lo, a, z):
                return [(hi[:, c, a:z], lo[:, c, a:z]) for c in range(C)]

            pe.wait_ge(weights_in.sem, 16 * (n_raw + 4))
            pe.wait_ge(consts.sem, CONSTS)
            for oc in range(C):
                for ic in range(C):
                    mm = pe.transpose(A.pair[:, ic * D + oc * P:ic * D + (oc + 1) * P],
                                      raw[:, 4, oc, ic * P:(ic + 1) * P], ident[:, :])
            mm.then_inc(w1_turned.sem, 1)
            pe.wait_ge(ready.sem, 1)

            def turn_norm(S, b, k):
                for c in range(C):
                    for t in range(NT):
                        mm = pe.transpose(S.pair[:, c * N + t * P:c * N + (t + 1) * P],
                                          S.xn[:, t, c * P:(c + 1) * P], ident[:, :])
                mm.then_inc(S.hT_psum.sem, 1)

            def halves_in(S, b, k):
                pe.wait_ge(S.hT_hi_ok.sem, S.hT_hi_ok.at(b, k))
                pe.wait_ge(S.hT_lo_ok.sem, S.hT_lo_ok.at(b, k))

            def values(S, b, wh, wl):
                for t in range(NT):
                    mm = three(S.pair[:, t * D:(t + 1) * D], cols(S.hT_hi, S.hT_lo, t * P, (t + 1) * P),
                               cols(wh, wl, 0, D))
                return mm

            def norm_a(b, s, k):
                pe.wait_ge(A.normed.sem, A.normed.at(b, k + 1))
                if k == 0:
                    if later(b, 1):
                        pe.wait_ge(y1_ok.sem, y1_ok.at(b - 1, 1))
                turn_norm(A, b, k)

            def qk(b, s, j):
                if j == 0:
                    halves_in(A, b, 1)
                if j >= 2:
                    pe.wait_ge(qk_hi_ok.sem, qk_hi_ok.at(b, j - 1))
                    pe.wait_ge(qk_lo_ok.sem, qk_lo_ok.at(b, j - 1))
                w = ("Wq", "Wk")[j % 2]
                c = j // 2
                three(A.pair[:, (j % 2) * N:(j % 2 + 1) * N], cols(w_hi[w], w_lo[w], c * P, (c + 1) * P),
                      cols(A.hT_hi, A.hT_lo, 0, N)).then_inc(qk_psum.sem, 1)

            def v(b, s, k):
                pe.wait_ge(qk_hi_ok.sem, qk_hi_ok.at(b, 2 * C))
                pe.wait_ge(qk_lo_ok.sem, qk_lo_ok.at(b, 2 * C))
                values(A, b, w_hi["Wv"], w_lo["Wv"]).then_inc(A.v_psum.sem, 1)

            def score0(b, s, k):
                c, t, g = k // (G * NT), k // G % NT, k % G
                h = G * c + g
                if k % (G * NT) == 0:
                    for which in stacked:
                        pe.wait_ge(which.sem, which.at(b, STACK * (c + 1)))
                if k == 0:
                    pe.wait_ge(A.v_ok.sem, A.v_ok.at(b, 1))
                    pe.wait_ge(mask_ready.sem, mask_ready.at(b, 2))
                if k >= 2:
                    pe.wait_ge(exps.sem, exps.at(b, k - 1))
                bank = A.pair[:, (k % 2) * N:(k % 2 + 1) * N]
                pe.matmul(bank, q_stack[:, h, t * P:(t + 1) * P], k_stack[:, h, :], start=True, stop=False)
                pe.matmul(bank, ident_bf[:, :], mask[s][:, t, :], start=False, stop=True).then_inc(scored.sem, 1)

            def turn(b, s, k):
                pe.wait_ge(exps.sem, exps.at(b, k + 1))
                if k > 0:
                    pe.wait_ge(kept.sem, kept.at(b, k))
                if k == G * NT or k == L0_BLOCKS:
                    pe.wait_ge(A.o_ok.sem, A.o_ok.at(b, k // (G * NT)))
                for m in range(NT):
                    mm = pe.transpose(A.bank[0][:, m * P:(m + 1) * P], probs[:, k % 3, m * P:(m + 1) * P],
                                      ident[:, :])
                mm.then_inc(turned.sem, 1)

            def turn_back(dst, src):
                for t in range(NT):
                    mm = pe.transpose(dst[:, t * P:(t + 1) * P], src[:, t * P:(t + 1) * P], ident[:, :])
                return mm

            def pv0(b, s, u):
                c, t = u // NT, u % NT
                pe.wait_ge(kept.sem, kept.at(b, G * (u + 1)))
                for m in range(NT):
                    for g in range(G):
                        h = G * c + g
                        mm = pe.matmul(A.bank[1][DK * g:DK * (g + 1), t * P:(t + 1) * P],
                                       A.val[:, m, h * DK:(h + 1) * DK],
                                       A.probsT[:, u % 2 * G + g, m * P:(m + 1) * P], start=m == 0, stop=m == NT - 1)
                if t == NT - 1:
                    mm.then_inc(A.pv.sem, 1)

            def out0(b, s, c):
                pe.wait_ge(A.oT_ok.sem, A.oT_ok.at(b, c + 1))
                turn_back(A.bank[0], A.oT).then_inc(A.o_psum.sem, 1)

            def wo(b, s, k):
                pe.wait_ge(A.o_ok.sem, A.o_ok.at(b, C))
                pe.wait_ge(exps.sem, exps.at(b, L0_BLOCKS))
                turn_norm(A, b, 1)
                halves_in(A, b, 2)
                values(A, b, w_hi["Wo"], w_lo["Wo"]).then_inc(wo_psum.sem, 1)

            def h1(b, s, k):
                halves_in(A, b, 3)
                values(A, b, w_hi["W1T"], w_lo["W1T"]).then_inc(h1_psum.sem, 1)

            def proj1(b, s, j):
                c = j % C
                bank = A.pair[:, c * N:(c + 1) * N]
                if j < C:
                    if j == 0:
                        pe.wait_ge(h1_ok.sem, h1_ok.at(b, 1))
                    three(bank, cols(w_hi["W1T"], w_lo["W1T"], c * P, (c + 1) * P),
                          cols(A.hT_hi, A.hT_lo, 0, N)).then_inc(p1_psum.sem, 1)
                else:
                    pe.wait_ge(p1_hi_ok.sem, p1_hi_ok.at(b, C))
                    pe.wait_ge(p1_lo_ok.sem, p1_lo_ok.at(b, C))
                    three(bank, cols(w_hi["attn"], w_lo["attn"], c * P, (c + 1) * P),
                          [(h1_hi[:, i, :], h1_lo[:, i, :]) for i in range(C)]).then_inc(p1_psum.sem, 1)

            def score1(b, s, m):
                if m == 0:
                    pe.wait_ge(p1_hi_ok.sem, p1_hi_ok.at(b, 2 * C))
                    pe.wait_ge(p1_lo_ok.sem, p1_lo_ok.at(b, 2 * C))
                if m >= 2:
                    pe.wait_ge(exps.sem, exps.at(b, L0_BLOCKS + m - 1))
                bank = A.pair[:, (m % 2) * N:(m % 2 + 1) * N]
                three(bank, [(h1_hi[:, C + c, m * P:(m + 1) * P], h1_lo[:, C + c, m * P:(m + 1) * P]) for c in range(C)],
                      [(h1_hi[:, c, :], h1_lo[:, c, :]) for c in range(C)], last=False)
                pe.matmul(bank, ident_bf[:, :], mask[s][:, m, :], start=False, stop=True).then_inc(scored.sem, 1)

            def rows_product(S, weights, value):
                for i in range(NT):
                    for j in range(NT):
                        mm = pe.matmul(S.pair[:, i * D:(i + 1) * D], weights(i, j),
                                       value[:, j, :], start=j == 0, stop=j == NT - 1)
                return mm

            def pv1(b, s, k):
                pe.wait_ge(kept.sem, kept.at(b, BLOCKS))
                rows_product(A, lambda i, j: A.probsT[:, i, j * P:(j + 1) * P], A.val).then_inc(o1_psum.sem, 1)

            def masks(b, s, k):
                for m in range(NT):
                    bank = B.bank[m % 2][:, :].bitcast(BF16)
                    if m >= 2:
                        pe.wait_ge(adjT_ok.sem, adjT_ok.at(b, m - 1))
                    if m == 0:
                        pe.wait_ge(mask_ready.sem, mask_ready.at(b, 2))
                    for t in range(NT):
                        mm = pe.transpose(bank[:, t * P:(t + 1) * P], mask[s][:, t, m * P:(m + 1) * P], ident_bf[:, :])
                    mm.then_inc(mT_psum.sem, 1)

            def norm_b(b, s, k):
                pe.wait_ge(B.normed.sem, B.normed.at(b, k + 1))
                if k == 0:
                    if later(b, 1):
                        pe.wait_ge(y3_ok.sem, y3_ok.at(b - 1, 1))
                turn_norm(B, b, k)

            def sums2(b, s, k):
                halves_in(B, b, 1)
                pe.wait_ge(adjT_ok.sem, adjT_ok.at(b, NT))
                three(B.bank[0][:, :], cols(wa2_hi, wa2_lo, 0, P), cols(B.hT_hi, B.hT_lo, 0, N)).then_inc(s2_psum.sem, 1)

            def v2(b, s, k):
                values(B, b, w_hi["W2"], w_lo["W2"]).then_inc(B.v_psum.sem, 1)

            def factors(b, s, k):
                pe.wait_ge(rgf_ok.sem, rgf_ok.at(b, 1))
                for t in range(NT):
                    mm = pe.transpose(B.bank[1][:, t * 3 * DK:(t + 1) * 3 * DK], rgf[:, t * P:(t + 1) * P],
                                      ident[0:3 * DK, 0:3 * DK])
                mm.then_inc(gf_psum.sem, 1)

            def spread(b, s, h):
                if h == 0:
                    pe.wait_ge(r_ok.sem, r_ok.at(b, 1))
                    pe.wait_ge(B.v_ok.sem, B.v_ok.at(b, 1))
                if h >= 2:
                    pe.wait_ge(r_all_ok.sem, r_all_ok.at(b, h - 1))
                pe.matmul(B.pair[:, (h % 2) * N:(h % 2 + 1) * N], pick[:, h, :], r_split[:, :],
                          start=True, stop=True).then_inc(r_psum.sem, 1)

            def pv2(b, s, u):
                c, j = u // NT, u % NT
                pe.wait_ge(w2_ok.sem, w2_ok.at(b, u + 1))
                if u == 0:
                    pe.wait_ge(gf_ok.sem, gf_ok.at(b, 1))
                if u == NT:
                    pe.wait_ge(B.oT_ok.sem, B.oT_ok.at(b, 1))
                for bank, stationary in ((B.bank[0], lambda h: B.val[:, j, h * DK:(h + 1) * DK]),
                                         (B.bank[1], lambda h: gf[:, j, DK + h:DK + h + 1].broadcast_to([P, DK]))):
                    for g in range(G):
                        mm = pe.matmul(bank[DK * g:DK * (g + 1), :], stationary(G * c + g),
                                       B.probsT[:, u % 2 * G + g, :], start=j == 0, stop=j == NT - 1)
                mm.then_inc(w2_used.sem, 1)

            def out2(b, s, c):
                pe.wait_ge(B.oT_ok.sem, B.oT_ok.at(b, c + 1))
                if c == 0:
                    pe.wait_ge(r_all_ok.sem, r_all_ok.at(b, H))
                else:
                    pe.wait_ge(B.o_ok.sem, B.o_ok.at(b, c))
                turn_back(B.pair[:, 0:N], B.oT)
                turn_back(B.pair[:, N:2 * N], dT).then_inc(B.o_psum.sem, 1)

            def sums3(b, s, k):
                halves_in(B, b, 2)
                three(B.bank[0][:, :], cols(wi3_hi, wi3_lo, 0, P), cols(B.hT_hi, B.hT_lo, 0, N))
                for t in range(NT):
                    mm = three(B.bank[1][:, 2 * t:2 * t + 2], cols(B.hT_hi, B.hT_lo, t * P, (t + 1) * P),
                               cols(wj3_hi, wj3_lo, 0, 2))
                mm.then_inc(s3_psum.sem, 1)

            def v3(b, s, k):
                values(B, b, w_hi["W3"], w_lo["W3"]).then_inc(v3_psum.sem, 1)

            def pv3(b, s, k):
                pe.wait_ge(att3.sem, att3.at(b, NT))
                pe.wait_ge(val3_ok.sem, val3_ok.at(b, 1))
                rows_product(B, lambda i, j: B.probsT[:, j, i * P:(i + 1) * P], B.val).then_inc(o3_psum.sem, 1)

            batches(pe, {("A", "norm"): norm_a, ("A", "qk"): qk, ("A", "v"): v, ("A", "score0"): score0,
                         ("A", "turn"): turn, ("A", "pv0"): pv0, ("A", "out0"): out0, ("A", "wo"): wo, ("A", "h1"): h1,
                         ("A", "proj1"): proj1, ("A", "score1"): score1, ("A", "pv1"): pv1,
                         ("B", "masks"): masks, ("B", "norm"): norm_b, ("B", "sums2"): sums2,
                         ("B", "v2"): v2, ("B", "factors"): factors, ("B", "spread"): spread,
                         ("B", "pv2"): pv2, ("B", "out2"): out2, ("B", "sums3"): sums3, ("B", "v3"): v3, ("B", "pv3"): pv3})

        @block.scalar
        def _(act):
            def upper(S, b, k):
                act.wait_ge(S.hT_psum.sem, S.hT_psum.at(b, k))
                act.activation(S.hT_hi[:, :, :].rearrange("p c n -> p (c n)"), S.pair[:, :], ACT.Relu).then_inc(S.hT_hi_ok.sem, 1)

            def norm_a(b, s, k):
                upper(A, b, 1 + 2 * k)

            def qk(b, s, j):
                which = j % 2
                if later(b, 1) or j // 2:
                    act.wait_ge(stacked[which].sem, stacked[which].at(b, STACK * (j // 2)))
                act.wait_ge(qk_psum.sem, qk_psum.at(b, j + 1))
                act.activation(qk_hi[:, which, :], A.pair[:, which * N:(which + 1) * N], ACT.Copy).then_inc(qk_hi_ok.sem, 1)

            def v(b, s, k):
                act.wait_ge(A.v_psum.sem, A.v_psum.at(b, 1))
                act.activation(A.val[:, :, :].rearrange("p t d -> p (t d)"), A.pair[:, :], ACT.Copy).then_inc(A.v_ok.sem, 1)

            def exp_block(b, k):
                act.wait_ge(maxed.sem, maxed.at(b, k + 1))
                if k >= 3:
                    act.wait_ge(turned.sem, turned.at(b, k - 2))
                act.activation(probs[:, k % 3, :], A.pair[:, (k % 2) * N:(k % 2 + 1) * N], ACT.Exp,
                               bias=neg_max[:, k:k + 1], accum_out=den[:, k:k + 1]).then_inc(exps.sem, 1)

            def score0(b, s, k):
                exp_block(b, k)

            def score1(b, s, m):
                exp_block(b, L0_BLOCKS + m)

            def turn(b, s, k):
                slot = k % (2 * G)
                act.wait_ge(turned.sem, turned.at(b, k + 1))
                act.activation(A.probsT[:, slot, :], A.bank[0][:, :], ACT.Copy).then_inc(kept.sem, 1)

            def out0(b, s, c):
                act.wait_ge(A.pv.sem, A.pv.at(b, c + 1))
                act.activation(A.oT[:, :], A.bank[1][:, :], ACT.Copy).then_inc(A.oT_ok.sem, 1)

            def wo(b, s, k):
                upper(A, b, 2)

            def proj1(b, s, j):
                c = j % C
                act.wait_ge(p1_psum.sem, p1_psum.at(b, j + 1))
                bank = A.pair[:, c * N:(c + 1) * N]
                if j < C:
                    act.activation(h1_hi[:, j, :], bank, ACT.Identity, bias=b1_col[:, c:c + 1]).then_inc(p1_hi_ok.sem, 1)
                else:
                    act.activation(h1_hi[:, j, :], bank, ACT.Copy).then_inc(p1_hi_ok.sem, 1)

            def exp_clipped(S):
                def step(b, s, k):
                    act.wait_ge(S.clip.sem, S.clip.at(b, 1))
                    act.activation(S.e[:, :, :], S.e[:, :, :], ACT.Exp).then_inc(S.exped.sem, 1)
                return step

            def norm_b(b, s, k):
                upper(B, b, 1 + k)

            def factors(b, s, k):
                act.wait_ge(cbias_ok.sem, cbias_ok.at(b, 1))
                act.activation(rgf[:, :], B.bank[0][0:3 * DK, :], ACT.Exp, scale=coef[0:3 * DK, :],
                               bias=cbias[0:3 * DK, :]).then_inc(rgf_ok.sem, 1)
                act.wait_ge(gf_psum.sem, gf_psum.at(b, 1))
                act.activation(gf[:, :, :], B.bank[1][:, 0:NT * 3 * DK].rearrange("p (t r) -> p t r", t=NT)[:, :, DK:3 * DK],
                               ACT.Copy).then_inc(gf_ok.sem, 1)

            def spread(b, s, h):
                act.wait_ge(r_psum.sem, r_psum.at(b, h + 1))
                if h == G:
                    act.wait_ge(w2_ok.sem, w2_ok.at(b, NT))
                act.activation(r_all[:, h % G, :], B.pair[:, (h % 2) * N:(h % 2 + 1) * N], ACT.Copy).then_inc(r_all_ok.sem, 1)

            def out2(b, s, c):
                act.wait_ge(w2_used.sem, w2_used.at(b, NT * (c + 1)))
                act.activation(B.oT[:, :], B.bank[0][:, :], ACT.Copy)
                act.activation(dT[:, :], B.bank[1][:, :], ACT.Copy).then_inc(B.oT_ok.sem, 1)

            def sum_edges(j):
                act.activation(B.probsT[:, G + j % 2, :], B.bank[0][:, :], ACT.Identity,
                               bias=sj3[:, 2 * j:2 * j + 1]).then_inc(u3.sem, 1)

            def sums3(b, s, k):
                act.wait_ge(s3_psum.sem, s3_psum.at(b, 1))
                act.activation(sj3[:, :], B.bank[1][:, 0:NT * 2], ACT.Copy).then_inc(sj3_ok.sem, 1)
                act.wait_ge(sj3_ok.sem, sj3_ok.at(b, 1))
                for j in range(2):
                    sum_edges(j)

            def v3(b, s, k):
                act.wait_ge(v3_psum.sem, v3_psum.at(b, 1))
                act.activation(B.val[:, :, :].rearrange("p t d -> p (t d)"), B.pair[:, :], ACT.Copy).then_inc(v3_ok.sem, 1)

            def edges3(b, s, j):
                if j + 2 < NT:
                    act.wait_ge(leaky3.sem, leaky3.at(b, j + 1))
                    sum_edges(j + 2)
                act.wait_ge(neg3_ok.sem, neg3_ok.at(b, j + 1))
                act.activation(B.probsT[:, j, :], B.probsT[:, G + 2 + j % 2, :], ACT.Exp, bias=neg3[:, j:j + 1],
                               accum_out=den3[:, j:j + 1]).then_inc(att3.sem, 1)

            def pv3(b, s, k):
                act.wait_ge(o3_psum.sem, o3_psum.at(b, 1))
                act.activation(B.y[:, :, :].rearrange("p t d -> p (t d)"), B.pair[:, :], ACT.Copy).then_inc(y3_ok.sem, 1)

            act.wait_ge(consts.sem, CONSTS)
            act.wait_ge(ready.sem, 1)
            batches(act, {("A", "norm"): norm_a, ("A", "qk"): qk, ("A", "v"): v, ("A", "score0"): score0,
                          ("A", "turn"): turn, ("A", "out0"): out0, ("A", "wo"): wo, ("A", "proj1"): proj1,
                          ("A", "score1"): score1, ("A", "pv1"): exp_clipped(A),
                          ("B", "norm"): norm_b, ("B", "factors"): factors,
                          ("B", "spread"): spread, ("B", "out2"): out2, ("B", "elu2"): exp_clipped(B),
                          ("B", "sums3"): sums3, ("B", "v3"): v3, ("B", "edges3"): edges3, ("B", "pv3"): pv3})

        @block.vector
        def _(dve):
            steps_done = [0]

            def link(ins):
                steps_done[0] += 1
                ins.then_inc(set_v.sem, 1)
                dve.wait_ge(set_v.sem, steps_done[0])

            def split(hi, lo, value):
                link(dve.tensor_copy(hi, value))
                return dve.tensor_tensor(lo, value, hi.bitcast(F32), ALU.subtract)

            dve.wait_ge(weights_in.sem, 16 * (n_raw + 4))
            dve.wait_ge(consts.sem, CONSTS)
            link(dve.tensor_copy(pick[:, :, :], pick_f))
            w2_heads = raw[:, MATRICES.index("W2"), :, :].rearrange("p c (h d) -> p c h d", h=H)
            prod_heads = prod.rearrange("p c (h d) -> p c h d", h=H)
            for part, where in ((0, (0,)), (1, (DK, 2 * DK))):
                for c in range(C):
                    link(dve.tensor_tensor(prod_heads[:, c, :, :], w2_heads[:, c, :, :], a2_bc[:, :, part, :], ALU.mult))
                for w in where:
                    link(dve.tensor_reduce(out=wa2[:, :, w:w + H], in_=prod_heads, axis=AX.X, op=ALU.add))
            w3_raw = raw[:, MATRICES.index("W3"), :, :]
            for part, dst in ((0, wi3), (1, wj3)):
                for c in range(C):
                    link(dve.tensor_tensor(prod[:, c, :], w3_raw[:, c, :], a3_bc[:, part, :], ALU.mult))
                    link(dve.tensor_reduce(out=cmax[:, :], in_=prod[:, c, :], axis=AX.X, op=ALU.add))
                    link(dve.tensor_copy(dst[:, c, :], cmax[:, :].broadcast_to([P, dst.shape[2]])))
            link(dve.tensor_scalar(raw[:, 0, :, :], raw[:, 0, :, :], 1.0 / math.sqrt(DK), None, ALU.mult))
            dve.wait_ge(w1_turned.sem, 1)
            link(dve.tensor_copy(raw[:, 4, :, :].rearrange("p c d -> p (c d)"), A.pair[:, 0:C * D]))
            for i, m in enumerate(MATRICES):
                link(split(w_hi[m][:, :, :], w_lo[m][:, :, :], raw[:, i, :, :]))
            link(split(wa2_hi[:, :, :], wa2_lo[:, :, :], wa2))
            link(split(wi3_hi[:, :, :], wi3_lo[:, :, :], wi3))
            split(wj3_hi[:, :, :], wj3_lo[:, :, :], wj3).then_inc(ready.sem, 1)

            def normalise(S, b, k, x):
                for t in range(NT):
                    last = dve.bn_stats(out=S.stats[:, t, :], in_=x[:, t, :])
                last.then_inc(S.stat.sem, 1)
                dve.wait_ge(S.stat.sem, S.stat.at(b, k + 1))
                hold_dve(dve)
                for t in range(NT):
                    last = dve.bn_aggr(out=S.meanvar[:, t, :], in_=S.stats[:, t, :])
                last.then_inc(S.aggr.sem, 1)
                dve.wait_ge(S.aggr.sem, S.aggr.at(b, k + 1))
                dve.tensor_scalar(S.vareps[:, :], S.meanvar[:, :, 1], EPS, None, ALU.add).then_inc(S.eps_in.sem, 1)
                dve.wait_ge(S.rstd_ok.sem, S.rstd_ok.at(b, k + 1))
                for t in range(NT):
                    last = dve.tensor_scalar(S.xn[:, t, :], x[:, t, :], S.meanvar[:, t, 0:1], S.rstd[:, t:t + 1],
                                             ALU.subtract, ALU.mult)
                last.then_inc(S.normed.sem, 1)

            def lower(S, b, k):
                dve.wait_ge(S.hT_hi_ok.sem, S.hT_hi_ok.at(b, k))
                dve.scalar_tensor_tensor(out=S.hT_lo[:, :, :].rearrange("p c n -> p (c n)"), in0=S.pair[:, :], scalar=0.0,
                                         in1=S.hT_hi[:, :, :].bitcast(F32).rearrange("p c n -> p (c n)"),
                                         op0=ALU.max, op1=ALU.subtract).then_inc(S.hT_lo_ok.sem, 1)

            def norm_a(b, s, k):
                if k == 0:
                    dve.wait_ge(x_loaded.sem, x_loaded.at(b, 16))
                    normalise(A, b, 0, x_in)
                else:
                    dve.wait_ge(res0.sem, res0.at(b, 1))
                    normalise(A, b, 1, x_mid[s])
                lower(A, b, 1 + 2 * k)

            def qk(b, s, j):
                which = j % 2
                dve.wait_ge(qk_hi_ok.sem, qk_hi_ok.at(b, j + 1))
                dve.tensor_tensor(qk_lo[:, which, :], A.pair[:, which * N:(which + 1) * N],
                                  qk_hi[:, which, :].bitcast(F32),
                                  ALU.subtract).then_inc(qk_lo_ok.sem, 1)

            def max_block(b, k):
                dve.wait_ge(scored.sem, scored.at(b, k + 1))
                dve.tensor_reduce(out=neg_max[:, k:k + 1], in_=A.pair[:, (k % 2) * N:(k % 2 + 1) * N],
                                  axis=AX.X, op=ALU.max, negate=True).then_inc(maxed.sem, 1)

            def score0(b, s, k):
                max_block(b, k)

            def score1(b, s, m):
                max_block(b, L0_BLOCKS + m)

            def out0(b, s, c):
                dve.wait_ge(A.o_psum.sem, A.o_psum.at(b, c + 1))
                cols = slice(c * G * NT, (c + 1) * G * NT)
                dve.reciprocal(rden[:, cols], den[:, cols]).then_inc(A.rd.sem, 1)
                dve.wait_ge(A.rd.sem, A.rd.at(b, c + 1))
                dve.tensor_tensor(
                    A.xn[:, :, c * P:(c + 1) * P].rearrange("p t (g d) -> p t g d", g=G),
                    A.bank[0][:, :].rearrange("p (t g d) -> p t g d", t=NT, g=G),
                    rden[:, cols].rearrange("p (t g o) -> p t g o", t=NT, o=1).broadcast_to([P, NT, G, DK]),
                    ALU.mult).then_inc(A.o_ok.sem, 1)

            def wo(b, s, k):
                lower(A, b, 2)
                dve.wait_ge(wo_psum.sem, wo_psum.at(b, 1))
                if later(b, 2):
                    dve.wait_ge(stored.sem, stored.at(b - 2, 16))
                dve.tensor_tensor(x_mid[s][:, :, :].rearrange("p t d -> p (t d)"), A.pair[:, :],
                                  x_in[:, :, :].rearrange("p t d -> p (t d)"), ALU.add).then_inc(res0.sem, 1)

            def h1(b, s, k):
                dve.wait_ge(h1_psum.sem, h1_psum.at(b, 1))
                dve.tensor_tensor(A.val[:, :, :], A.pair[:, :].rearrange("p (t d) -> p t d", t=NT),
                                  b1_row[:, :].rearrange("p (o d) -> p o d", o=1).broadcast_to([P, NT, D]),
                                  ALU.add).then_inc(h1_ok.sem, 1)

            def proj1(b, s, j):
                c = j % C
                dve.wait_ge(p1_hi_ok.sem, p1_hi_ok.at(b, j + 1))
                bank = A.pair[:, c * N:(c + 1) * N]
                hi = h1_hi[:, j, :].bitcast(F32)
                if j < C:
                    dve.scalar_tensor_tensor(out=h1_lo[:, j, :], in0=bank, scalar=b1_col[:, c:c + 1], in1=hi,
                                             op0=ALU.add, op1=ALU.subtract).then_inc(p1_lo_ok.sem, 1)
                else:
                    dve.tensor_tensor(h1_lo[:, j, :], bank, hi, ALU.subtract).then_inc(p1_lo_ok.sem, 1)

            def elu_add(S, b, s):
                dve.tensor_scalar(S.e[:, :, :], S.y[:, :, :], 0.0, None, ALU.min).then_inc(S.clip.sem, 1)
                dve.wait_ge(S.exped.sem, S.exped.at(b, 1))
                dve.scalar_tensor_tensor(out=S.y[:, :, :], in0=S.e[:, :, :], scalar=-1.0, in1=S.y[:, :, :],
                                         op0=ALU.add, op1=ALU.max).then_inc(S.elu.sem, 1)
                dve.wait_ge(S.elu.sem, S.elu.at(b, 1))
                dve.tensor_tensor(x_mid[s][:, :, :], x_mid[s][:, :, :], S.y[:, :, :], ALU.add).then_inc(S.x_ok.sem, 1)

            def pv1(b, s, k):
                dve.wait_ge(o1_psum.sem, o1_psum.at(b, 1))
                dve.reciprocal(rden[:, L0_BLOCKS:BLOCKS], den[:, L0_BLOCKS:BLOCKS]).then_inc(rd1.sem, 1)
                dve.wait_ge(rd1.sem, rd1.at(b, 1))
                dve.tensor_tensor(A.y[:, :, :], A.pair[:, :].rearrange("p (t d) -> p t d", t=NT),
                                  rden[:, L0_BLOCKS:BLOCKS].rearrange("p (t o) -> p t o", o=1).broadcast_to([P, NT, D]),
                                  ALU.mult).then_inc(y1_ok.sem, 1)
                dve.wait_ge(y1_ok.sem, y1_ok.at(b, 1))
                elu_add(A, b, s)

            def masks(b, s, k):
                for m in range(NT):
                    dve.wait_ge(mT_psum.sem, mT_psum.at(b, m + 1))
                    dve.tensor_scalar(adjT[:, m, :], B.bank[m % 2][:, :].bitcast(BF16)[:, 0:N], -1.0, None,
                                      ALU.is_ge).then_inc(adjT_ok.sem, 1)

            def norm_b(b, s, k):
                dve.wait_ge((A if k == 0 else B).x_ok.sem, (A if k == 0 else B).x_ok.at(b, 1))
                normalise(B, b, k, x_mid[s])
                lower(B, b, 1 + k)

            def sums2(b, s, k):
                dve.wait_ge(s2_psum.sem, s2_psum.at(b, 1))
                dve.tensor_reduce(out=cmax[0:3 * DK, :], in_=B.bank[0][0:3 * DK, :], axis=AX.X,
                                  op=ALU.max, negate=True).then_inc(cmax_part.sem, 1)
                dve.wait_ge(cmax_part.sem, cmax_part.at(b, 1))
                dve.tensor_scalar(cmax[0:DK, :], cmax[DK:2 * DK, :], -1.0, None, ALU.mult).then_inc(cmax_part.sem, 1)
                dve.wait_ge(cmax_part.sem, cmax_part.at(b, 2))
                dve.tensor_tensor(cbias[0:3 * DK, :], cmax[0:3 * DK, :], coef[0:3 * DK, :], ALU.mult).then_inc(cbias_ok.sem, 1)

            def factors(b, s, k):
                dve.wait_ge(rgf_ok.sem, rgf_ok.at(b, 1))
                dve.tensor_scalar(r_split[0:DK, :], rgf[0:DK, :], 1.0, None, ALU.min).then_inc(r_hi.sem, 1)
                dve.wait_ge(r_hi.sem, r_hi.at(b, 1))
                dve.scalar_tensor_tensor(out=r_split[DK:2 * DK, :], in0=rgf[0:DK, :], scalar=1.0,
                                         in1=r_split[0:DK, :].bitcast(F32), op0=ALU.min,
                                         op1=ALU.subtract).then_inc(r_ok.sem, 1)
                dve.wait_ge(gf_ok.sem, gf_ok.at(b, 1))
                dve.wait_ge(B.v_psum.sem, B.v_psum.at(b, 1))
                dve.tensor_tensor(
                    B.val[:, :, :].rearrange("p t (h d) -> p t h d", h=H),
                    B.pair[:, :].rearrange("p (t h d) -> p t h d", t=NT, h=H),
                    gf[:, :, DK:DK + H].rearrange("p t (h o) -> p t h o", o=1).broadcast_to([P, NT, H, DK]),
                    ALU.mult).then_inc(B.v_ok.sem, 1)

            def weights2(b, s, u):
                c, j = u // NT, u % NT
                if u >= 2:
                    dve.wait_ge(w2_used.sem, w2_used.at(b, u - 1))
                for g in range(G):
                    h = G * c + g
                    if j == 0:
                        dve.wait_ge(r_all_ok.sem, r_all_ok.at(b, h + 1))
                    last = dve.scalar_tensor_tensor(out=B.probsT[:, u % 2 * G + g, :], in0=r_all[:, g, :],
                                                    scalar=gf[:, j, h:h + 1], in1=adjT[:, j, :],
                                                    op0=ALU.max, op1=ALU.mult)
                last.then_inc(w2_ok.sem, 1)

            def out2(b, s, c):
                dve.wait_ge(B.o_psum.sem, B.o_psum.at(b, c + 1))
                dve.reciprocal(rden2[:, c, :].rearrange("p (t g) -> p t g", t=NT),
                               B.pair[:, N:2 * N].rearrange("p (t g d) -> p t g d", t=NT, g=G)[:, :, :, 0]).then_inc(B.rd.sem, 1)
                dve.wait_ge(B.rd.sem, B.rd.at(b, c + 1))
                dve.tensor_tensor(
                    B.y[:, :, c * P:(c + 1) * P].rearrange("p t (g d) -> p t g d", g=G),
                    B.pair[:, 0:N].rearrange("p (t g d) -> p t g d", t=NT, g=G),
                    rden2[:, c, :].rearrange("p (t g o) -> p t g o", t=NT, o=1).broadcast_to([P, NT, G, DK]),
                    ALU.mult).then_inc(B.o_ok.sem, 1)

            def elu2(b, s, k):
                dve.wait_ge(B.o_ok.sem, B.o_ok.at(b, C))
                elu_add(B, b, s)

            def edges3(b, s, j):
                dve.wait_ge(u3.sem, u3.at(b, j + 1))
                if j == 0:
                    dve.wait_ge(maskT_ok.sem, maskT_ok.at(b, 1))
                if j >= 2:
                    dve.wait_ge(att3.sem, att3.at(b, j - 1))
                u, row = B.probsT[:, G + j % 2, :], B.probsT[:, G + 2 + j % 2, :]
                dve.scalar_tensor_tensor(out=row, in0=u, scalar=SLOPE, in1=u, op0=ALU.mult,
                                         op1=ALU.max).then_inc(leaky3.sem, 1)
                dve.wait_ge(leaky3.sem, leaky3.at(b, j + 1))
                hold_dve(dve)
                dve.tensor_tensor_reduce(out=row, in0=row, in1=maskT[:, j, :],
                                         scale=1.0, scalar=-3e38, op0=ALU.add, op1=ALU.max,
                                         accum_out=max3[:, j:j + 1]).then_inc(masked3.sem, 1)
                dve.wait_ge(masked3.sem, masked3.at(b, j + 1))
                dve.tensor_scalar(neg3[:, j:j + 1], max3[:, j:j + 1], -1.0, None, ALU.mult).then_inc(neg3_ok.sem, 1)

            def pv3(b, s, k):
                dve.wait_ge(att3.sem, att3.at(b, NT))
                dve.reciprocal(rden3[:, :], den3[:, :]).then_inc(rd3.sem, 1)
                dve.wait_ge(rd3.sem, rd3.at(b, 1))
                dve.wait_ge(v3_ok.sem, v3_ok.at(b, 1))
                for j in range(NT):
                    last = dve.tensor_scalar(B.val[:, j, :], B.val[:, j, :], rden3[:, j:j + 1], None, ALU.mult)
                last.then_inc(val3_ok.sem, 1)
                dve.wait_ge(y3_ok.sem, y3_ok.at(b, 1))
                dve.scalar_tensor_tensor(out=B.xn[:, :, :], in0=B.y[:, :, :], scalar=SLOPE, in1=B.y[:, :, :],
                                         op0=ALU.mult, op1=ALU.max).then_inc(leaky_out.sem, 1)
                dve.wait_ge(leaky_out.sem, leaky_out.at(b, 1))
                dve.tensor_tensor(x_mid[s][:, :, :], x_mid[s][:, :, :], B.xn[:, :, :], ALU.add).then_inc(final_ok.sem, 1)

            batches(dve, {("A", "norm"): norm_a, ("A", "qk"): qk, ("A", "score0"): score0, ("A", "out0"): out0,
                          ("A", "wo"): wo, ("A", "h1"): h1, ("A", "proj1"): proj1, ("A", "score1"): score1,
                          ("A", "pv1"): pv1, ("B", "masks"): masks, ("B", "norm"): norm_b, ("B", "sums2"): sums2,
                          ("B", "factors"): factors, ("B", "weights2"): weights2, ("B", "out2"): out2,
                          ("B", "elu2"): elu2, ("B", "edges3"): edges3, ("B", "pv3"): pv3})


_INS = ["x", "adj", "L0_gnn_Wq", "L0_gnn_Wk", "L0_gnn_Wv", "L0_gnn_Wo", "L1_gnn_W", "L1_gnn_b", "L1_gnn_attn",
        "L2_gnn_W", "L2_gnn_a", "L3_gnn_W", "L3_gnn_a"]


def kernel(**inputs):
    import numpy as _np
    import concourse.bacc as _bacc
    from concourse import mybir as _mybir
    from concourse.bass_utils import run_bass_kernel_spmd as _run

    nc = _bacc.Bacc("TRN2", target_bir_lowering=False, num_devices=1)
    arrays, args = {}, []
    for name in _INS:
        a = _np.ascontiguousarray(inputs[name])
        arrays[f"in_{name}"] = a
        args.append(nc.dram_tensor(f"in_{name}", a.shape, _mybir.dt.from_np(a.dtype), kind="ExternalInput").ap())
    args.append(nc.dram_tensor("out_x", (BATCH, N, D), F32, kind="ExternalOutput").ap())
    build(nc, *args)
    r = _run(nc, [arrays], core_ids=[0])
    return r.results[0]["out_x"]
```

```python
import math
from contextlib import ExitStack

import numpy as np

import concourse.bass as bass
from concourse import mybir

F32 = mybir.dt.float32
F32R = mybir.dt.float32r
BF16 = mybir.dt.bfloat16
I32 = mybir.dt.int32
ALU = mybir.AluOpType
ACT = mybir.ActivationFunctionType
AX = mybir.AxisListType

P = 128
BATCH = 16
N = 512
D = 256
H = 8
DK = D // H
NT = N // P
C = D // P
G = P // DK
MASKED = 1e30
EPS = 1e-5
SLOPE = 0.2
L0_BLOCKS = H * NT
BLOCKS = L0_BLOCKS + NT
STACK = 16 * 4 * G
CONSTS = 11
QK_AFTER = 4
LAG = 3
OUT_AFTER = 3
RING = 4
MATRICES = ["Wq", "Wk", "Wv", "Wo", "W1T", "M1", "W2", "W3"]


class Signal:

    def __init__(self, sem, per):
        self.sem, self.per = sem, per

    def at(self, b, k):
        return b * self.per + k


def later(b, n):
    return not isinstance(b, int) or b >= n


class Stream:
    pass


def interleave(first, second):
    streams = [list(first), list(second)]
    left = [sum(work + wait for *_, work, wait in s) for s in streams]
    ready, now, order = [0.0, 0.0], 0.0, []
    while streams[0] or streams[1]:
        starts = [max(now, ready[s]) if streams[s] else math.inf for s in range(2)]
        s = 0 if (starts[0], -left[0]) <= (starts[1], -left[1]) else 1
        *step, work, wait = streams[s].pop(0)
        now = starts[s] + work
        ready[s] = now + wait
        left[s] -= work + wait
        order.append(tuple(step))
    return order


def steps_a(last=False):
    yield ("A", "v", 0, 2.6, 1.0)
    for k in range(L0_BLOCKS + LAG):
        if k < L0_BLOCKS:
            yield ("A", "score0", k, 0.22, 0)
        if k == QK_AFTER - 1:
            for j in range(2, 2 * C):
                yield ("A", "qk", j, 1.3, 0)
        if k >= LAG:
            yield ("A", "turn", k - LAG, 0.5, 0.4)
        if 1 <= k <= L0_BLOCKS:
            yield ("A", "exp", k - 1, 0, 0)
        if k >= LAG:
            if (k - LAG) % G == 0 and k > LAG:
                yield ("A", "pv0", (k - LAG) // G - 1, 0.9, 0)
            if (k - LAG) == G * NT:
                yield ("A", "copy0", 0, 0, 0.3)
            if k - LAG == G * NT + OUT_AFTER - 1:
                yield ("A", "out0", 0, 0.5, 0)
    yield ("A", "pv0", C * NT - 1, 0.9, 0)
    yield ("A", "copy0", C - 1, 0, 0.8)
    yield ("A", "out0", C - 1, 0.47, 1.5)
    yield ("A", "turn_out", 0, 1.0, 2.3)
    yield ("A", "wo", 0, 2.6, 1.3)
    if not last:
        yield ("A", "load_next", 0, 0, 0)
    yield ("A", "stats", 1, 0, 4.0)
    yield ("A", "turn_norm", 1, 1.0, 2.3)
    yield ("A", "h1", 0, 2.6, 1.3)
    for j in range(C):
        yield ("A", "proj1", j, 1.3, 0)
    if not last:
        yield ("A", "stats_next", 0, 0, 1.0)
    for m in range(NT + LAG):
        if m < NT:
            yield ("A", "score1", m, 1.3, 0)
        if m >= LAG:
            yield ("A", "turn", L0_BLOCKS + m - LAG, 0.5, 0.4)
        if 1 <= m <= NT:
            yield ("A", "exp", L0_BLOCKS + m - 1, 0, 0)
        if m == NT and not last:
            yield ("A", "turn_norm_next", 0, 1.0, 0)
    if not last:
        for j in range(2):
            yield ("A", "qk_next", j, 1.3, 0)
    yield ("A", "pv1", 0, 6.9, 1.3)
    yield ("A", "elu1", 0, 0, 0)


def steps_b(last=False):
    yield ("B", "stats", 0, 0, 4.0)
    yield ("B", "turn_norm", 0, 1.0, 2.3)
    yield ("B", "sums2", 0, 1.3, 0)
    yield ("B", "v2", 0, 2.6, 1.5)
    yield ("B", "factors", 0, 0.5, 1.5)
    for g in range(G):
        yield ("B", "spread", g, 0.22, 0.3)
    for g in range(G):
        yield ("B", "weights2", g, 0, 0.66)
    for u in range(1, C * NT + 1):
        if u == NT:
            for g in range(G):
                yield ("B", "spread", G + g, 0.22, 0.3)
        for half in range(2):
            if u < C * NT:
                for g in range(2):
                    yield ("B", "weights2", G * u + 2 * half + g, 0, 0.2)
            yield ("B", "pv2", 2 * (u - 1) + half, 0.95, 0)
        if u % NT == 0:
            yield ("B", "copy2", u // NT - 1, 0, 1.2)
            yield ("B", "out2", u // NT - 1, 1, 0 if u == NT else 2.5)
    yield ("B", "elu2", 0, 0, 4.0)
    yield ("B", "stats", 1, 0, 4.0)
    yield ("B", "turn_norm", 1, 1.0, 2.3)
    yield ("B", "sums3", 0, 2.6, 0)
    yield ("B", "v3", 0, 2.6, 1.5)
    for j in range(NT):
        yield ("B", "edges3", j, 0, 1.5)
    if not last:
        for m in range(NT):
            yield ("B", "masks_next", m, 0.4, 0)
    yield ("B", "pv3", 0, 7, 2)
    yield ("B", "store", 0, 0, 0)


def build(nc, x, adj, Wq, Wk, Wv, Wo, W1, b1, attn, W2, a2, W3, a3, out):
    x_dram = x.rearrange("b (t p) d -> b p t d", p=P)
    adj_dram = adj.rearrange("b (t p) m -> b p t m", p=P)
    out_dram = out.rearrange("b (t p) d -> b p t d", p=P)

    ctx = ExitStack()
    with ctx:
        def sb(name, shape, dt=F32):
            return ctx.enter_context(nc.sbuf_tensor(name, shape, dt))

        def signal(name, per=1):
            return Signal(ctx.enter_context(nc.semaphore(name)), per)

        ident = sb("ident", [P, P])
        ident_bf = sb("ident_bf", [P, P], BF16)
        pick = sb("pick", [2 * DK, H, P], F32R)
        halves = sb("halves", [P, NT])
        coef = sb("coef", [P, 1])
        w_hi = {m: sb(f"{m}_hi", [P, C, D], F32R) for m in MATRICES}
        w_lo = {m: sb(f"{m}_lo", [P, C, D], F32R) for m in MATRICES}
        wa2_hi = sb("wa2_hi", [P, C, P], F32R)
        wa2_lo = sb("wa2_lo", [P, C, P], F32R)
        wi3_hi = sb("wi3_hi", [P, C, P], F32R)
        wi3_lo = sb("wi3_lo", [P, C, P], F32R)
        wj3_hi = sb("wj3_hi", [P, C, 2], F32R)
        wj3_lo = sb("wj3_lo", [P, C, 2], F32R)
        b1_row = sb("b1_row", [P, D])
        t1_bias = sb("t1_bias", [P, C])

        x_in = sb("x_in", [P, NT, D])
        adj_in = sb("adj_in", [P, NT // 2, N], I32)
        mask = [sb(f"mask{s}", [P, NT, N], BF16) for s in range(2)]
        x_mid = [sb(f"x_mid{s}", [P, NT, D]) for s in range(2)]

        A, B = Stream(), Stream()
        for S, name in ((A, "A"), (B, "B")):
            S.name = name
            S.stats = sb(f"{name}_stats", [P, NT, 6])
            S.meanvar = sb(f"{name}_meanvar", [P, NT, 2])
            S.vareps = sb(f"{name}_vareps", [P, NT])
            S.rstd = sb(f"{name}_rstd", [P, NT])
            S.xn = sb(f"{name}_xn", [P, NT, D])
            S.hT_hi = sb(f"{name}_hT_hi", [P, C, N], F32R)
            S.hT_lo = sb(f"{name}_hT_lo", [P, C, N], F32R)
            S.val = sb(f"{name}_val", [P, NT, D])
            S.probsT = sb(f"{name}_probsT", [P, 2 * G, N])
            S.oT = sb(f"{name}_oT", [P, N])
            S.pair = ctx.enter_context(nc.psum_tensor(f"{name}_pair", [P, 2 * N], F32))
            S.bank = [ctx.enter_context(nc.psum_tensor(f"{name}_bank{i}", [P, N], F32)) for i in range(2)]
        B.y = sb("B_y", [P, NT, D])
        qk_hi = sb("qk_hi", [P, 2, N], F32R)
        qk_lo = sb("qk_lo", [P, 2, N], F32R)
        q_stack = sb("q_stack", [P, H, N], F32R)
        k_stack = sb("k_stack", [P, H, N], F32R)
        t1_hi, t1_lo = q_stack, k_stack
        probs = sb("probs", [P, RING, N])
        A.y = probs[:, 0:2, :].rearrange("p a (t d) -> p (a t) d", d=D)
        A.e, B.e = A.val, B.xn
        neg_max = sb("neg_max", [P, BLOCKS])
        den = sb("den", [P, BLOCKS])
        rden = sb("rden", [P, BLOCKS])
        adjT = sb("adjT", [P, NT, N], BF16)
        maskT = adjT
        cmax = sb("cmax", [P, 1])
        cbias = sb("cbias", [P, 1])
        rgf = sb("rgf", [3 * DK, N])
        r_split = sb("r_split", [2 * DK, N], F32R)
        r_all = sb("r_all", [P, G, N])
        gf = sb("gf", [P, NT, 2 * DK])
        dT = sb("dT", [P, N])
        rden2 = sb("rden2", [P, C, NT * G])
        sj3 = sb("sj3", [P, NT * 2])
        neg3 = sb("neg3", [P, NT])
        den3 = sb("den3", [P, NT])
        rden3 = sb("rden3", [P, NT])

        weights_in = signal("weights_in")
        consts = signal("consts")
        set_v = signal("set_v")
        w1_turned = signal("w1_turned")
        attn_turned = signal("attn_turned")
        attnT_ok = signal("attnT_ok")
        aw_psum = signal("aw_psum")
        aw_ok = signal("aw_ok")
        m1_psum = signal("m1_psum")
        ready = signal("ready")
        x_loaded = signal("x_loaded", 16)
        adj_loaded = signal("adj_loaded", 32)
        mask_ready = signal("mask_ready", 2)
        stacked = [signal(f"{n}_stacked", C * STACK) for n in "qk"]
        stored = signal("stored", 16)
        for S, norms, turns in ((A, 2, 3), (B, 2, 2)):
            n = S.name
            S.stat = signal(f"{n}_stat", norms)
            S.aggr = signal(f"{n}_aggr", norms)
            S.eps_in = signal(f"{n}_eps_in", norms)
            S.rstd_ok = signal(f"{n}_rstd_ok", norms)
            S.normed = signal(f"{n}_normed", norms)
            S.hT_psum = signal(f"{n}_hT_psum", turns)
            S.hT_hi_ok = signal(f"{n}_hT_hi_ok", turns)
            S.hT_lo_ok = signal(f"{n}_hT_lo_ok", turns)
            S.v_psum = signal(f"{n}_v_psum")
            S.v_ok = signal(f"{n}_v_ok")
            S.pv = signal(f"{n}_pv", C)
            S.oT_ok = signal(f"{n}_oT_ok", C)
            S.o_psum = signal(f"{n}_o_psum", C)
            S.rd = signal(f"{n}_rd", C)
            S.o_ok = signal(f"{n}_o_ok", C)
            S.clip = signal(f"{n}_clip")
            S.exped = signal(f"{n}_exped")
            S.elu = signal(f"{n}_elu")
            S.x_ok = signal(f"{n}_x_ok")
        qk_psum = signal("qk_psum", 2 * C)
        qk_hi_ok = signal("qk_hi_ok", 2 * C)
        qk_lo_ok = signal("qk_lo_ok", 2 * C)
        scored = signal("scored", BLOCKS)
        masked = signal("masked", BLOCKS)
        exps = signal("exps", BLOCKS)
        turned = signal("turned", BLOCKS)
        kept = signal("kept", BLOCKS)
        wo_psum = signal("wo_psum")
        res0 = signal("res0")
        h1_psum = signal("h1_psum")
        h1_ok = signal("h1_ok")
        p1_psum = signal("p1_psum", C)
        p1_hi_ok = signal("p1_hi_ok", C)
        p1_lo_ok = signal("p1_lo_ok", C)
        o1_psum = signal("o1_psum")
        rd1 = signal("rd1")
        y1_ok = signal("y1_ok")
        mT_psum = signal("mT_psum", NT)
        maskT_ok = signal("maskT_ok")
        adjT_ok = signal("adjT_ok", NT)
        s2_psum = signal("s2_psum")
        cmax_part = signal("cmax_part", 2)
        cbias_ok = signal("cbias_ok")
        rgf_ok = signal("rgf_ok")
        r_hi = signal("r_hi")
        r_ok = signal("r_ok")
        gf_psum = signal("gf_psum")
        gf_ok = signal("gf_ok")
        r_psum = signal("r_psum", H)
        r_all_ok = signal("r_all_ok", H)
        w2_ok = signal("w2_ok", C * NT)
        w2_used = signal("w2_used", C * NT)
        s3_psum = signal("s3_psum")
        sj3_ok = signal("sj3_ok")
        v3_psum = signal("v3_psum")
        v3_ok = signal("v3_ok")
        u3 = signal("u3", NT)
        leaky3 = signal("leaky3", NT)
        neg3_ok = signal("neg3_ok", NT)
        att3 = signal("att3", NT)
        rd3 = signal("rd3")
        val3_ok = signal("val3_ok")
        o3_psum = signal("o3_psum")
        y3_ok = signal("y3_ok")
        leaky_out = signal("leaky_out")
        final_ok = signal("final_ok")

        raw = A.probsT[:, :, :].rearrange("p w (c d) -> p w c d", c=C)
        raw2 = B.probsT[:, :, :].rearrange("p w n -> p (w n)")
        a2_bc = raw2[:, 0:2 * D].rearrange("p (h s d) -> p h s d", h=H, s=2)
        a3_bc = raw2[:, 2 * D:4 * D].rearrange("p (s d) -> p s d", s=2)
        prod = raw2[:, 4 * D:6 * D].rearrange("p (c d) -> p c d", c=C)
        wa2 = raw2[:, 2048:2048 + C * P].rearrange("p (c m) -> p c m", c=C)
        wi3 = raw2[:, 2304:2304 + C * P].rearrange("p (c m) -> p c m", c=C)
        wj3 = raw2[:, 2560:2560 + C * 2].rearrange("p (c m) -> p c m", c=C)
        aw = probs[:, 1, :].rearrange("p (c d) -> p c d", c=C)
        attn_t = probs[:, 0, :].rearrange("p (c d) -> p c d", c=C)
        pick_f = raw2[0:2 * DK, 3072:3072 + H * P].rearrange("p (h m) -> p h m", h=H)
        n_raw = len(MATRICES)

        def batches(engine, steps):
            def run(order, b, s):
                for stream, name, k in order:
                    if (stream, name) not in steps:
                        continue
                    ahead = (stream == "A") + name.endswith("_next")
                    steps[stream, name](b - 1 + ahead, s if ahead == 1 else 1 - s, k)

            run([("A", name, k) for name, k in (("load_next", 0), ("stats_next", 0), ("turn_norm_next", 0),
                                                ("qk_next", 0), ("qk_next", 1))], -1, 1)
            run(interleave(steps_a(), []), 0, 0)
            run([("B", "masks_next", m) for m in range(NT)], 0, 0)
            run(interleave(steps_a(), steps_b()), 1, 1)
            with engine.Fori(1, BATCH // 2 - 1) as i:
                run(interleave(steps_a(), steps_b()), 2 * i, 0)
                run(interleave(steps_a(), steps_b()), 2 * i + 1, 1)
            run(interleave(steps_a(), steps_b()), BATCH - 2, 0)
            run(interleave(steps_a(last=True), steps_b()), BATCH - 1, 1)
            run(interleave([], steps_b(last=True)), BATCH, 0)

        dve_passed = ctx.enter_context(nc.semaphore("dve_passed"))
        pool_passed = ctx.enter_context(nc.semaphore("pool_passed"))

        block = ctx.enter_context(nc.Block())

        @block.sync
        def _(sp):
            for i, w in enumerate([Wq, Wk, Wv, Wo, W1, attn, W2, W3]):
                sp.dma_start(raw[:, i, :, :], w.rearrange("(c p) d -> p c d", p=P)).then_inc(weights_in.sem, 16)
            sp.dma_start(t1_bias[:, :], b1.rearrange("(c p) -> p c", p=P), allow_slow_non_contiguous=True
                         ).then_inc(weights_in.sem, 16)
            sp.dma_start(b1_row[:, :], b1.rearrange("(o d) -> o d", o=1).broadcast_to([P, D])).then_inc(weights_in.sem, 16)
            sp.dma_start(raw2[:, 0:2 * D], a2.rearrange("h d -> (h d)").rearrange("(o d) -> o d", o=1).broadcast_to([P, 2 * D])).then_inc(weights_in.sem, 16)
            sp.dma_start(raw2[:, 2 * D:4 * D], a3.rearrange("d o -> o d").broadcast_to([P, 2 * D])).then_inc(weights_in.sem, 16)

            def load(b, s, k):
                if later(b, 1):
                    sp.wait_ge(res0.sem, res0.at(b, 0))
                sp.dma_start(x_in[:, :, :], x_dram[b]).then_inc(x_loaded.sem, 16)
                for half in range(2):
                    if later(b, 1) or half:
                        sp.wait_ge(mask_ready.sem, mask_ready.at(b, half))
                    sp.dma_start(adj_in[:, :, :], adj_dram[b, :, half * 2:half * 2 + 2, :]).then_inc(adj_loaded.sem, 16)

            def stack(b, s, j):
                c, which = j // 2, j % 2
                hi, lo = qk_hi[:, which, :], qk_lo[:, which, :]
                dst, parts = ((q_stack, (hi, hi, lo, lo)), (k_stack, (hi, lo, hi, lo)))[which]
                if j == 0:
                    if later(b, 1):
                        sp.wait_ge(scored.sem, scored.at(b - 1, BLOCKS))
                sp.wait_ge(qk_hi_ok.sem, qk_hi_ok.at(b, j + 1))
                sp.wait_ge(qk_lo_ok.sem, qk_lo_ok.at(b, j + 1))
                for r, part in enumerate(parts):
                    for g in range(G):
                        sp.dma_start(dst[DK * r:DK * (r + 1), G * c + g, :].bitcast(F32),
                                     part[DK * g:DK * (g + 1), :].bitcast(F32)).then_inc(stacked[which].sem, 16)

            batches(sp, {("A", "load_next"): load, ("A", "qk"): stack, ("A", "qk_next"): stack})

        @block.gpsimd
        def _(pool):
            pool.memset(ident[:, :], 0.0).then_inc(consts.sem, 1)
            pool.memset(pick_f, 0.0).then_inc(consts.sem, 1)
            pool.memset(wa2, 0.0).then_inc(consts.sem, 1)
            pool.memset(halves[:, :], -0.5).then_inc(consts.sem, 1)
            for q, exponent in enumerate((SLOPE - 1, 1 - SLOPE, SLOPE)):
                pool.wait_ge(consts.sem, 4 + q)
                pool.memset(coef[q * DK:(q + 1) * DK, :], exponent).then_inc(consts.sem, 1)
            pool.wait_ge(consts.sem, 7)
            pool.affine_select(out=ident[:, :], in_=ident[:, :], compare_op=ALU.not_equal, fill=1.0,
                               base=0, pattern=[[-1, P]], channel_multiplier=1).then_inc(consts.sem, 1)
            pool.affine_select(out=pick_f, in_=pick_f, compare_op=ALU.not_equal, fill=1.0,
                               base=0, pattern=[[-1, H], [0, P]], channel_multiplier=1).then_inc(consts.sem, 1)
            pool.wait_ge(consts.sem, 9)
            pool.affine_select(out=pick_f, in_=pick_f, compare_op=ALU.not_equal, fill=1.0,
                               base=-DK, pattern=[[-1, H], [0, P]], channel_multiplier=1).then_inc(consts.sem, 1)
            pool.tensor_copy(ident_bf[:, :], ident[:, :]).then_inc(consts.sem, 1)

            def load(b, s, k):
                if later(b, 2):
                    pool.wait_ge(mT_psum.sem, mT_psum.at(b - 2, NT))
                for half in range(2):
                    pool.wait_ge(adj_loaded.sem, adj_loaded.at(b, 16 * (half + 1)))
                    pool.sem_inc(pool_passed)
                    pool.tensor_scalar(mask[s][:, half * 2:half * 2 + 2, :], adj_in[:, :, :], -1.0, -MASKED,
                                       ALU.add, ALU.mult).then_inc(mask_ready.sem, 1)

            def rstd(S):
                def stats(b, s, k):
                    pool.wait_ge(S.eps_in.sem, S.eps_in.at(b, k + 1))
                    pool.tensor_tensor(S.rstd[:, :], S.vareps[:, :], halves[:, :], ALU.pow).then_inc(S.rstd_ok.sem, 1)
                return stats

            def edge_mask(b, s, k):
                pool.wait_ge(w2_ok.sem, w2_ok.at(b, C * NT))
                pool.sem_inc(pool_passed)
                pool.tensor_scalar(maskT[:, :, :], adjT[:, :, :], -1.0, -MASKED,
                                   ALU.add, ALU.mult).then_inc(maskT_ok.sem, 1)

            def store(b, s, k):
                pool.wait_ge(final_ok.sem, final_ok.at(b, 1))
                pool.dma_start(out_dram[b], x_mid[s][:, :, :]).then_inc(stored.sem, 16)

            batches(pool, {("A", "load_next"): load, ("A", "stats_next"): rstd(A), ("A", "stats"): rstd(A),
                           ("B", "stats"): rstd(B),
                           ("B", "elu2"): edge_mask, ("B", "store"): store})
            pool.wait_ge(stored.sem, stored.at(BATCH - 1, 16))

        @block.tensor
        def _(pe):
            def three(psum, lhs, rhs, first=True, last=True):
                n = len(lhs)
                for c in range(n):
                    (lh, ll), (rh, rl) = lhs[c], rhs[c]
                    for i, (l, r) in enumerate(((lh, rh), (lh, rl), (ll, rh))):
                        mm = pe.matmul(psum, l, r, start=first and c == 0 and i == 0,
                                       stop=last and c == n - 1 and i == 2)
                return mm

            def cols(hi, lo, a, z):
                return [(hi[:, c, a:z], lo[:, c, a:z]) for c in range(C)]

            pe.wait_ge(weights_in.sem, 16 * (n_raw + 4))
            pe.wait_ge(consts.sem, CONSTS)
            for oc in range(C):
                for ic in range(C):
                    mm = pe.transpose(A.pair[:, ic * D + oc * P:ic * D + (oc + 1) * P],
                                      raw[:, 4, oc, ic * P:(ic + 1) * P], ident[:, :])
            mm.then_inc(w1_turned.sem, 1)
            for jc in range(C):
                for kc in range(C):
                    mm = pe.transpose(B.pair[:, kc * D + jc * P:kc * D + (jc + 1) * P],
                                      raw[:, 5, jc, kc * P:(kc + 1) * P], ident[:, :])
            mm.then_inc(attn_turned.sem, 1)
            pe.wait_ge(attnT_ok.sem, 1)
            for jc in range(C):
                for kc in range(C):
                    mm = pe.matmul(B.pair[:, jc * D:(jc + 1) * D], attn_t[:, kc, jc * P:(jc + 1) * P],
                                   raw[:, 4, kc, :], start=kc == 0, stop=kc == C - 1)
            mm.then_inc(aw_psum.sem, 1)
            pe.wait_ge(aw_ok.sem, 1)
            for ic in range(C):
                for jc in range(C):
                    mm = pe.matmul(A.bank[0][:, ic * D:(ic + 1) * D], raw[:, 4, jc, ic * P:(ic + 1) * P],
                                   aw[:, jc, :], start=jc == 0, stop=jc == C - 1)
            for ic in range(C):
                for jc in range(C):
                    mm = pe.matmul(A.bank[1][:, ic:ic + 1], aw[:, jc, ic * P:(ic + 1) * P],
                                   t1_bias[:, jc:jc + 1], start=jc == 0, stop=jc == C - 1)
            mm.then_inc(m1_psum.sem, 1)
            pe.wait_ge(ready.sem, 1)

            def turn_norm(S, b, k):
                for c in range(C):
                    for t in range(NT):
                        mm = pe.transpose(S.pair[:, c * N + t * P:c * N + (t + 1) * P],
                                          S.xn[:, t, c * P:(c + 1) * P], ident[:, :])
                mm.then_inc(S.hT_psum.sem, 1)

            def halves_in(S, b, k):
                pe.wait_ge(S.hT_hi_ok.sem, S.hT_hi_ok.at(b, k))
                pe.wait_ge(S.hT_lo_ok.sem, S.hT_lo_ok.at(b, k))

            def values(S, b, wh, wl):
                for t in range(NT):
                    mm = three(S.pair[:, t * D:(t + 1) * D], cols(S.hT_hi, S.hT_lo, t * P, (t + 1) * P),
                               cols(wh, wl, 0, D))
                return mm

            def turn_norm_a(b, s, k):
                pe.wait_ge(A.normed.sem, A.normed.at(b, k + 1))
                if k == 0:
                    if later(b, 1):
                        pe.wait_ge(masked.sem, masked.at(b - 1, BLOCKS))
                turn_norm(A, b, k)

            def qk(b, s, j):
                if j == 0:
                    halves_in(A, b, 1)
                if j >= 2:
                    pe.wait_ge(masked.sem, masked.at(b, QK_AFTER - 3 + j))
                w = ("Wq", "Wk")[j % 2]
                c = j // 2
                three(A.pair[:, (j % 2) * N:(j % 2 + 1) * N], cols(w_hi[w], w_lo[w], c * P, (c + 1) * P),
                      cols(A.hT_hi, A.hT_lo, 0, N)).then_inc(qk_psum.sem, 1)

            def v(b, s, k):
                if later(b, 1):
                    pe.wait_ge(y1_ok.sem, y1_ok.at(b - 1, 1))
                else:
                    pe.wait_ge(qk_lo_ok.sem, qk_lo_ok.at(b, 2))
                values(A, b, w_hi["Wv"], w_lo["Wv"]).then_inc(A.v_psum.sem, 1)

            def score0(b, s, k):
                c, t, g = k // (G * NT), k // G % NT, k % G
                h = G * c + g
                if k % (G * NT) == 0:
                    for which in stacked:
                        pe.wait_ge(which.sem, which.at(b, STACK * (c + 1)))
                if k == 0:
                    pe.wait_ge(A.v_ok.sem, A.v_ok.at(b, 1))
                if QK_AFTER <= k < QK_AFTER + 2:
                    pe.wait_ge(qk_lo_ok.sem, qk_lo_ok.at(b, 3 + k - QK_AFTER))
                elif k >= 2:
                    pe.wait_ge(masked.sem, masked.at(b, k - 1))
                bank = A.pair[:, (k % 2) * N:(k % 2 + 1) * N]
                pe.matmul(bank, q_stack[:, h, t * P:(t + 1) * P], k_stack[:, h, :],
                          start=True, stop=True).then_inc(scored.sem, 1)

            def turn(b, s, k):
                pe.wait_ge(exps.sem, exps.at(b, k + 1))
                if k > 0:
                    pe.wait_ge(kept.sem, kept.at(b, k))
                if k == G * NT + OUT_AFTER or k == L0_BLOCKS:
                    pe.wait_ge(A.o_ok.sem, A.o_ok.at(b, k // (G * NT)))
                for m in range(NT):
                    mm = pe.transpose(A.bank[0][:, m * P:(m + 1) * P], probs[:, k % RING, m * P:(m + 1) * P],
                                      ident[:, :])
                mm.then_inc(turned.sem, 1)

            def turn_back(dst, src):
                for t in range(NT):
                    mm = pe.transpose(dst[:, t * P:(t + 1) * P], src[:, t * P:(t + 1) * P], ident[:, :])
                return mm

            def pv0(b, s, u):
                c, t = u // NT, u % NT
                pe.wait_ge(kept.sem, kept.at(b, G * (u + 1)))
                for m in range(NT):
                    for g in range(G):
                        h = G * c + g
                        mm = pe.matmul(A.bank[1][DK * g:DK * (g + 1), t * P:(t + 1) * P],
                                       A.val[:, m, h * DK:(h + 1) * DK],
                                       A.probsT[:, u % 2 * G + g, m * P:(m + 1) * P], start=m == 0, stop=m == NT - 1)
                if t == NT - 1:
                    mm.then_inc(A.pv.sem, 1)

            def out0(b, s, c):
                blocks = G * NT * (c + 1) + (OUT_AFTER if c == 0 else 0)
                pe.wait_ge(kept.sem, kept.at(b, blocks))
                pe.wait_ge(A.oT_ok.sem, A.oT_ok.at(b, c + 1))
                turn_back(A.bank[0], A.oT).then_inc(A.o_psum.sem, 1)

            def turn_out(b, s, k):
                pe.wait_ge(A.o_ok.sem, A.o_ok.at(b, C))
                turn_norm(A, b, 1)

            def wo(b, s, k):
                halves_in(A, b, 2)
                values(A, b, w_hi["Wo"], w_lo["Wo"]).then_inc(wo_psum.sem, 1)

            def h1(b, s, k):
                halves_in(A, b, 3)
                values(A, b, w_hi["W1T"], w_lo["W1T"]).then_inc(h1_psum.sem, 1)

            def proj1(b, s, c):
                if c == 0:
                    pe.wait_ge(h1_ok.sem, h1_ok.at(b, 1))
                three(A.pair[:, c * N:(c + 1) * N], cols(w_hi["M1"], w_lo["M1"], c * P, (c + 1) * P),
                      cols(A.hT_hi, A.hT_lo, 0, N)).then_inc(p1_psum.sem, 1)

            def score1(b, s, m):
                if m == 0:
                    pe.wait_ge(p1_hi_ok.sem, p1_hi_ok.at(b, C))
                    pe.wait_ge(p1_lo_ok.sem, p1_lo_ok.at(b, C))
                if m >= 2:
                    pe.wait_ge(masked.sem, masked.at(b, L0_BLOCKS + m - 1))
                three(A.pair[:, (m % 2) * N:(m % 2 + 1) * N], cols(t1_hi, t1_lo, m * P, (m + 1) * P),
                      cols(A.hT_hi, A.hT_lo, 0, N)).then_inc(scored.sem, 1)

            def rows_product(S, weights, value):
                for i in range(NT):
                    for j in range(NT):
                        mm = pe.matmul(S.pair[:, i * D:(i + 1) * D], weights(i, j),
                                       value[:, j, :], start=j == 0, stop=j == NT - 1)
                return mm

            def pv1(b, s, k):
                pe.wait_ge(kept.sem, kept.at(b, BLOCKS))
                if isinstance(b, int) and b == BATCH - 1:
                    pe.wait_ge(masked.sem, masked.at(b, BLOCKS))
                else:
                    pe.wait_ge(qk_lo_ok.sem, qk_lo_ok.at(b + 1, 2))
                rows_product(A, lambda i, j: A.probsT[:, i, j * P:(j + 1) * P], A.val).then_inc(o1_psum.sem, 1)

            def masks(b, s, m):
                bank = B.bank[m % 2][:, :].bitcast(BF16)
                if m == 0:
                    pe.wait_ge(mask_ready.sem, mask_ready.at(b, 2))
                    if later(b, 1):
                        pe.wait_ge(u3.sem, u3.at(b - 1, NT))
                if m >= 2:
                    pe.wait_ge(adjT_ok.sem, adjT_ok.at(b, m - 1))
                for t in range(NT):
                    mm = pe.transpose(bank[:, t * P:(t + 1) * P], mask[s][:, t, m * P:(m + 1) * P], ident_bf[:, :])
                mm.then_inc(mT_psum.sem, 1)

            def turn_norm_b(b, s, k):
                pe.wait_ge(B.normed.sem, B.normed.at(b, k + 1))
                if k == 0:
                    if later(b, 1):
                        pe.wait_ge(y3_ok.sem, y3_ok.at(b - 1, 1))
                turn_norm(B, b, k)

            def sums2(b, s, k):
                halves_in(B, b, 1)
                pe.wait_ge(adjT_ok.sem, adjT_ok.at(b, NT))
                three(B.bank[0][:, :], cols(wa2_hi, wa2_lo, 0, P), cols(B.hT_hi, B.hT_lo, 0, N)).then_inc(s2_psum.sem, 1)

            def v2(b, s, k):
                values(B, b, w_hi["W2"], w_lo["W2"]).then_inc(B.v_psum.sem, 1)

            def factors(b, s, k):
                pe.wait_ge(rgf_ok.sem, rgf_ok.at(b, 1))
                for t in range(NT):
                    mm = pe.transpose(B.bank[1][:, t * 3 * DK:(t + 1) * 3 * DK], rgf[:, t * P:(t + 1) * P],
                                      ident[0:3 * DK, 0:3 * DK])
                mm.then_inc(gf_psum.sem, 1)

            def spread(b, s, h):
                if h == 0:
                    pe.wait_ge(r_ok.sem, r_ok.at(b, 1))
                    pe.wait_ge(B.v_ok.sem, B.v_ok.at(b, 1))
                if h >= 2:
                    pe.wait_ge(r_all_ok.sem, r_all_ok.at(b, h - 1))
                pe.matmul(B.pair[:, (h % 2) * N:(h % 2 + 1) * N], pick[:, h, :], r_split[:, :],
                          start=True, stop=True).then_inc(r_psum.sem, 1)

            def pv2(b, s, k):
                u, dens = k // 2, k % 2
                c, j = u // NT, u % NT
                if not dens:
                    pe.wait_ge(w2_ok.sem, w2_ok.at(b, u + 1))
                    if u == 0:
                        pe.wait_ge(gf_ok.sem, gf_ok.at(b, 1))
                    if u == NT:
                        pe.wait_ge(B.oT_ok.sem, B.oT_ok.at(b, 1))
                for g in range(G):
                    h = G * c + g
                    stationary = gf[:, j, DK + h:DK + h + 1].broadcast_to([P, DK]) if dens else \
                        B.val[:, j, h * DK:(h + 1) * DK]
                    mm = pe.matmul(B.bank[dens][DK * g:DK * (g + 1), :], stationary,
                                   B.probsT[:, u % 2 * G + g, :], start=j == 0, stop=j == NT - 1)
                if dens:
                    mm.then_inc(w2_used.sem, 1)

            def out2(b, s, c):
                pe.wait_ge(B.oT_ok.sem, B.oT_ok.at(b, c + 1))
                if c == 0:
                    pe.wait_ge(r_all_ok.sem, r_all_ok.at(b, H))
                else:
                    pe.wait_ge(B.o_ok.sem, B.o_ok.at(b, c))
                turn_back(B.pair[:, 0:N], B.oT)
                turn_back(B.pair[:, N:2 * N], dT).then_inc(B.o_psum.sem, 1)

            def sums3(b, s, k):
                halves_in(B, b, 2)
                three(B.bank[0][:, :], cols(wi3_hi, wi3_lo, 0, P), cols(B.hT_hi, B.hT_lo, 0, N))
                for t in range(NT):
                    mm = three(B.bank[1][:, 2 * t:2 * t + 2], cols(B.hT_hi, B.hT_lo, t * P, (t + 1) * P),
                               cols(wj3_hi, wj3_lo, 0, 2))
                mm.then_inc(s3_psum.sem, 1)

            def v3(b, s, k):
                values(B, b, w_hi["W3"], w_lo["W3"]).then_inc(v3_psum.sem, 1)

            def pv3(b, s, k):
                pe.wait_ge(att3.sem, att3.at(b, NT))
                pe.wait_ge(val3_ok.sem, val3_ok.at(b, 1))
                rows_product(B, lambda i, j: B.probsT[:, j, i * P:(i + 1) * P], B.val).then_inc(o3_psum.sem, 1)

            batches(pe, {("A", "turn_norm"): turn_norm_a, ("A", "turn_norm_next"): turn_norm_a, ("A", "turn_out"): turn_out, ("A", "qk"): qk, ("A", "qk_next"): qk, ("A", "v"): v, ("A", "score0"): score0,
                         ("A", "turn"): turn, ("A", "pv0"): pv0, ("A", "out0"): out0, ("A", "wo"): wo, ("A", "h1"): h1,
                         ("A", "proj1"): proj1, ("A", "score1"): score1, ("A", "pv1"): pv1,
                         ("B", "masks_next"): masks, ("B", "turn_norm"): turn_norm_b, ("B", "sums2"): sums2,
                         ("B", "v2"): v2, ("B", "factors"): factors, ("B", "spread"): spread,
                         ("B", "pv2"): pv2, ("B", "out2"): out2, ("B", "sums3"): sums3, ("B", "v3"): v3, ("B", "pv3"): pv3})

        @block.scalar
        def _(act):
            def upper(S, b, k):
                act.wait_ge(S.hT_psum.sem, S.hT_psum.at(b, k))
                act.activation(S.hT_hi[:, :, :].rearrange("p c n -> p (c n)"), S.pair[:, :], ACT.Relu).then_inc(S.hT_hi_ok.sem, 1)

            def turn_norm_a(b, s, k):
                upper(A, b, 1 + 2 * k)

            def qk(b, s, j):
                which = j % 2
                if later(b, 1) or j // 2:
                    act.wait_ge(stacked[which].sem, stacked[which].at(b, STACK * (j // 2)))
                act.wait_ge(qk_psum.sem, qk_psum.at(b, j + 1))
                act.activation(qk_hi[:, which, :], A.pair[:, which * N:(which + 1) * N], ACT.Copy).then_inc(qk_hi_ok.sem, 1)

            def v(b, s, k):
                act.wait_ge(A.v_psum.sem, A.v_psum.at(b, 1))
                if later(b, 1):
                    act.wait_ge(A.elu.sem, A.elu.at(b - 1, 1))
                act.activation(A.val[:, :, :].rearrange("p t d -> p (t d)"), A.pair[:, :], ACT.Copy).then_inc(A.v_ok.sem, 1)

            def exp(b, s, k):
                act.wait_ge(masked.sem, masked.at(b, k + 1))
                act.activation(probs[:, k % RING, :], probs[:, k % RING, :], ACT.Exp, scale=-1.0,
                               bias=neg_max[:, k:k + 1], accum_out=den[:, k:k + 1]).then_inc(exps.sem, 1)

            def turn(b, s, k):
                slot = k % (2 * G)
                act.wait_ge(turned.sem, turned.at(b, k + 1))
                act.activation(A.probsT[:, slot, :], A.bank[0][:, :], ACT.Copy).then_inc(kept.sem, 1)

            def copy0(b, s, c):
                act.wait_ge(A.pv.sem, A.pv.at(b, c + 1))
                act.activation(A.oT[:, :], A.bank[1][:, :], ACT.Copy).then_inc(A.oT_ok.sem, 1)

            def turn_out(b, s, k):
                upper(A, b, 2)

            def proj1(b, s, c):
                act.wait_ge(p1_psum.sem, p1_psum.at(b, c + 1))
                act.activation(t1_hi[:, c, :], A.pair[:, c * N:(c + 1) * N], ACT.Identity,
                               bias=t1_bias[:, c:c + 1]).then_inc(p1_hi_ok.sem, 1)

            def exp_clipped(S):
                def step(b, s, k):
                    act.wait_ge(S.clip.sem, S.clip.at(b, 1))
                    act.activation(S.e[:, :, :], S.e[:, :, :], ACT.Exp).then_inc(S.exped.sem, 1)
                return step

            def turn_norm_b(b, s, k):
                upper(B, b, 1 + k)

            def factors(b, s, k):
                act.wait_ge(cbias_ok.sem, cbias_ok.at(b, 1))
                act.activation(rgf[:, :], B.bank[0][0:3 * DK, :], ACT.Exp, scale=coef[0:3 * DK, :],
                               bias=cbias[0:3 * DK, :]).then_inc(rgf_ok.sem, 1)
                act.wait_ge(gf_psum.sem, gf_psum.at(b, 1))
                act.activation(gf[:, :, :], B.bank[1][:, 0:NT * 3 * DK].rearrange("p (t r) -> p t r", t=NT)[:, :, DK:3 * DK],
                               ACT.Copy).then_inc(gf_ok.sem, 1)

            def spread(b, s, h):
                act.wait_ge(r_psum.sem, r_psum.at(b, h + 1))
                if h == G:
                    act.wait_ge(w2_ok.sem, w2_ok.at(b, NT))
                act.activation(r_all[:, h % G, :], B.pair[:, (h % 2) * N:(h % 2 + 1) * N], ACT.Copy).then_inc(r_all_ok.sem, 1)

            def copy2(b, s, c):
                act.wait_ge(w2_used.sem, w2_used.at(b, NT * (c + 1)))
                act.activation(B.oT[:, :], B.bank[0][:, :], ACT.Copy)
                act.activation(dT[:, :], B.bank[1][:, :], ACT.Copy).then_inc(B.oT_ok.sem, 1)

            def sum_edges(j):
                act.activation(B.probsT[:, G + j % 2, :], B.bank[0][:, :], ACT.Identity,
                               bias=sj3[:, 2 * j:2 * j + 1]).then_inc(u3.sem, 1)

            def sums3(b, s, k):
                act.wait_ge(s3_psum.sem, s3_psum.at(b, 1))
                act.activation(sj3[:, :], B.bank[1][:, 0:NT * 2], ACT.Copy).then_inc(sj3_ok.sem, 1)
                act.wait_ge(sj3_ok.sem, sj3_ok.at(b, 1))
                for j in range(2):
                    sum_edges(j)

            def v3(b, s, k):
                act.wait_ge(v3_psum.sem, v3_psum.at(b, 1))
                act.activation(B.val[:, :, :].rearrange("p t d -> p (t d)"), B.pair[:, :], ACT.Copy).then_inc(v3_ok.sem, 1)

            def edges3(b, s, j):
                if j + 2 < NT:
                    act.wait_ge(leaky3.sem, leaky3.at(b, j + 1))
                    sum_edges(j + 2)
                act.wait_ge(neg3_ok.sem, neg3_ok.at(b, j + 1))
                act.activation(B.probsT[:, j, :], B.probsT[:, G + 2 + j % 2, :], ACT.Exp, scale=-1.0, bias=neg3[:, j:j + 1],
                               accum_out=den3[:, j:j + 1]).then_inc(att3.sem, 1)

            def pv3(b, s, k):
                act.wait_ge(o3_psum.sem, o3_psum.at(b, 1))
                act.activation(B.y[:, :, :].rearrange("p t d -> p (t d)"), B.pair[:, :], ACT.Copy).then_inc(y3_ok.sem, 1)

            act.wait_ge(consts.sem, CONSTS)
            act.wait_ge(attn_turned.sem, 1)
            act.activation(attn_t.rearrange("p c d -> p (c d)"), B.pair[:, 0:C * D], ACT.Copy).then_inc(attnT_ok.sem, 1)
            act.wait_ge(aw_psum.sem, 1)
            act.activation(aw.rearrange("p c d -> p (c d)"), B.pair[:, 0:C * D], ACT.Copy).then_inc(aw_ok.sem, 1)
            act.wait_ge(ready.sem, 1)
            batches(act, {("A", "turn_norm"): turn_norm_a, ("A", "turn_norm_next"): turn_norm_a, ("A", "qk"): qk, ("A", "qk_next"): qk, ("A", "v"): v, ("A", "exp"): exp,
                          ("A", "turn"): turn, ("A", "copy0"): copy0, ("A", "turn_out"): turn_out,
                          ("A", "proj1"): proj1, ("A", "elu1"): exp_clipped(A),
                          ("B", "turn_norm"): turn_norm_b, ("B", "factors"): factors,
                          ("B", "spread"): spread, ("B", "copy2"): copy2, ("B", "elu2"): exp_clipped(B),
                          ("B", "sums3"): sums3, ("B", "v3"): v3, ("B", "edges3"): edges3, ("B", "pv3"): pv3})

        @block.vector
        def _(dve):
            steps_done = [0]

            def link(ins):
                steps_done[0] += 1
                ins.then_inc(set_v.sem, 1)
                dve.wait_ge(set_v.sem, steps_done[0])

            def split(hi, lo, value):
                link(dve.tensor_copy(hi, value))
                return dve.tensor_tensor(lo, value, hi.bitcast(F32), ALU.subtract)

            dve.wait_ge(weights_in.sem, 16 * (n_raw + 4))
            dve.wait_ge(consts.sem, CONSTS)
            link(dve.tensor_copy(pick[:, :, :], pick_f))
            w2_heads = raw[:, MATRICES.index("W2"), :, :].rearrange("p c (h d) -> p c h d", h=H)
            prod_heads = prod.rearrange("p c (h d) -> p c h d", h=H)
            for part, where in ((0, (0,)), (1, (DK, 2 * DK))):
                for c in range(C):
                    link(dve.tensor_tensor(prod_heads[:, c, :, :], w2_heads[:, c, :, :], a2_bc[:, :, part, :], ALU.mult))
                for w in where:
                    link(dve.tensor_reduce(out=wa2[:, :, w:w + H], in_=prod_heads, axis=AX.X, op=ALU.add))
            w3_raw = raw[:, MATRICES.index("W3"), :, :]
            for part, dst in ((0, wi3), (1, wj3)):
                for c in range(C):
                    link(dve.tensor_tensor(prod[:, c, :], w3_raw[:, c, :], a3_bc[:, part, :], ALU.mult))
                    link(dve.tensor_reduce(out=cmax[:, :], in_=prod[:, c, :], axis=AX.X, op=ALU.add, negate=True))
                    link(dve.tensor_copy(dst[:, c, :], cmax[:, :].broadcast_to([P, dst.shape[2]])))
            link(dve.tensor_scalar(raw[:, 0, :, :], raw[:, 0, :, :], -1.0 / math.sqrt(DK), None, ALU.mult))
            dve.wait_ge(m1_psum.sem, 1)
            link(dve.tensor_copy(raw[:, 4, :, :].rearrange("p c d -> p (c d)"), A.pair[:, 0:C * D]))
            link(dve.tensor_scalar(raw[:, 5, :, :].rearrange("p c d -> p (c d)"), A.bank[0][:, :], -1.0, None, ALU.mult))
            link(dve.tensor_scalar(t1_bias[:, :], A.bank[1][:, 0:C], -1.0, None, ALU.mult))
            for i, m in enumerate(MATRICES):
                link(split(w_hi[m][:, :, :], w_lo[m][:, :, :], raw[:, i, :, :]))
            link(split(wa2_hi[:, :, :], wa2_lo[:, :, :], wa2))
            link(split(wi3_hi[:, :, :], wi3_lo[:, :, :], wi3))
            split(wj3_hi[:, :, :], wj3_lo[:, :, :], wj3).then_inc(ready.sem, 1)

            def normalise(S, b, k, x):
                for t in range(NT):
                    last = dve.bn_stats(out=S.stats[:, t, :], in_=x[:, t, :])
                last.then_inc(S.stat.sem, 1)
                dve.wait_ge(S.stat.sem, S.stat.at(b, k + 1))
                dve.sem_inc(dve_passed)
                for t in range(NT):
                    last = dve.bn_aggr(out=S.meanvar[:, t, :], in_=S.stats[:, t, :])
                last.then_inc(S.aggr.sem, 1)
                dve.wait_ge(S.aggr.sem, S.aggr.at(b, k + 1))
                dve.tensor_scalar(S.vareps[:, :], S.meanvar[:, :, 1], EPS, None, ALU.add).then_inc(S.eps_in.sem, 1)
                dve.wait_ge(S.rstd_ok.sem, S.rstd_ok.at(b, k + 1))
                for t in range(NT):
                    last = dve.tensor_scalar(S.xn[:, t, :], x[:, t, :], S.meanvar[:, t, 0:1], S.rstd[:, t:t + 1],
                                             ALU.subtract, ALU.mult)
                last.then_inc(S.normed.sem, 1)

            def lower(S, b, k):
                dve.wait_ge(S.hT_hi_ok.sem, S.hT_hi_ok.at(b, k))
                dve.scalar_tensor_tensor(out=S.hT_lo[:, :, :].rearrange("p c n -> p (c n)"), in0=S.pair[:, :], scalar=0.0,
                                         in1=S.hT_hi[:, :, :].bitcast(F32).rearrange("p c n -> p (c n)"),
                                         op0=ALU.max, op1=ALU.subtract).then_inc(S.hT_lo_ok.sem, 1)

            def stats_a(b, s, k):
                if k == 0:
                    dve.wait_ge(x_loaded.sem, x_loaded.at(b, 16))
                    if later(b, 1):
                        dve.wait_ge(A.hT_psum.sem, A.hT_psum.at(b - 1, 3))
                    normalise(A, b, 0, x_in)
                else:
                    dve.wait_ge(res0.sem, res0.at(b, 1))
                    normalise(A, b, 1, x_mid[s])

            def turn_norm_a(b, s, k):
                lower(A, b, 1 + 2 * k)

            def qk(b, s, j):
                which = j % 2
                dve.wait_ge(qk_hi_ok.sem, qk_hi_ok.at(b, j + 1))
                dve.tensor_tensor(qk_lo[:, which, :], A.pair[:, which * N:(which + 1) * N],
                                  qk_hi[:, which, :].bitcast(F32),
                                  ALU.subtract).then_inc(qk_lo_ok.sem, 1)

            def mask_block(b, s, k):
                t = (k // G if k < L0_BLOCKS else k) % NT
                if k >= RING:
                    dve.wait_ge(turned.sem, turned.at(b, k - RING + 1))
                dve.wait_ge(scored.sem, scored.at(b, k + 1))
                dve.sem_inc(dve_passed)
                dve.tensor_tensor_reduce(out=probs[:, k % RING, :], in0=A.pair[:, (k % 2) * N:(k % 2 + 1) * N],
                                         in1=mask[s][:, t, :], scale=1.0, scalar=3e38, op0=ALU.add,
                                         op1=ALU.min, accum_out=neg_max[:, k:k + 1]).then_inc(masked.sem, 1)

            def score0(b, s, k):
                if k == 0:
                    dve.wait_ge(mask_ready.sem, mask_ready.at(b, 2))
                mask_block(b, s, k)

            def score1(b, s, m):
                mask_block(b, s, L0_BLOCKS + m)

            def out0(b, s, c):
                dve.wait_ge(A.o_psum.sem, A.o_psum.at(b, c + 1))
                cols = slice(c * G * NT, (c + 1) * G * NT)
                dve.reciprocal(rden[:, cols], den[:, cols]).then_inc(A.rd.sem, 1)
                dve.wait_ge(A.rd.sem, A.rd.at(b, c + 1))
                dve.tensor_tensor(
                    A.xn[:, :, c * P:(c + 1) * P].rearrange("p t (g d) -> p t g d", g=G),
                    A.bank[0][:, :].rearrange("p (t g d) -> p t g d", t=NT, g=G),
                    rden[:, cols].rearrange("p (t g o) -> p t g o", t=NT, o=1).broadcast_to([P, NT, G, DK]),
                    ALU.mult).then_inc(A.o_ok.sem, 1)

            def turn_out(b, s, k):
                lower(A, b, 2)

            def wo(b, s, k):
                dve.wait_ge(wo_psum.sem, wo_psum.at(b, 1))
                if later(b, 2):
                    dve.wait_ge(stored.sem, stored.at(b - 2, 16))
                dve.tensor_tensor(x_mid[s][:, :, :].rearrange("p t d -> p (t d)"), A.pair[:, :],
                                  x_in[:, :, :].rearrange("p t d -> p (t d)"), ALU.add).then_inc(res0.sem, 1)

            def h1(b, s, k):
                dve.wait_ge(h1_psum.sem, h1_psum.at(b, 1))
                dve.tensor_tensor(A.val[:, :, :], A.pair[:, :].rearrange("p (t d) -> p t d", t=NT),
                                  b1_row[:, :].rearrange("p (o d) -> p o d", o=1).broadcast_to([P, NT, D]),
                                  ALU.add).then_inc(h1_ok.sem, 1)

            def proj1(b, s, c):
                dve.wait_ge(p1_hi_ok.sem, p1_hi_ok.at(b, c + 1))
                dve.scalar_tensor_tensor(out=t1_lo[:, c, :], in0=A.pair[:, c * N:(c + 1) * N],
                                         scalar=t1_bias[:, c:c + 1], in1=t1_hi[:, c, :].bitcast(F32),
                                         op0=ALU.add, op1=ALU.subtract).then_inc(p1_lo_ok.sem, 1)

            def elu_add(S, b, s):
                dve.tensor_scalar(S.e[:, :, :], S.y[:, :, :], 0.0, None, ALU.min).then_inc(S.clip.sem, 1)
                dve.wait_ge(S.exped.sem, S.exped.at(b, 1))
                dve.scalar_tensor_tensor(out=S.y[:, :, :], in0=S.e[:, :, :], scalar=-1.0, in1=S.y[:, :, :],
                                         op0=ALU.add, op1=ALU.max).then_inc(S.elu.sem, 1)
                dve.wait_ge(S.elu.sem, S.elu.at(b, 1))
                dve.tensor_tensor(x_mid[s][:, :, :], x_mid[s][:, :, :], S.y[:, :, :], ALU.add).then_inc(S.x_ok.sem, 1)

            def pv1(b, s, k):
                dve.wait_ge(o1_psum.sem, o1_psum.at(b, 1))
                dve.reciprocal(rden[:, L0_BLOCKS:BLOCKS], den[:, L0_BLOCKS:BLOCKS]).then_inc(rd1.sem, 1)
                dve.wait_ge(rd1.sem, rd1.at(b, 1))
                dve.tensor_tensor(A.y[:, :, :], A.pair[:, :].rearrange("p (t d) -> p t d", t=NT),
                                  rden[:, L0_BLOCKS:BLOCKS].rearrange("p (t o) -> p t o", o=1).broadcast_to([P, NT, D]),
                                  ALU.mult).then_inc(y1_ok.sem, 1)

            def elu1(b, s, k):
                dve.wait_ge(y1_ok.sem, y1_ok.at(b, 1))
                elu_add(A, b, s)

            def masks(b, s, m):
                dve.wait_ge(mT_psum.sem, mT_psum.at(b, m + 1))
                if m == 0 and later(b, 1):
                    dve.wait_ge(neg3_ok.sem, neg3_ok.at(b - 1, NT))
                dve.tensor_scalar(adjT[:, m, :], B.bank[m % 2][:, :].bitcast(BF16)[:, 0:N], 1.0, None,
                                  ALU.is_le).then_inc(adjT_ok.sem, 1)

            def stats_b(b, s, k):
                dve.wait_ge((A if k == 0 else B).x_ok.sem, (A if k == 0 else B).x_ok.at(b, 1))
                normalise(B, b, k, x_mid[s])

            def turn_norm_b(b, s, k):
                lower(B, b, 1 + k)

            def sums2(b, s, k):
                dve.wait_ge(s2_psum.sem, s2_psum.at(b, 1))
                dve.tensor_reduce(out=cmax[0:3 * DK, :], in_=B.bank[0][0:3 * DK, :], axis=AX.X,
                                  op=ALU.max, negate=True).then_inc(cmax_part.sem, 1)
                dve.wait_ge(cmax_part.sem, cmax_part.at(b, 1))
                dve.tensor_scalar(cmax[0:DK, :], cmax[DK:2 * DK, :], -1.0, None, ALU.mult).then_inc(cmax_part.sem, 1)
                dve.wait_ge(cmax_part.sem, cmax_part.at(b, 2))
                dve.tensor_tensor(cbias[0:3 * DK, :], cmax[0:3 * DK, :], coef[0:3 * DK, :], ALU.mult).then_inc(cbias_ok.sem, 1)

            def factors(b, s, k):
                dve.wait_ge(rgf_ok.sem, rgf_ok.at(b, 1))
                dve.tensor_scalar(r_split[0:DK, :], rgf[0:DK, :], 1.0, None, ALU.min).then_inc(r_hi.sem, 1)
                dve.wait_ge(r_hi.sem, r_hi.at(b, 1))
                dve.scalar_tensor_tensor(out=r_split[DK:2 * DK, :], in0=rgf[0:DK, :], scalar=1.0,
                                         in1=r_split[0:DK, :].bitcast(F32), op0=ALU.min,
                                         op1=ALU.subtract).then_inc(r_ok.sem, 1)
                dve.wait_ge(gf_ok.sem, gf_ok.at(b, 1))
                dve.wait_ge(B.v_psum.sem, B.v_psum.at(b, 1))
                dve.tensor_tensor(
                    B.val[:, :, :].rearrange("p t (h d) -> p t h d", h=H),
                    B.pair[:, :].rearrange("p (t h d) -> p t h d", t=NT, h=H),
                    gf[:, :, DK:DK + H].rearrange("p t (h o) -> p t h o", o=1).broadcast_to([P, NT, H, DK]),
                    ALU.mult).then_inc(B.v_ok.sem, 1)

            def weights2(b, s, k):
                u, g = k // G, k % G
                c, j = u // NT, u % NT
                h = G * c + g
                if u >= 2 and g == 0:
                    dve.wait_ge(w2_used.sem, w2_used.at(b, u - 1))
                if j == 0:
                    dve.wait_ge(r_all_ok.sem, r_all_ok.at(b, h + 1))
                last = dve.scalar_tensor_tensor(out=B.probsT[:, u % 2 * G + g, :], in0=r_all[:, g, :],
                                                scalar=gf[:, j, h:h + 1], in1=adjT[:, j, :],
                                                op0=ALU.max, op1=ALU.mult)
                if g == G - 1:
                    last.then_inc(w2_ok.sem, 1)

            def out2(b, s, c):
                dve.wait_ge(B.o_psum.sem, B.o_psum.at(b, c + 1))
                dve.reciprocal(rden2[:, c, :].rearrange("p (t g) -> p t g", t=NT),
                               B.pair[:, N:2 * N].rearrange("p (t g d) -> p t g d", t=NT, g=G)[:, :, :, 0]).then_inc(B.rd.sem, 1)
                dve.wait_ge(B.rd.sem, B.rd.at(b, c + 1))
                dve.tensor_tensor(
                    B.y[:, :, c * P:(c + 1) * P].rearrange("p t (g d) -> p t g d", g=G),
                    B.pair[:, 0:N].rearrange("p (t g d) -> p t g d", t=NT, g=G),
                    rden2[:, c, :].rearrange("p (t g o) -> p t g o", t=NT, o=1).broadcast_to([P, NT, G, DK]),
                    ALU.mult).then_inc(B.o_ok.sem, 1)

            def elu2(b, s, k):
                dve.wait_ge(B.o_ok.sem, B.o_ok.at(b, C))
                elu_add(B, b, s)

            def edges3(b, s, j):
                dve.wait_ge(u3.sem, u3.at(b, j + 1))
                if j == 0:
                    dve.wait_ge(maskT_ok.sem, maskT_ok.at(b, 1))
                if j >= 2:
                    dve.wait_ge(att3.sem, att3.at(b, j - 1))
                u, row = B.probsT[:, G + j % 2, :], B.probsT[:, G + 2 + j % 2, :]
                dve.scalar_tensor_tensor(out=row, in0=u, scalar=SLOPE, in1=u, op0=ALU.mult,
                                         op1=ALU.min).then_inc(leaky3.sem, 1)
                dve.wait_ge(leaky3.sem, leaky3.at(b, j + 1))
                dve.sem_inc(dve_passed)
                dve.tensor_tensor_reduce(out=row, in0=row, in1=maskT[:, j, :],
                                         scale=1.0, scalar=3e38, op0=ALU.add, op1=ALU.min,
                                         accum_out=neg3[:, j:j + 1]).then_inc(neg3_ok.sem, 1)

            def pv3(b, s, k):
                dve.wait_ge(att3.sem, att3.at(b, NT))
                dve.reciprocal(rden3[:, :], den3[:, :]).then_inc(rd3.sem, 1)
                dve.wait_ge(rd3.sem, rd3.at(b, 1))
                dve.wait_ge(v3_ok.sem, v3_ok.at(b, 1))
                for j in range(NT):
                    last = dve.tensor_scalar(B.val[:, j, :], B.val[:, j, :], rden3[:, j:j + 1], None, ALU.mult)
                last.then_inc(val3_ok.sem, 1)
                dve.wait_ge(y3_ok.sem, y3_ok.at(b, 1))
                dve.scalar_tensor_tensor(out=B.xn[:, :, :], in0=B.y[:, :, :], scalar=SLOPE, in1=B.y[:, :, :],
                                         op0=ALU.mult, op1=ALU.max).then_inc(leaky_out.sem, 1)
                dve.wait_ge(leaky_out.sem, leaky_out.at(b, 1))
                dve.tensor_tensor(x_mid[s][:, :, :], x_mid[s][:, :, :], B.xn[:, :, :], ALU.add).then_inc(final_ok.sem, 1)

            batches(dve, {("A", "stats_next"): stats_a, ("A", "stats"): stats_a, ("A", "turn_norm"): turn_norm_a, ("A", "turn_norm_next"): turn_norm_a,
                          ("A", "qk"): qk, ("A", "qk_next"): qk, ("A", "score0"): score0, ("A", "out0"): out0,
                          ("A", "turn_out"): turn_out, ("A", "wo"): wo, ("A", "h1"): h1, ("A", "proj1"): proj1,
                          ("A", "score1"): score1, ("A", "pv1"): pv1, ("A", "elu1"): elu1,
                          ("B", "masks_next"): masks, ("B", "stats"): stats_b, ("B", "turn_norm"): turn_norm_b,
                          ("B", "sums2"): sums2, ("B", "factors"): factors, ("B", "weights2"): weights2,
                          ("B", "out2"): out2, ("B", "elu2"): elu2, ("B", "edges3"): edges3, ("B", "pv3"): pv3})


_INS = ["x", "adj", "L0_gnn_Wq", "L0_gnn_Wk", "L0_gnn_Wv", "L0_gnn_Wo", "L1_gnn_W", "L1_gnn_b", "L1_gnn_attn",
        "L2_gnn_W", "L2_gnn_a", "L3_gnn_W", "L3_gnn_a"]


def kernel(**inputs):
    import numpy as _np
    import concourse.bacc as _bacc
    from concourse import mybir as _mybir
    from concourse.bass_utils import run_bass_kernel_spmd as _run

    nc = _bacc.Bacc("TRN2", target_bir_lowering=False, num_devices=1)
    arrays, args = {}, []
    for name in _INS:
        a = _np.ascontiguousarray(inputs[name])
        arrays[f"in_{name}"] = a
        args.append(nc.dram_tensor(f"in_{name}", a.shape, _mybir.dt.from_np(a.dtype), kind="ExternalInput").ap())
    args.append(nc.dram_tensor("out_x", (BATCH, N, D), F32, kind="ExternalOutput").ap())
    build(nc, *args)
    r = _run(nc, [arrays], core_ids=[0])
    return r.results[0]["out_x"]
```

```python
import math
from contextlib import ExitStack

import numpy as np

import concourse.bass as bass
from concourse import mybir

F32 = mybir.dt.float32
F32R = mybir.dt.float32r
BF16 = mybir.dt.bfloat16
I32 = mybir.dt.int32
ALU = mybir.AluOpType
ACT = mybir.ActivationFunctionType
AX = mybir.AxisListType

P = 128
BATCH = 16
N = 512
D = 256
H = 8
DK = D // H
NT = N // P
C = D // P
G = P // DK
MASKED = 1e30
EPS = 1e-5
SLOPE = 0.2
L0_BLOCKS = H * NT
BLOCKS = L0_BLOCKS + NT
SP_QUARTERS = 3
STACK = 16 * SP_QUARTERS * G
STACK_REST = 16 * (4 - SP_QUARTERS) * G
CONSTS = 11
QK_AFTER = 2
LAG = 3
OUT_AFTER = 3
STACKED_BEFORE = 4.0
STACKING = 7.5
HOP = 0.16
RING = 4
MATRICES = ["Wq", "Wk", "Wv", "Wo", "W1T", "M1", "W2", "W3"]


class Signal:

    def __init__(self, sem, per):
        self.sem, self.per = sem, per

    def at(self, b, k):
        return b * self.per + k


def later(b, n):
    return not isinstance(b, int) or b >= n


class Stream:
    pass


PE, DVE, POOL, SCA, SP, BEFORE = range(6)


def interleave(first, second):
    streams = [list(first), list(second)]

    def take(state, stream, step):
        _, free, ends, last, order = state
        free, ends, last = list(free), dict(ends), list(last)
        free[BEFORE] = 0.0
        name, k, stages = step[1:]
        end = 0.0
        for i, (engine, work, *needs) in enumerate(stages):
            start = max([end, free[engine]] + [ends.get((stream, *need), 0.0) for need in needs])
            end = start + work + HOP
            free[engine] = start + work
            ends[stream, name, k, i] = end
        last[stream] = max(last[stream], end)
        late = 5 * free[PE] + 2 * free[DVE] + free[SCA] + 4 * last[0] + 1.5 * last[1]
        return (late, free, ends, last, (order, step))

    row = {}
    for i in range(len(streams[0]) + 1):
        for j in range(len(streams[1]) + 1):
            options = [] if i or j else [(0.0, [0.0] * 6, {}, [0.0, 0.0], None)]
            if i:
                options.append(take(row[j], 0, streams[0][i - 1]))
            if j:
                options.append(take(row[j - 1], 1, streams[1][j - 1]))
            row[j] = min(options, key=lambda state: state[0])
    order, steps = row[len(streams[1])][4], []
    while order:
        order, step = order
        steps.append(step[:3])
    return steps[::-1]


def steps_a(last=False):
    def turn(k):
        free = [("out0", k // (G * NT) - 1, 2)] if k in (G * NT + OUT_AFTER, L0_BLOCKS) else []
        return ("A", "turn", k, [(PE, 0.44, ("exp", k, 0), ("turn", k - 1, 1), *free), (SCA, 0.48)])

    yield ("A", "v", 0, [(BEFORE, 1.3), (PE, 2.6), (SCA, 0.5)])
    yield ("A", "stack_before", 0, [(SP, STACKED_BEFORE)])
    for k in range(L0_BLOCKS + LAG):
        if k < L0_BLOCKS:
            yield ("A", "score0", k, [(PE, 0.22, ("v", 0, 2), ("score0", k - 2, 1), ("qk", k - QK_AFTER + 2, 2),
                                       ("stack_before", 0, 0), ("qk", 3 if k == G * NT else -1, 3)),
                                      (DVE, 0.61, ("turn", k - RING, 0))])
        if k == QK_AFTER - 1:
            for j in range(2, 2 * C):
                yield ("A", "qk", j, [(PE, 1.3, ("score0", QK_AFTER - 4 + j, 1), ("v", 0, 2)),
                                      (SCA, 0.48, ("stack_before", 0, 0)), (DVE, 0.6), (SP, STACKING)])
        if k >= LAG:
            yield turn(k - LAG)
        if 1 <= k <= L0_BLOCKS:
            yield ("A", "exp", k - 1, [(SCA, 0.71, ("score0", k - 1, 1))])
        if k >= LAG:
            if (k - LAG) % G == 0 and k > LAG:
                yield ("A", "pv0", (k - LAG) // G - 1, [(PE, 1.1, ("turn", k - LAG - 1, 1))])
            if (k - LAG) == G * NT:
                yield ("A", "copy0", 0, [(SCA, 0.48, ("pv0", NT - 1, 0))])
            if k - LAG == G * NT + OUT_AFTER - 1:
                yield ("A", "out0", 0, [(PE, 0.44, ("copy0", 0, 0), ("turn", k - LAG, 1)), (DVE, 0.2), (DVE, 0.6)])
    yield ("A", "pv0", C * NT - 1, [(PE, 1.1, ("turn", L0_BLOCKS - 1, 1))])
    yield ("A", "copy0", C - 1, [(SCA, 0.48, ("pv0", C * NT - 1, 0))])
    yield ("A", "out0", C - 1, [(PE, 0.44, ("copy0", C - 1, 0)), (DVE, 0.2), (DVE, 0.6)])
    yield ("A", "turn_out", 0, [(PE, 0.9, ("out0", C - 1, 2)), (SCA, 0.5), (DVE, 0.66)])
    yield ("A", "wo", 0, [(PE, 2.6, ("turn_out", 0, 2)), (DVE, 0.6)])
    if not last:
        yield ("A", "load_next", 0, [])
    yield ("A", "stats", 1, [(DVE, 2.1, ("wo", 0, 1)), (POOL, 1.0)])
    yield ("A", "norm", 1, [(DVE, 1.3, ("stats", 1, 1))])
    yield ("A", "turn_norm", 1, [(PE, 0.9, ("norm", 1, 0)), (SCA, 0.5), (DVE, 0.66)])
    yield ("A", "h1", 0, [(PE, 2.6, ("turn_norm", 1, 2)), (DVE, 0.6)])
    for j in range(C):
        yield ("A", "proj1", j, [(PE, 1.3), (SCA, 0.57), (DVE, 0.66)])
    if not last:
        for half in range(2):
            yield ("A", "edges_next", half, [(POOL, 1.0)])
        yield ("A", "stats_next", 0, [(DVE, 2.1), (POOL, 1.0)])
    for k in range(L0_BLOCKS, BLOCKS + LAG):
        if k == BLOCKS - 1 and not last:
            yield ("A", "norm_next", 0, [(DVE, 1.3, ("stats_next", 0, 1))])
        if k < BLOCKS:
            yield ("A", "score1", k - L0_BLOCKS, [(PE, 1.3, ("proj1", C - 1, 2), ("score1", k - L0_BLOCKS - 2, 1)),
                                                  (DVE, 0.61, ("turn", k - RING, 0))])
        if k >= L0_BLOCKS + LAG:
            yield turn(k - LAG)
        if L0_BLOCKS < k <= BLOCKS:
            yield ("A", "exp", k - 1, [(SCA, 0.71, ("score1", k - 1 - L0_BLOCKS, 1))])
        if k == BLOCKS and not last:
            yield ("A", "turn_norm_next", 0, [(PE, 0.9, ("norm_next", 0, 0), ("score1", NT - 1, 1)), (SCA, 0.5), (DVE, 0.66)])
    if not last:
        for j in range(2):
            yield ("A", "qk_next", j, [(PE, 1.3, ("turn_norm_next", 0, 2)), (SCA, 0.48), (DVE, 0.6)])
    yield ("A", "pv1", 0, [(PE, 6.9, ("turn", BLOCKS - 1, 1), ("qk_next", 1, 2)), (DVE, 0.6)])
    yield ("A", "elu1", 0, [(DVE, 1.13, ("pv1", 0, 1)), (DVE, 1.13)])


def steps_b(last=False):
    def start(k):
        yield ("B", "stats", k, [(BEFORE, 0.0 if k else 4.0), (DVE, 2.1, ("elu2", k - 1, 1)), (POOL, 1.0)])
        yield ("B", "norm", k, [(DVE, 1.3, ("stats", k, 2))])
        yield ("B", "turn_norm", k, [(PE, 0.9, ("norm", k, 0)), (SCA, 0.5), (DVE, 0.66)])

    def spread(h):
        return ("B", "spread", h, [(PE, 0.22, ("factors", 0, 4), ("spread", h - 2, 1)),
                                   (SCA, 0.48, ("weights2", G * NT - 1 if h == G else -1, 0))])

    yield from start(0)
    yield ("B", "sums2", 0, [(PE, 1.3, ("turn_norm", 0, 2)), (DVE, 0.9)])
    yield ("B", "v2", 0, [(PE, 2.6, ("turn_norm", 0, 2))])
    yield ("B", "factors", 0, [(SCA, 0.6, ("sums2", 0, 1)), (PE, 0.4), (DVE, 0.9), (SCA, 0.4), (DVE, 1.13, ("v2", 0, 0))])
    for g in range(G):
        yield spread(g)
    for u in range(C * NT + 1):
        if u == NT:
            for g in range(G):
                yield spread(G + g)
        for half in range(2):
            if u < C * NT:
                for g in range(2 * half, 2 * half + 2):
                    c, j = u // NT, u % NT
                    yield ("B", "weights2", G * u + g, [(DVE, 0.66, ("spread", G * c + g if j == 0 else -1, 1),
                                                         ("pv2", 2 * (u - 2) + 1, 0))])
            if u > 0:
                yield ("B", "pv2", 2 * (u - 1) + half, [(PE, 0.94, ("weights2", G * u - 1, 0), ("copy2", (u - 1) // NT - 1, 0))])
        if u in (NT, C * NT):
            c = u // NT - 1
            yield ("B", "copy2", c, [(SCA, 0.96, ("pv2", 2 * u - 1, 0))])
            yield ("B", "out2", c, [(PE, 0.9, ("copy2", c, 0), ("spread", H - 1, 1)), (DVE, 0.2), (DVE, 0.6)])
    yield ("B", "elu2", 0, [(DVE, 1.13, ("out2", C - 1, 2)), (DVE, 1.13)])
    yield from start(1)
    yield ("B", "sums3", 0, [(PE, 2.9, ("turn_norm", 1, 2)), (SCA, 0.2), (SCA, 1.1)])
    yield ("B", "v3", 0, [(PE, 2.6), (SCA, 0.92)])
    for j in range(NT + 1):
        if j < NT:
            yield ("B", "edges3", j, [(DVE, 1.2, ("sums3", 0, 2), ("edges3", j - 2, 1)), (SCA, 1.3 if j < 2 else 0.7)])
        if j > 0:
            yield ("B", "values3", j - 1, [(DVE, 0.12, ("edges3", j - 1, 1)), (DVE, 0.26)])
    if not last:
        for m in range(NT):
            yield ("B", "masks_next", m, [(PE, 0.24, ("masks_next", m - 2, 1)), (DVE, 0.33)])
    yield ("B", "pv3", 0, [(PE, 7.0, ("values3", NT - 1, 1))])
    yield ("B", "store", 0, [(DVE, 1.13, ("pv3", 0, 0)), (SCA, 0.92)])


def build(nc, x, adj, Wq, Wk, Wv, Wo, W1, b1, attn, W2, a2, W3, a3, out):
    x_dram = x.rearrange("b (t p) d -> b p t d", p=P)
    adj_dram = adj.rearrange("b (t p) m -> b p t m", p=P)
    out_dram = out.rearrange("b (t p) d -> b p t d", p=P)

    ctx = ExitStack()
    with ctx:
        def sb(name, shape, dt=F32):
            return ctx.enter_context(nc.sbuf_tensor(name, shape, dt))

        def signal(name, per=1):
            return Signal(ctx.enter_context(nc.semaphore(name)), per)

        ident = sb("ident", [P, P])
        ident_bf = sb("ident_bf", [P, P], BF16)
        pick = sb("pick", [2 * DK, H, P], F32R)
        halves = sb("halves", [P, NT])
        coef = sb("coef", [P, 1])
        w_hi = {m: sb(f"{m}_hi", [P, C, D], F32R) for m in MATRICES}
        w_lo = {m: sb(f"{m}_lo", [P, C, D], F32R) for m in MATRICES}
        wa2_hi = sb("wa2_hi", [P, C, P], F32R)
        wa2_lo = sb("wa2_lo", [P, C, P], F32R)
        wi3_hi = sb("wi3_hi", [P, C, P], F32R)
        wi3_lo = sb("wi3_lo", [P, C, P], F32R)
        wj3_hi = sb("wj3_hi", [P, C, 2], F32R)
        wj3_lo = sb("wj3_lo", [P, C, 2], F32R)
        b1_row = sb("b1_row", [P, D])
        t1_bias = sb("t1_bias", [P, C])

        x_in = sb("x_in", [P, NT, D])
        adj_in = sb("adj_in", [P, NT // 2, N], I32)
        mask = [sb(f"mask{s}", [P, NT, N], BF16) for s in range(2)]
        x_mid = [sb(f"x_mid{s}", [P, NT, D]) for s in range(2)]

        A, B = Stream(), Stream()
        for S, name in ((A, "A"), (B, "B")):
            S.name = name
            S.stats = sb(f"{name}_stats", [P, NT, 6])
            S.meanvar = sb(f"{name}_meanvar", [P, NT, 2])
            S.vareps = sb(f"{name}_vareps", [P, NT])
            S.rstd = sb(f"{name}_rstd", [P, NT])
            S.xn = sb(f"{name}_xn", [P, NT, D])
            S.hT_hi = sb(f"{name}_hT_hi", [P, C, N], F32R)
            S.hT_lo = sb(f"{name}_hT_lo", [P, C, N], F32R)
            S.val = sb(f"{name}_val", [P, NT, D])
            S.probsT = sb(f"{name}_probsT", [P, 2 * G, N])
            S.oT = sb(f"{name}_oT", [P, N])
            S.pair = ctx.enter_context(nc.psum_tensor(f"{name}_pair", [P, 2 * N], F32))
            S.bank = [ctx.enter_context(nc.psum_tensor(f"{name}_bank{i}", [P, N], F32)) for i in range(2)]
        B.y = sb("B_y", [P, NT, D])
        qk_hi = sb("qk_hi", [P, 2, N], F32R)
        qk_lo = sb("qk_lo", [P, 2, N], F32R)
        q_stack = sb("q_stack", [P, H, N], F32R)
        k_stack = sb("k_stack", [P, H, N], F32R)
        t1_hi, t1_lo = q_stack, k_stack
        probs = sb("probs", [P, RING, N])
        A.y = probs[:, 0:2, :].rearrange("p a (t d) -> p (a t) d", d=D)
        A.e, B.e = A.val, B.xn
        neg_max = sb("neg_max", [P, BLOCKS])
        den = sb("den", [P, BLOCKS])
        rden = sb("rden", [P, BLOCKS])
        adjT = sb("adjT", [P, NT, N], BF16)
        maskT = adjT
        cmax = sb("cmax", [P, 1])
        cbias = sb("cbias", [P, 1])
        rgf = sb("rgf", [3 * DK, N])
        r_split = sb("r_split", [2 * DK, N], F32R)
        r_all = sb("r_all", [P, G, N])
        gf = sb("gf", [P, NT, 2 * DK])
        dT = sb("dT", [P, N])
        rden2 = sb("rden2", [P, C, NT * G])
        sj3 = sb("sj3", [P, NT * 2])
        neg3 = sb("neg3", [P, NT])
        den3 = sb("den3", [P, NT])
        rden3 = sb("rden3", [P, NT])

        weights_in = signal("weights_in")
        consts = signal("consts")
        set_v = signal("set_v")
        w1_turned = signal("w1_turned")
        attn_turned = signal("attn_turned")
        attnT_ok = signal("attnT_ok")
        aw_psum = signal("aw_psum")
        aw_ok = signal("aw_ok")
        m1_psum = signal("m1_psum")
        ready = signal("ready")
        x_loaded = signal("x_loaded", 16)
        adj_loaded = signal("adj_loaded", 32)
        mask_ready = signal("mask_ready", 2)
        stacked = [signal(f"{n}_stacked", C * STACK) for n in "qk"]
        stacked_rest = [signal(f"{n}_stacked_rest", C * STACK_REST) for n in "qk"]
        stored = signal("stored", 16)
        for S, norms, turns in ((A, 2, 3), (B, 2, 2)):
            n = S.name
            S.stat = signal(f"{n}_stat", norms)
            S.aggr = signal(f"{n}_aggr", norms)
            S.eps_in = signal(f"{n}_eps_in", norms)
            S.rstd_ok = signal(f"{n}_rstd_ok", norms)
            S.normed = signal(f"{n}_normed", norms)
            S.hT_psum = signal(f"{n}_hT_psum", turns * C)
            S.hT_hi_ok = signal(f"{n}_hT_hi_ok", turns * C)
            S.hT_lo_ok = signal(f"{n}_hT_lo_ok", turns * C)
            S.v_psum = signal(f"{n}_v_psum", 2)
            S.v_ok = signal(f"{n}_v_ok", 2)
            S.pv = signal(f"{n}_pv", C)
            S.oT_ok = signal(f"{n}_oT_ok", C)
            S.o_psum = signal(f"{n}_o_psum", C)
            S.rd = signal(f"{n}_rd", C)
            S.o_ok = signal(f"{n}_o_ok", C)
            S.less_one = signal(f"{n}_less_one")
            S.exped = signal(f"{n}_exped")
            S.upper_part = signal(f"{n}_upper_part")
            S.x_ok = signal(f"{n}_x_ok")
        qk_psum = signal("qk_psum", 2 * C)
        qk_hi_ok = signal("qk_hi_ok", 2 * C)
        qk_lo_ok = signal("qk_lo_ok", 2 * C)
        scored = signal("scored", BLOCKS)
        masked = signal("masked", BLOCKS)
        exps = signal("exps", BLOCKS)
        turned = signal("turned", BLOCKS)
        kept = signal("kept", BLOCKS)
        wo_psum = signal("wo_psum", 2)
        res0 = signal("res0", 2)
        h1_psum = signal("h1_psum", 2)
        h1_ok = signal("h1_ok", 2)
        p1_psum = signal("p1_psum", C)
        p1_hi_ok = signal("p1_hi_ok", C)
        p1_lo_ok = signal("p1_lo_ok", C)
        o1_psum = signal("o1_psum", 2)
        rd1 = signal("rd1")
        y1_ok = signal("y1_ok", 2)
        mT_psum = signal("mT_psum", NT)
        maskT_ok = signal("maskT_ok")
        adjT_ok = signal("adjT_ok", NT)
        s2_psum = signal("s2_psum")
        cmax_part = signal("cmax_part", 2)
        cbias_ok = signal("cbias_ok")
        rgf_ok = signal("rgf_ok")
        r_hi = signal("r_hi")
        r_ok = signal("r_ok")
        gf_psum = signal("gf_psum")
        gf_ok = signal("gf_ok")
        r_psum = signal("r_psum", H)
        r_all_ok = signal("r_all_ok", H)
        w2_ok = signal("w2_ok", C * NT)
        w2_used = signal("w2_used", C * NT)
        s3_psum = signal("s3_psum")
        sj3_ok = signal("sj3_ok")
        v3_psum = signal("v3_psum", 2)
        v3_ok = signal("v3_ok")
        u3 = signal("u3", NT)
        leaky3 = signal("leaky3", NT)
        neg3_ok = signal("neg3_ok", NT)
        att3 = signal("att3", NT)
        rd3 = signal("rd3", NT)
        val3_ok = signal("val3_ok", NT)
        o3_psum = signal("o3_psum", 2)
        y3_ok = signal("y3_ok")
        slope_part = signal("slope_part")
        final_ok = signal("final_ok")

        raw = A.probsT[:, :, :].rearrange("p w (c d) -> p w c d", c=C)
        raw2 = B.probsT[:, :, :].rearrange("p w n -> p (w n)")
        a2_bc = raw2[:, 0:2 * D].rearrange("p (h s d) -> p h s d", h=H, s=2)
        a3_bc = raw2[:, 2 * D:4 * D].rearrange("p (s d) -> p s d", s=2)
        prod = raw2[:, 4 * D:6 * D].rearrange("p (c d) -> p c d", c=C)
        wa2 = raw2[:, 2048:2048 + C * P].rearrange("p (c m) -> p c m", c=C)
        wi3 = raw2[:, 2304:2304 + C * P].rearrange("p (c m) -> p c m", c=C)
        wj3 = raw2[:, 2560:2560 + C * 2].rearrange("p (c m) -> p c m", c=C)
        aw = probs[:, 1, :].rearrange("p (c d) -> p c d", c=C)
        attn_t = probs[:, 0, :].rearrange("p (c d) -> p c d", c=C)
        pick_f = raw2[0:2 * DK, 3072:3072 + H * P].rearrange("p (h m) -> p h m", h=H)
        n_raw = len(MATRICES)

        alone, both = interleave(steps_a(), []), interleave(steps_a(), steps_b())
        both_last, rest = interleave(steps_a(last=True), steps_b()), interleave([], steps_b(last=True))

        def batches(engine, steps):
            def run(order, b, s):
                for stream, name, k in order:
                    if (stream, name) not in steps:
                        continue
                    ahead = (stream == "A") + name.endswith("_next")
                    steps[stream, name](b - 1 + ahead, s if ahead == 1 else 1 - s, k)

            run([("A", name, k) for name, k in (("load_next", 0), ("edges_next", 0), ("edges_next", 1),
                                                ("stats_next", 0), ("norm_next", 0), ("turn_norm_next", 0),
                                                ("qk_next", 0), ("qk_next", 1))], -1, 1)
            run(alone, 0, 0)
            run([("B", "masks_next", m) for m in range(NT)], 0, 0)
            run(both, 1, 1)
            with engine.Fori(1, BATCH // 2 - 1) as i:
                run(both, 2 * i, 0)
                run(both, 2 * i + 1, 1)
            run(both, BATCH - 2, 0)
            run(both_last, BATCH - 1, 1)
            run(rest, BATCH, 0)

        dve_passed = ctx.enter_context(nc.semaphore("dve_passed"))
        pool_passed = ctx.enter_context(nc.semaphore("pool_passed"))

        def stack_quarters(engine, j, quarters, signals):
            c, which = j // 2, j % 2
            hi, lo = qk_hi[:, which, :], qk_lo[:, which, :]
            dst, parts = ((q_stack, (hi, hi, lo, lo)), (k_stack, (hi, lo, hi, lo)))[which]
            for r in quarters:
                for g in range(G):
                    engine.dma_start(dst[DK * r:DK * (r + 1), G * c + g, :].bitcast(F32),
                                     parts[r][DK * g:DK * (g + 1), :].bitcast(F32)).then_inc(signals[which].sem, 16)

        block = ctx.enter_context(nc.Block())

        @block.sync
        def _(sp):
            for i, w in enumerate([Wq, Wk, Wv, Wo, W1, attn, W2, W3]):
                sp.dma_start(raw[:, i, :, :], w.rearrange("(c p) d -> p c d", p=P)).then_inc(weights_in.sem, 16)
            sp.dma_start(t1_bias[:, :], b1.rearrange("(c p) -> p c", p=P), allow_slow_non_contiguous=True
                         ).then_inc(weights_in.sem, 16)
            sp.dma_start(b1_row[:, :], b1.rearrange("(o d) -> o d", o=1).broadcast_to([P, D])).then_inc(weights_in.sem, 16)
            sp.dma_start(raw2[:, 0:2 * D], a2.rearrange("h d -> (h d)").rearrange("(o d) -> o d", o=1).broadcast_to([P, 2 * D])).then_inc(weights_in.sem, 16)
            sp.dma_start(raw2[:, 2 * D:4 * D], a3.rearrange("d o -> o d").broadcast_to([P, 2 * D])).then_inc(weights_in.sem, 16)

            def load(b, s, k):
                if later(b, 1):
                    sp.wait_ge(res0.sem, res0.at(b, 0))
                sp.dma_start(x_in[:, :, :], x_dram[b]).then_inc(x_loaded.sem, 16)
                for half in range(2):
                    if later(b, 1) or half:
                        sp.wait_ge(mask_ready.sem, mask_ready.at(b, half))
                    sp.dma_start(adj_in[:, :, :], adj_dram[b, :, half * 2:half * 2 + 2, :]).then_inc(adj_loaded.sem, 16)

            def stack(b, s, j):
                if j == 0 and later(b, 1):
                    sp.wait_ge(scored.sem, scored.at(b - 1, BLOCKS))
                sp.wait_ge(qk_hi_ok.sem, qk_hi_ok.at(b, j + 1))
                sp.wait_ge(qk_lo_ok.sem, qk_lo_ok.at(b, j + 1))
                stack_quarters(sp, j, range(SP_QUARTERS), stacked)

            batches(sp, {("A", "load_next"): load, ("A", "qk"): stack, ("A", "qk_next"): stack})

        @block.gpsimd
        def _(pool):
            pool.memset(ident[:, :], 0.0).then_inc(consts.sem, 1)
            pool.memset(pick_f, 0.0).then_inc(consts.sem, 1)
            pool.memset(wa2, 0.0).then_inc(consts.sem, 1)
            pool.memset(halves[:, :], -0.5).then_inc(consts.sem, 1)
            for q, exponent in enumerate((SLOPE - 1, 1 - SLOPE, SLOPE)):
                pool.wait_ge(consts.sem, 4 + q)
                pool.memset(coef[q * DK:(q + 1) * DK, :], exponent).then_inc(consts.sem, 1)
            pool.wait_ge(consts.sem, 7)
            pool.affine_select(out=ident[:, :], in_=ident[:, :], compare_op=ALU.not_equal, fill=1.0,
                               base=0, pattern=[[-1, P]], channel_multiplier=1).then_inc(consts.sem, 1)
            pool.affine_select(out=pick_f, in_=pick_f, compare_op=ALU.not_equal, fill=1.0,
                               base=0, pattern=[[-1, H], [0, P]], channel_multiplier=1).then_inc(consts.sem, 1)
            pool.wait_ge(consts.sem, 9)
            pool.affine_select(out=pick_f, in_=pick_f, compare_op=ALU.not_equal, fill=1.0,
                               base=-DK, pattern=[[-1, H], [0, P]], channel_multiplier=1).then_inc(consts.sem, 1)
            pool.tensor_copy(ident_bf[:, :], ident[:, :]).then_inc(consts.sem, 1)

            def edges(b, s, half):
                if half == 0 and later(b, 2):
                    pool.wait_ge(mT_psum.sem, mT_psum.at(b - 2, NT))
                pool.wait_ge(adj_loaded.sem, adj_loaded.at(b, 16 * (half + 1)))
                pool.sem_inc(pool_passed)
                pool.tensor_scalar(mask[s][:, half * 2:half * 2 + 2, :], adj_in[:, :, :], -1.0, -MASKED,
                                   ALU.add, ALU.mult).then_inc(mask_ready.sem, 1)

            def rstd(S):
                def stats(b, s, k):
                    pool.wait_ge(S.eps_in.sem, S.eps_in.at(b, k + 1))
                    pool.tensor_tensor(S.rstd[:, :], S.vareps[:, :], halves[:, :], ALU.pow).then_inc(S.rstd_ok.sem, 1)
                return stats

            def edge_mask(b, s, k):
                pool.wait_ge(w2_ok.sem, w2_ok.at(b, C * NT))
                pool.sem_inc(pool_passed)
                pool.tensor_scalar(maskT[:, :, :], adjT[:, :, :], -1.0, -MASKED,
                                   ALU.add, ALU.mult).then_inc(maskT_ok.sem, 1)

            def store(b, s, k):
                pool.wait_ge(y3_ok.sem, y3_ok.at(b, 1))
                pool.tensor_tensor(x_mid[s][:, :, :], x_mid[s][:, :, :], B.y[:, :, :], ALU.add).then_inc(final_ok.sem, 1)
                pool.wait_ge(final_ok.sem, final_ok.at(b, 1))
                pool.dma_start(out_dram[b], x_mid[s][:, :, :]).then_inc(stored.sem, 16)

            def less_one(S, k):
                def norm(b, s, i):
                    if i == k:
                        pool.wait_ge(S.normed.sem, S.normed.at(b, i + 1))
                        pool.sem_inc(pool_passed)
                        pool.tensor_scalar(x_mid[s][:, :, :], x_mid[s][:, :, :], 1.0, -1.0,
                                           ALU.mult, ALU.add).then_inc(S.less_one.sem, 1)
                return norm

            def stack(b, s, j):
                if j == 0 and later(b, 1):
                    pool.wait_ge(scored.sem, scored.at(b - 1, BLOCKS))
                pool.wait_ge(qk_hi_ok.sem, qk_hi_ok.at(b, j + 1))
                pool.wait_ge(qk_lo_ok.sem, qk_lo_ok.at(b, j + 1))
                pool.sem_inc(pool_passed)
                stack_quarters(pool, j, range(SP_QUARTERS, 4), stacked_rest)

            batches(pool, {("A", "qk"): stack, ("A", "qk_next"): stack,
                           ("A", "edges_next"): edges, ("A", "stats_next"): rstd(A), ("A", "stats"): rstd(A),
                           ("B", "stats"): rstd(B), ("A", "norm"): less_one(A, 1), ("B", "norm"): less_one(B, 0),
                           ("B", "elu2"): edge_mask, ("B", "store"): store})
            pool.wait_ge(stored.sem, stored.at(BATCH - 1, 16))

        @block.tensor
        def _(pe):
            def three(psum, lhs, rhs, first=True, last=True):
                n = len(lhs)
                for c in range(n):
                    (lh, ll), (rh, rl) = lhs[c], rhs[c]
                    for i, (l, r) in enumerate(((lh, rh), (lh, rl), (ll, rh))):
                        mm = pe.matmul(psum, l, r, start=first and c == 0 and i == 0,
                                       stop=last and c == n - 1 and i == 2)
                return mm

            def cols(hi, lo, a, z):
                return [(hi[:, c, a:z], lo[:, c, a:z]) for c in range(C)]

            pe.wait_ge(weights_in.sem, 16 * (n_raw + 4))
            pe.wait_ge(consts.sem, CONSTS)
            for oc in range(C):
                for ic in range(C):
                    mm = pe.transpose(A.pair[:, ic * D + oc * P:ic * D + (oc + 1) * P],
                                      raw[:, 4, oc, ic * P:(ic + 1) * P], ident[:, :])
            mm.then_inc(w1_turned.sem, 1)
            for jc in range(C):
                for kc in range(C):
                    mm = pe.transpose(B.pair[:, kc * D + jc * P:kc * D + (jc + 1) * P],
                                      raw[:, 5, jc, kc * P:(kc + 1) * P], ident[:, :])
            mm.then_inc(attn_turned.sem, 1)
            pe.wait_ge(attnT_ok.sem, 1)
            for jc in range(C):
                for kc in range(C):
                    mm = pe.matmul(B.pair[:, jc * D:(jc + 1) * D], attn_t[:, kc, jc * P:(jc + 1) * P],
                                   raw[:, 4, kc, :], start=kc == 0, stop=kc == C - 1)
            mm.then_inc(aw_psum.sem, 1)
            pe.wait_ge(aw_ok.sem, 1)
            for ic in range(C):
                for jc in range(C):
                    mm = pe.matmul(A.bank[0][:, ic * D:(ic + 1) * D], raw[:, 4, jc, ic * P:(ic + 1) * P],
                                   aw[:, jc, :], start=jc == 0, stop=jc == C - 1)
            for ic in range(C):
                for jc in range(C):
                    mm = pe.matmul(A.bank[1][:, ic:ic + 1], aw[:, jc, ic * P:(ic + 1) * P],
                                   t1_bias[:, jc:jc + 1], start=jc == 0, stop=jc == C - 1)
            mm.then_inc(m1_psum.sem, 1)
            pe.wait_ge(ready.sem, 1)

            def turn_norm(S, b, k):
                for c in range(C):
                    for t in range(NT):
                        mm = pe.transpose(S.pair[:, c * N + t * P:c * N + (t + 1) * P],
                                          S.xn[:, t, c * P:(c + 1) * P], ident[:, :])
                    mm.then_inc(S.hT_psum.sem, 1)

            def halves_in(S, b, k):
                pe.wait_ge(S.hT_hi_ok.sem, S.hT_hi_ok.at(b, C * k))
                pe.wait_ge(S.hT_lo_ok.sem, S.hT_lo_ok.at(b, C * k))

            def values(S, b, wh, wl, psum):
                for t in range(NT):
                    mm = three(S.pair[:, t * D:(t + 1) * D], cols(S.hT_hi, S.hT_lo, t * P, (t + 1) * P),
                               cols(wh, wl, 0, D))
                    if t % (NT // 2) == NT // 2 - 1:
                        mm.then_inc(psum.sem, 1)

            def turn_norm_a(b, s, k):
                pe.wait_ge(A.normed.sem, A.normed.at(b, k + 1))
                if k == 0:
                    if later(b, 1):
                        pe.wait_ge(masked.sem, masked.at(b - 1, BLOCKS))
                turn_norm(A, b, k)

            def qk(b, s, j):
                if j == 0:
                    halves_in(A, b, 1)
                if j >= 2:
                    pe.wait_ge(masked.sem, masked.at(b, QK_AFTER - 3 + j))
                w = ("Wq", "Wk")[j % 2]
                c = j // 2
                three(A.pair[:, (j % 2) * N:(j % 2 + 1) * N], cols(w_hi[w], w_lo[w], c * P, (c + 1) * P),
                      cols(A.hT_hi, A.hT_lo, 0, N)).then_inc(qk_psum.sem, 1)

            def v(b, s, k):
                if later(b, 1):
                    pe.wait_ge(y1_ok.sem, y1_ok.at(b - 1, 2))
                else:
                    pe.wait_ge(qk_lo_ok.sem, qk_lo_ok.at(b, 2))
                values(A, b, w_hi["Wv"], w_lo["Wv"], A.v_psum)

            def score0(b, s, k):
                c, t, g = k // (G * NT), k // G % NT, k % G
                h = G * c + g
                if k % (G * NT) == 0:
                    for which in range(2):
                        pe.wait_ge(stacked[which].sem, stacked[which].at(b, STACK * (c + 1)))
                        pe.wait_ge(stacked_rest[which].sem, stacked_rest[which].at(b, STACK_REST * (c + 1)))
                if k == 0:
                    pe.wait_ge(A.v_ok.sem, A.v_ok.at(b, 2))
                if QK_AFTER <= k < QK_AFTER + 2:
                    pe.wait_ge(qk_lo_ok.sem, qk_lo_ok.at(b, 3 + k - QK_AFTER))
                elif k >= 2:
                    pe.wait_ge(masked.sem, masked.at(b, k - 1))
                bank = A.pair[:, (k % 2) * N:(k % 2 + 1) * N]
                pe.matmul(bank, q_stack[:, h, t * P:(t + 1) * P], k_stack[:, h, :],
                          start=True, stop=True).then_inc(scored.sem, 1)

            def turn(b, s, k):
                pe.wait_ge(exps.sem, exps.at(b, k + 1))
                if k > 0:
                    pe.wait_ge(kept.sem, kept.at(b, k))
                if k == G * NT + OUT_AFTER or k == L0_BLOCKS:
                    pe.wait_ge(A.o_ok.sem, A.o_ok.at(b, k // (G * NT)))
                for m in range(NT):
                    mm = pe.transpose(A.bank[0][:, m * P:(m + 1) * P], probs[:, k % RING, m * P:(m + 1) * P],
                                      ident[:, :])
                mm.then_inc(turned.sem, 1)

            def turn_back(dst, src):
                for t in range(NT):
                    mm = pe.transpose(dst[:, t * P:(t + 1) * P], src[:, t * P:(t + 1) * P], ident[:, :])
                return mm

            def pv0(b, s, u):
                c, t = u // NT, u % NT
                pe.wait_ge(kept.sem, kept.at(b, G * (u + 1)))
                for m in range(NT):
                    for g in range(G):
                        h = G * c + g
                        mm = pe.matmul(A.bank[1][DK * g:DK * (g + 1), t * P:(t + 1) * P],
                                       A.val[:, m, h * DK:(h + 1) * DK],
                                       A.probsT[:, u % 2 * G + g, m * P:(m + 1) * P], start=m == 0, stop=m == NT - 1)
                if t == NT - 1:
                    mm.then_inc(A.pv.sem, 1)

            def out0(b, s, c):
                blocks = G * NT * (c + 1) + (OUT_AFTER if c == 0 else 0)
                pe.wait_ge(kept.sem, kept.at(b, blocks))
                pe.wait_ge(A.oT_ok.sem, A.oT_ok.at(b, c + 1))
                turn_back(A.bank[0], A.oT).then_inc(A.o_psum.sem, 1)

            def turn_out(b, s, k):
                pe.wait_ge(A.o_ok.sem, A.o_ok.at(b, C))
                turn_norm(A, b, 1)

            def wo(b, s, k):
                halves_in(A, b, 2)
                values(A, b, w_hi["Wo"], w_lo["Wo"], wo_psum)

            def h1(b, s, k):
                halves_in(A, b, 3)
                values(A, b, w_hi["W1T"], w_lo["W1T"], h1_psum)

            def proj1(b, s, c):
                pe.wait_ge(h1_ok.sem, h1_ok.at(b, c + 1))
                three(A.pair[:, c * N:(c + 1) * N], cols(w_hi["M1"], w_lo["M1"], c * P, (c + 1) * P),
                      cols(A.hT_hi, A.hT_lo, 0, N)).then_inc(p1_psum.sem, 1)

            def score1(b, s, m):
                if m == 0:
                    pe.wait_ge(p1_hi_ok.sem, p1_hi_ok.at(b, C))
                    pe.wait_ge(p1_lo_ok.sem, p1_lo_ok.at(b, C))
                if m >= 2:
                    pe.wait_ge(masked.sem, masked.at(b, L0_BLOCKS + m - 1))
                three(A.pair[:, (m % 2) * N:(m % 2 + 1) * N], cols(t1_hi, t1_lo, m * P, (m + 1) * P),
                      cols(A.hT_hi, A.hT_lo, 0, N)).then_inc(scored.sem, 1)

            def rows_product(S, weights, value, psum):
                for i in range(NT):
                    for j in range(NT):
                        mm = pe.matmul(S.pair[:, i * D:(i + 1) * D], weights(i, j),
                                       value[:, j, :], start=j == 0, stop=j == NT - 1)
                    if i % (NT // 2) == NT // 2 - 1:
                        mm.then_inc(psum.sem, 1)

            def pv1(b, s, k):
                pe.wait_ge(kept.sem, kept.at(b, BLOCKS))
                if isinstance(b, int) and b == BATCH - 1:
                    pe.wait_ge(masked.sem, masked.at(b, BLOCKS))
                else:
                    pe.wait_ge(qk_lo_ok.sem, qk_lo_ok.at(b + 1, 2))
                rows_product(A, lambda i, j: A.probsT[:, i, j * P:(j + 1) * P], A.val, o1_psum)

            def masks(b, s, m):
                bank = B.bank[m % 2][:, :].bitcast(BF16)
                if m == 0:
                    pe.wait_ge(mask_ready.sem, mask_ready.at(b, 2))
                    if later(b, 1):
                        pe.wait_ge(u3.sem, u3.at(b - 1, NT))
                if m >= 2:
                    pe.wait_ge(adjT_ok.sem, adjT_ok.at(b, m - 1))
                for t in range(NT):
                    mm = pe.transpose(bank[:, t * P:(t + 1) * P], mask[s][:, t, m * P:(m + 1) * P], ident_bf[:, :])
                mm.then_inc(mT_psum.sem, 1)

            def turn_norm_b(b, s, k):
                pe.wait_ge(B.normed.sem, B.normed.at(b, k + 1))
                if k == 0:
                    if later(b, 1):
                        pe.wait_ge(y3_ok.sem, y3_ok.at(b - 1, 1))
                turn_norm(B, b, k)

            def sums2(b, s, k):
                halves_in(B, b, 1)
                pe.wait_ge(adjT_ok.sem, adjT_ok.at(b, NT))
                three(B.bank[0][:, :], cols(wa2_hi, wa2_lo, 0, P), cols(B.hT_hi, B.hT_lo, 0, N)).then_inc(s2_psum.sem, 1)

            def v2(b, s, k):
                values(B, b, w_hi["W2"], w_lo["W2"], B.v_psum)

            def factors(b, s, k):
                pe.wait_ge(rgf_ok.sem, rgf_ok.at(b, 1))
                for t in range(NT):
                    mm = pe.transpose(B.bank[1][:, t * 3 * DK:(t + 1) * 3 * DK], rgf[:, t * P:(t + 1) * P],
                                      ident[0:3 * DK, 0:3 * DK])
                mm.then_inc(gf_psum.sem, 1)

            def spread(b, s, h):
                if h == 0:
                    pe.wait_ge(r_ok.sem, r_ok.at(b, 1))
                    pe.wait_ge(B.v_ok.sem, B.v_ok.at(b, 2))
                if h >= 2:
                    pe.wait_ge(r_all_ok.sem, r_all_ok.at(b, h - 1))
                pe.matmul(B.pair[:, (h % 2) * N:(h % 2 + 1) * N], pick[:, h, :], r_split[:, :],
                          start=True, stop=True).then_inc(r_psum.sem, 1)

            def pv2(b, s, k):
                u, dens = k // 2, k % 2
                c, j = u // NT, u % NT
                if not dens:
                    pe.wait_ge(w2_ok.sem, w2_ok.at(b, u + 1))
                    if u == 0:
                        pe.wait_ge(gf_ok.sem, gf_ok.at(b, 1))
                    if u == NT:
                        pe.wait_ge(B.oT_ok.sem, B.oT_ok.at(b, 1))
                for g in range(G):
                    h = G * c + g
                    stationary = gf[:, j, DK + h:DK + h + 1].broadcast_to([P, DK]) if dens else \
                        B.val[:, j, h * DK:(h + 1) * DK]
                    mm = pe.matmul(B.bank[dens][DK * g:DK * (g + 1), :], stationary,
                                   B.probsT[:, u % 2 * G + g, :], start=j == 0, stop=j == NT - 1)
                if dens:
                    mm.then_inc(w2_used.sem, 1)

            def out2(b, s, c):
                pe.wait_ge(B.oT_ok.sem, B.oT_ok.at(b, c + 1))
                if c == 0:
                    pe.wait_ge(r_all_ok.sem, r_all_ok.at(b, H))
                else:
                    pe.wait_ge(B.o_ok.sem, B.o_ok.at(b, c))
                turn_back(B.pair[:, 0:N], B.oT)
                turn_back(B.pair[:, N:2 * N], dT).then_inc(B.o_psum.sem, 1)

            def sums3(b, s, k):
                halves_in(B, b, 2)
                three(B.bank[0][:, :], cols(wi3_hi, wi3_lo, 0, P), cols(B.hT_hi, B.hT_lo, 0, N))
                for t in range(NT):
                    mm = three(B.bank[1][:, 2 * t:2 * t + 2], cols(B.hT_hi, B.hT_lo, t * P, (t + 1) * P),
                               cols(wj3_hi, wj3_lo, 0, 2))
                mm.then_inc(s3_psum.sem, 1)

            def v3(b, s, k):
                values(B, b, w_hi["W3"], w_lo["W3"], v3_psum)

            def pv3(b, s, k):
                pe.wait_ge(att3.sem, att3.at(b, NT))
                pe.wait_ge(val3_ok.sem, val3_ok.at(b, NT))
                rows_product(B, lambda i, j: B.probsT[:, j, i * P:(i + 1) * P], B.val, o3_psum)

            batches(pe, {("A", "turn_norm"): turn_norm_a, ("A", "turn_norm_next"): turn_norm_a, ("A", "turn_out"): turn_out, ("A", "qk"): qk, ("A", "qk_next"): qk, ("A", "v"): v, ("A", "score0"): score0,
                         ("A", "turn"): turn, ("A", "pv0"): pv0, ("A", "out0"): out0, ("A", "wo"): wo, ("A", "h1"): h1,
                         ("A", "proj1"): proj1, ("A", "score1"): score1, ("A", "pv1"): pv1,
                         ("B", "masks_next"): masks, ("B", "turn_norm"): turn_norm_b, ("B", "sums2"): sums2,
                         ("B", "v2"): v2, ("B", "factors"): factors, ("B", "spread"): spread,
                         ("B", "pv2"): pv2, ("B", "out2"): out2, ("B", "sums3"): sums3, ("B", "v3"): v3, ("B", "pv3"): pv3})

        @block.scalar
        def _(act):
            def upper(S, b, k):
                for c in range(C):
                    act.wait_ge(S.hT_psum.sem, S.hT_psum.at(b, C * (k - 1) + c + 1))
                    act.activation(S.hT_hi[:, c, :], S.pair[:, c * N:(c + 1) * N], ACT.Relu).then_inc(S.hT_hi_ok.sem, 1)

            def turn_norm_a(b, s, k):
                upper(A, b, 1 + 2 * k)

            def qk(b, s, j):
                which = j % 2
                if later(b, 1) or j // 2:
                    act.wait_ge(stacked[which].sem, stacked[which].at(b, STACK * (j // 2)))
                    act.wait_ge(stacked_rest[which].sem, stacked_rest[which].at(b, STACK_REST * (j // 2)))
                act.wait_ge(qk_psum.sem, qk_psum.at(b, j + 1))
                act.activation(qk_hi[:, which, :], A.pair[:, which * N:(which + 1) * N], ACT.Copy).then_inc(qk_hi_ok.sem, 1)

            def v(b, s, k):
                if later(b, 1):
                    act.wait_ge(A.x_ok.sem, A.x_ok.at(b - 1, 1))
                for half in range(2):
                    act.wait_ge(A.v_psum.sem, A.v_psum.at(b, half + 1))
                    act.activation(A.val[:, 2 * half:2 * half + 2, :].rearrange("p t d -> p (t d)"),
                                   A.pair[:, half * N:(half + 1) * N], ACT.Copy).then_inc(A.v_ok.sem, 1)

            def exp(b, s, k):
                act.wait_ge(masked.sem, masked.at(b, k + 1))
                act.activation(probs[:, k % RING, :], probs[:, k % RING, :], ACT.Exp, scale=-1.0,
                               bias=neg_max[:, k:k + 1], accum_out=den[:, k:k + 1]).then_inc(exps.sem, 1)

            def turn(b, s, k):
                slot = k % (2 * G)
                act.wait_ge(turned.sem, turned.at(b, k + 1))
                act.activation(A.probsT[:, slot, :], A.bank[0][:, :], ACT.Copy).then_inc(kept.sem, 1)

            def copy0(b, s, c):
                act.wait_ge(A.pv.sem, A.pv.at(b, c + 1))
                act.activation(A.oT[:, :], A.bank[1][:, :], ACT.Copy).then_inc(A.oT_ok.sem, 1)

            def turn_out(b, s, k):
                upper(A, b, 2)

            def proj1(b, s, c):
                act.wait_ge(p1_psum.sem, p1_psum.at(b, c + 1))
                act.activation(t1_hi[:, c, :], A.pair[:, c * N:(c + 1) * N], ACT.Identity,
                               bias=t1_bias[:, c:c + 1]).then_inc(p1_hi_ok.sem, 1)

            def elu1(b, s, k):
                act.wait_ge(y1_ok.sem, y1_ok.at(b, 2))
                act.activation(A.e[:, :, :], A.y[:, :, :], ACT.Exp).then_inc(A.exped.sem, 1)

            def elu2(b, s, k):
                act.wait_ge(B.o_ok.sem, B.o_ok.at(b, C))
                act.activation(B.e[:, :, :], B.y[:, :, :], ACT.Exp).then_inc(B.exped.sem, 1)

            def turn_norm_b(b, s, k):
                upper(B, b, 1 + k)

            def factors(b, s, k):
                act.wait_ge(cbias_ok.sem, cbias_ok.at(b, 1))
                act.activation(rgf[:, :], B.bank[0][0:3 * DK, :], ACT.Exp, scale=coef[0:3 * DK, :],
                               bias=cbias[0:3 * DK, :]).then_inc(rgf_ok.sem, 1)
                act.wait_ge(gf_psum.sem, gf_psum.at(b, 1))
                act.activation(gf[:, :, :], B.bank[1][:, 0:NT * 3 * DK].rearrange("p (t r) -> p t r", t=NT)[:, :, DK:3 * DK],
                               ACT.Copy).then_inc(gf_ok.sem, 1)

            def spread(b, s, h):
                act.wait_ge(r_psum.sem, r_psum.at(b, h + 1))
                if h == G:
                    act.wait_ge(w2_ok.sem, w2_ok.at(b, NT))
                act.activation(r_all[:, h % G, :], B.pair[:, (h % 2) * N:(h % 2 + 1) * N], ACT.Copy).then_inc(r_all_ok.sem, 1)

            def copy2(b, s, c):
                act.wait_ge(w2_used.sem, w2_used.at(b, NT * (c + 1)))
                act.activation(B.oT[:, :], B.bank[0][:, :], ACT.Copy)
                act.activation(dT[:, :], B.bank[1][:, :], ACT.Copy).then_inc(B.oT_ok.sem, 1)

            def sum_edges(j):
                act.activation(B.probsT[:, G + j % 2, :], B.bank[0][:, :], ACT.Identity,
                               bias=sj3[:, 2 * j:2 * j + 1]).then_inc(u3.sem, 1)

            def sums3(b, s, k):
                act.wait_ge(s3_psum.sem, s3_psum.at(b, 1))
                act.activation(sj3[:, :], B.bank[1][:, 0:NT * 2], ACT.Copy).then_inc(sj3_ok.sem, 1)
                act.wait_ge(sj3_ok.sem, sj3_ok.at(b, 1))
                for j in range(2):
                    sum_edges(j)

            def v3(b, s, k):
                act.wait_ge(v3_psum.sem, v3_psum.at(b, 2))
                act.activation(B.val[:, :, :].rearrange("p t d -> p (t d)"), B.pair[:, :], ACT.Copy).then_inc(v3_ok.sem, 1)

            def edges3(b, s, j):
                if j + 2 < NT:
                    act.wait_ge(leaky3.sem, leaky3.at(b, j + 1))
                    sum_edges(j + 2)
                act.wait_ge(neg3_ok.sem, neg3_ok.at(b, j + 1))
                act.activation(B.probsT[:, j, :], B.probsT[:, G + 2 + j % 2, :], ACT.Exp, scale=-1.0, bias=neg3[:, j:j + 1],
                               accum_out=den3[:, j:j + 1]).then_inc(att3.sem, 1)

            def store(b, s, k):
                act.wait_ge(slope_part.sem, slope_part.at(b, 1))
                act.activation(B.y[:, :, :].rearrange("p t d -> p (t d)"), B.pair[:, :], ACT.Relu,
                               scale=1 - SLOPE).then_inc(y3_ok.sem, 1)

            act.wait_ge(consts.sem, CONSTS)
            act.wait_ge(attn_turned.sem, 1)
            act.activation(attn_t.rearrange("p c d -> p (c d)"), B.pair[:, 0:C * D], ACT.Copy).then_inc(attnT_ok.sem, 1)
            act.wait_ge(aw_psum.sem, 1)
            act.activation(aw.rearrange("p c d -> p (c d)"), B.pair[:, 0:C * D], ACT.Copy).then_inc(aw_ok.sem, 1)
            act.wait_ge(ready.sem, 1)
            batches(act, {("A", "turn_norm"): turn_norm_a, ("A", "turn_norm_next"): turn_norm_a, ("A", "qk"): qk, ("A", "qk_next"): qk, ("A", "v"): v, ("A", "exp"): exp,
                          ("A", "turn"): turn, ("A", "copy0"): copy0, ("A", "turn_out"): turn_out,
                          ("A", "proj1"): proj1, ("A", "elu1"): elu1,
                          ("B", "turn_norm"): turn_norm_b, ("B", "factors"): factors,
                          ("B", "spread"): spread, ("B", "copy2"): copy2, ("B", "elu2"): elu2,
                          ("B", "sums3"): sums3, ("B", "v3"): v3, ("B", "edges3"): edges3, ("B", "store"): store})

        @block.vector
        def _(dve):
            steps_done = [0]

            def link(ins):
                steps_done[0] += 1
                ins.then_inc(set_v.sem, 1)
                dve.wait_ge(set_v.sem, steps_done[0])

            def split(hi, lo, value):
                link(dve.tensor_copy(hi, value))
                return dve.tensor_tensor(lo, value, hi.bitcast(F32), ALU.subtract)

            dve.wait_ge(weights_in.sem, 16 * (n_raw + 4))
            dve.wait_ge(consts.sem, CONSTS)
            link(dve.tensor_copy(pick[:, :, :], pick_f))
            w2_heads = raw[:, MATRICES.index("W2"), :, :].rearrange("p c (h d) -> p c h d", h=H)
            prod_heads = prod.rearrange("p c (h d) -> p c h d", h=H)
            for part, where in ((0, (0,)), (1, (DK, 2 * DK))):
                for c in range(C):
                    link(dve.tensor_tensor(prod_heads[:, c, :, :], w2_heads[:, c, :, :], a2_bc[:, :, part, :], ALU.mult))
                for w in where:
                    link(dve.tensor_reduce(out=wa2[:, :, w:w + H], in_=prod_heads, axis=AX.X, op=ALU.add))
            w3_raw = raw[:, MATRICES.index("W3"), :, :]
            for part, dst in ((0, wi3), (1, wj3)):
                for c in range(C):
                    link(dve.tensor_tensor(prod[:, c, :], w3_raw[:, c, :], a3_bc[:, part, :], ALU.mult))
                    link(dve.tensor_reduce(out=cmax[:, :], in_=prod[:, c, :], axis=AX.X, op=ALU.add, negate=True))
                    link(dve.tensor_copy(dst[:, c, :], cmax[:, :].broadcast_to([P, dst.shape[2]])))
            link(dve.tensor_scalar(raw[:, 0, :, :], raw[:, 0, :, :], -1.0 / math.sqrt(DK), None, ALU.mult))
            dve.wait_ge(m1_psum.sem, 1)
            link(dve.tensor_copy(raw[:, 4, :, :].rearrange("p c d -> p (c d)"), A.pair[:, 0:C * D]))
            link(dve.tensor_scalar(raw[:, 5, :, :].rearrange("p c d -> p (c d)"), A.bank[0][:, :], -1.0, None, ALU.mult))
            link(dve.tensor_scalar(t1_bias[:, :], A.bank[1][:, 0:C], -1.0, None, ALU.mult))
            for i, m in enumerate(MATRICES):
                link(split(w_hi[m][:, :, :], w_lo[m][:, :, :], raw[:, i, :, :]))
            link(split(wa2_hi[:, :, :], wa2_lo[:, :, :], wa2))
            link(split(wi3_hi[:, :, :], wi3_lo[:, :, :], wi3))
            split(wj3_hi[:, :, :], wj3_lo[:, :, :], wj3).then_inc(ready.sem, 1)

            def moments(S, b, k, x):
                for t in range(NT):
                    last = dve.bn_stats(out=S.stats[:, t, :], in_=x[:, t, :])
                last.then_inc(S.stat.sem, 1)
                dve.wait_ge(S.stat.sem, S.stat.at(b, k + 1))
                dve.sem_inc(dve_passed)
                for t in range(NT):
                    last = dve.bn_aggr(out=S.meanvar[:, t, :], in_=S.stats[:, t, :])
                last.then_inc(S.aggr.sem, 1)
                dve.wait_ge(S.aggr.sem, S.aggr.at(b, k + 1))
                dve.tensor_scalar(S.vareps[:, :], S.meanvar[:, :, 1], EPS, None, ALU.add).then_inc(S.eps_in.sem, 1)

            def normalise(S, b, k, x):
                dve.wait_ge(S.rstd_ok.sem, S.rstd_ok.at(b, k + 1))
                for t in range(NT):
                    last = dve.tensor_scalar(S.xn[:, t, :], x[:, t, :], S.meanvar[:, t, 0:1], S.rstd[:, t:t + 1],
                                             ALU.subtract, ALU.mult)
                last.then_inc(S.normed.sem, 1)

            def lower(S, b, k):
                for c in range(C):
                    dve.wait_ge(S.hT_hi_ok.sem, S.hT_hi_ok.at(b, C * (k - 1) + c + 1))
                    dve.scalar_tensor_tensor(out=S.hT_lo[:, c, :], in0=S.pair[:, c * N:(c + 1) * N], scalar=0.0,
                                             in1=S.hT_hi[:, c, :].bitcast(F32),
                                             op0=ALU.max, op1=ALU.subtract).then_inc(S.hT_lo_ok.sem, 1)

            def stats_a(b, s, k):
                if k == 0:
                    dve.wait_ge(x_loaded.sem, x_loaded.at(b, 16))
                    moments(A, b, 0, x_in)
                else:
                    dve.wait_ge(res0.sem, res0.at(b, 2))
                    moments(A, b, 1, x_mid[s])

            def norm_a(b, s, k):
                if k == 0 and later(b, 1):
                    dve.wait_ge(A.hT_psum.sem, A.hT_psum.at(b - 1, 3 * C))
                normalise(A, b, k, x_in if k == 0 else x_mid[s])

            def turn_norm_a(b, s, k):
                lower(A, b, 1 + 2 * k)

            def qk(b, s, j):
                which = j % 2
                dve.wait_ge(qk_hi_ok.sem, qk_hi_ok.at(b, j + 1))
                dve.tensor_tensor(qk_lo[:, which, :], A.pair[:, which * N:(which + 1) * N],
                                  qk_hi[:, which, :].bitcast(F32),
                                  ALU.subtract).then_inc(qk_lo_ok.sem, 1)

            def mask_block(b, s, k):
                t = (k // G if k < L0_BLOCKS else k) % NT
                if k >= RING:
                    dve.wait_ge(turned.sem, turned.at(b, k - RING + 1))
                dve.wait_ge(scored.sem, scored.at(b, k + 1))
                dve.sem_inc(dve_passed)
                dve.tensor_tensor_reduce(out=probs[:, k % RING, :], in0=A.pair[:, (k % 2) * N:(k % 2 + 1) * N],
                                         in1=mask[s][:, t, :], scale=1.0, scalar=3e38, op0=ALU.add,
                                         op1=ALU.min, accum_out=neg_max[:, k:k + 1]).then_inc(masked.sem, 1)

            def score0(b, s, k):
                if k == 0:
                    dve.wait_ge(mask_ready.sem, mask_ready.at(b, 2))
                mask_block(b, s, k)

            def score1(b, s, m):
                mask_block(b, s, L0_BLOCKS + m)

            def out0(b, s, c):
                dve.wait_ge(A.o_psum.sem, A.o_psum.at(b, c + 1))
                cols = slice(c * G * NT, (c + 1) * G * NT)
                dve.reciprocal(rden[:, cols], den[:, cols]).then_inc(A.rd.sem, 1)
                dve.wait_ge(A.rd.sem, A.rd.at(b, c + 1))
                dve.tensor_tensor(
                    A.xn[:, :, c * P:(c + 1) * P].rearrange("p t (g d) -> p t g d", g=G),
                    A.bank[0][:, :].rearrange("p (t g d) -> p t g d", t=NT, g=G),
                    rden[:, cols].rearrange("p (t g o) -> p t g o", t=NT, o=1).broadcast_to([P, NT, G, DK]),
                    ALU.mult).then_inc(A.o_ok.sem, 1)

            def turn_out(b, s, k):
                lower(A, b, 2)

            def wo(b, s, k):
                if later(b, 2):
                    dve.wait_ge(stored.sem, stored.at(b - 2, 16))
                for half in range(2):
                    tiles = slice(2 * half, 2 * half + 2)
                    dve.wait_ge(wo_psum.sem, wo_psum.at(b, half + 1))
                    dve.tensor_tensor(x_mid[s][:, tiles, :].rearrange("p t d -> p (t d)"), A.pair[:, half * N:(half + 1) * N],
                                      x_in[:, tiles, :].rearrange("p t d -> p (t d)"), ALU.add).then_inc(res0.sem, 1)

            def h1(b, s, k):
                for half in range(2):
                    dve.wait_ge(h1_psum.sem, h1_psum.at(b, half + 1))
                    dve.tensor_tensor(A.val[:, 2 * half:2 * half + 2, :],
                                      A.pair[:, half * N:(half + 1) * N].rearrange("p (t d) -> p t d", t=2),
                                      b1_row[:, :].rearrange("p (o d) -> p o d", o=1).broadcast_to([P, 2, D]),
                                      ALU.add).then_inc(h1_ok.sem, 1)

            def proj1(b, s, c):
                dve.wait_ge(p1_hi_ok.sem, p1_hi_ok.at(b, c + 1))
                dve.scalar_tensor_tensor(out=t1_lo[:, c, :], in0=A.pair[:, c * N:(c + 1) * N],
                                         scalar=t1_bias[:, c:c + 1], in1=t1_hi[:, c, :].bitcast(F32),
                                         op0=ALU.add, op1=ALU.subtract).then_inc(p1_lo_ok.sem, 1)

            def elu_add(S, b, s):
                dve.wait_ge(S.less_one.sem, S.less_one.at(b, 1))
                dve.scalar_tensor_tensor(out=x_mid[s][:, :, :], in0=S.y[:, :, :], scalar=0.0, in1=x_mid[s][:, :, :],
                                         op0=ALU.max, op1=ALU.add).then_inc(S.upper_part.sem, 1)
                dve.wait_ge(S.exped.sem, S.exped.at(b, 1))
                dve.wait_ge(S.upper_part.sem, S.upper_part.at(b, 1))
                dve.scalar_tensor_tensor(out=x_mid[s][:, :, :], in0=S.e[:, :, :], scalar=1.0, in1=x_mid[s][:, :, :],
                                         op0=ALU.min, op1=ALU.add).then_inc(S.x_ok.sem, 1)

            def pv1(b, s, k):
                dve.wait_ge(exps.sem, exps.at(b, BLOCKS))
                dve.reciprocal(rden[:, L0_BLOCKS:BLOCKS], den[:, L0_BLOCKS:BLOCKS]).then_inc(rd1.sem, 1)
                dve.wait_ge(rd1.sem, rd1.at(b, 1))
                for half in range(2):
                    blocks = slice(L0_BLOCKS + 2 * half, L0_BLOCKS + 2 * half + 2)
                    dve.wait_ge(o1_psum.sem, o1_psum.at(b, half + 1))
                    dve.tensor_tensor(A.y[:, 2 * half:2 * half + 2, :],
                                      A.pair[:, half * N:(half + 1) * N].rearrange("p (t d) -> p t d", t=2),
                                      rden[:, blocks].rearrange("p (t o) -> p t o", o=1).broadcast_to([P, 2, D]),
                                      ALU.mult).then_inc(y1_ok.sem, 1)

            def elu1(b, s, k):
                dve.wait_ge(y1_ok.sem, y1_ok.at(b, 2))
                elu_add(A, b, s)

            def masks(b, s, m):
                dve.wait_ge(mT_psum.sem, mT_psum.at(b, m + 1))
                if m == 0 and later(b, 1):
                    dve.wait_ge(neg3_ok.sem, neg3_ok.at(b - 1, NT))
                dve.tensor_scalar(adjT[:, m, :], B.bank[m % 2][:, :].bitcast(BF16)[:, 0:N], 1.0, None,
                                  ALU.is_le).then_inc(adjT_ok.sem, 1)

            def stats_b(b, s, k):
                dve.wait_ge((A if k == 0 else B).x_ok.sem, (A if k == 0 else B).x_ok.at(b, 1))
                moments(B, b, k, x_mid[s])

            def norm_b(b, s, k):
                normalise(B, b, k, x_mid[s])

            def turn_norm_b(b, s, k):
                lower(B, b, 1 + k)

            def sums2(b, s, k):
                dve.wait_ge(s2_psum.sem, s2_psum.at(b, 1))
                dve.tensor_reduce(out=cmax[0:3 * DK, :], in_=B.bank[0][0:3 * DK, :], axis=AX.X,
                                  op=ALU.max, negate=True).then_inc(cmax_part.sem, 1)
                dve.wait_ge(cmax_part.sem, cmax_part.at(b, 1))
                dve.tensor_scalar(cmax[0:DK, :], cmax[DK:2 * DK, :], -1.0, None, ALU.mult).then_inc(cmax_part.sem, 1)
                dve.wait_ge(cmax_part.sem, cmax_part.at(b, 2))
                dve.tensor_tensor(cbias[0:3 * DK, :], cmax[0:3 * DK, :], coef[0:3 * DK, :], ALU.mult).then_inc(cbias_ok.sem, 1)

            def factors(b, s, k):
                dve.wait_ge(rgf_ok.sem, rgf_ok.at(b, 1))
                dve.tensor_scalar(r_split[0:DK, :], rgf[0:DK, :], 1.0, None, ALU.min).then_inc(r_hi.sem, 1)
                dve.wait_ge(r_hi.sem, r_hi.at(b, 1))
                dve.scalar_tensor_tensor(out=r_split[DK:2 * DK, :], in0=rgf[0:DK, :], scalar=1.0,
                                         in1=r_split[0:DK, :].bitcast(F32), op0=ALU.min,
                                         op1=ALU.subtract).then_inc(r_ok.sem, 1)
                dve.wait_ge(gf_ok.sem, gf_ok.at(b, 1))
                dve.wait_ge(B.v_psum.sem, B.v_psum.at(b, 2))
                dve.tensor_tensor(
                    B.val[:, :, :].rearrange("p t (h d) -> p t h d", h=H),
                    B.pair[:, :].rearrange("p (t h d) -> p t h d", t=NT, h=H),
                    gf[:, :, DK:DK + H].rearrange("p t (h o) -> p t h o", o=1).broadcast_to([P, NT, H, DK]),
                    ALU.mult).then_inc(B.v_ok.sem, 2)

            def weights2(b, s, k):
                u, g = k // G, k % G
                c, j = u // NT, u % NT
                h = G * c + g
                if u >= 2 and g == 0:
                    dve.wait_ge(w2_used.sem, w2_used.at(b, u - 1))
                if j == 0:
                    dve.wait_ge(r_all_ok.sem, r_all_ok.at(b, h + 1))
                last = dve.scalar_tensor_tensor(out=B.probsT[:, u % 2 * G + g, :], in0=r_all[:, g, :],
                                                scalar=gf[:, j, h:h + 1], in1=adjT[:, j, :],
                                                op0=ALU.max, op1=ALU.mult)
                if g == G - 1:
                    last.then_inc(w2_ok.sem, 1)

            def out2(b, s, c):
                dve.wait_ge(B.o_psum.sem, B.o_psum.at(b, c + 1))
                dve.reciprocal(rden2[:, c, :].rearrange("p (t g) -> p t g", t=NT),
                               B.pair[:, N:2 * N].rearrange("p (t g d) -> p t g d", t=NT, g=G)[:, :, :, 0]).then_inc(B.rd.sem, 1)
                dve.wait_ge(B.rd.sem, B.rd.at(b, c + 1))
                dve.tensor_tensor(
                    B.y[:, :, c * P:(c + 1) * P].rearrange("p t (g d) -> p t g d", g=G),
                    B.pair[:, 0:N].rearrange("p (t g d) -> p t g d", t=NT, g=G),
                    rden2[:, c, :].rearrange("p (t g o) -> p t g o", t=NT, o=1).broadcast_to([P, NT, G, DK]),
                    ALU.mult).then_inc(B.o_ok.sem, 1)

            def elu2(b, s, k):
                dve.wait_ge(B.o_ok.sem, B.o_ok.at(b, C))
                elu_add(B, b, s)

            def edges3(b, s, j):
                dve.wait_ge(u3.sem, u3.at(b, j + 1))
                if j == 0:
                    dve.wait_ge(maskT_ok.sem, maskT_ok.at(b, 1))
                if j >= 2:
                    dve.wait_ge(att3.sem, att3.at(b, j - 1))
                u, row = B.probsT[:, G + j % 2, :], B.probsT[:, G + 2 + j % 2, :]
                dve.scalar_tensor_tensor(out=row, in0=u, scalar=SLOPE, in1=u, op0=ALU.mult,
                                         op1=ALU.min).then_inc(leaky3.sem, 1)
                dve.wait_ge(leaky3.sem, leaky3.at(b, j + 1))
                dve.sem_inc(dve_passed)
                dve.tensor_tensor_reduce(out=row, in0=row, in1=maskT[:, j, :],
                                         scale=1.0, scalar=3e38, op0=ALU.add, op1=ALU.min,
                                         accum_out=neg3[:, j:j + 1]).then_inc(neg3_ok.sem, 1)

            def values3(b, s, j):
                if j == 0:
                    dve.wait_ge(v3_ok.sem, v3_ok.at(b, 1))
                dve.wait_ge(att3.sem, att3.at(b, j + 1))
                dve.reciprocal(rden3[:, j:j + 1], den3[:, j:j + 1]).then_inc(rd3.sem, 1)
                dve.wait_ge(rd3.sem, rd3.at(b, j + 1))
                dve.sem_inc(dve_passed)
                dve.tensor_scalar(B.val[:, j, :], B.val[:, j, :], rden3[:, j:j + 1], None, ALU.mult).then_inc(val3_ok.sem, 1)

            def store(b, s, k):
                dve.wait_ge(o3_psum.sem, o3_psum.at(b, 2))
                dve.scalar_tensor_tensor(out=x_mid[s][:, :, :].rearrange("p t d -> p (t d)"), in0=B.pair[:, :],
                                         scalar=SLOPE, in1=x_mid[s][:, :, :].rearrange("p t d -> p (t d)"),
                                         op0=ALU.mult, op1=ALU.add).then_inc(slope_part.sem, 1)

            batches(dve, {("A", "stats_next"): stats_a, ("A", "stats"): stats_a, ("A", "norm"): norm_a, ("A", "norm_next"): norm_a,
                          ("A", "turn_norm"): turn_norm_a, ("A", "turn_norm_next"): turn_norm_a,
                          ("A", "qk"): qk, ("A", "qk_next"): qk, ("A", "score0"): score0, ("A", "out0"): out0,
                          ("A", "turn_out"): turn_out, ("A", "wo"): wo, ("A", "h1"): h1, ("A", "proj1"): proj1,
                          ("A", "score1"): score1, ("A", "pv1"): pv1, ("A", "elu1"): elu1,
                          ("B", "masks_next"): masks, ("B", "stats"): stats_b, ("B", "norm"): norm_b, ("B", "turn_norm"): turn_norm_b,
                          ("B", "sums2"): sums2, ("B", "factors"): factors, ("B", "weights2"): weights2,
                          ("B", "out2"): out2, ("B", "elu2"): elu2, ("B", "edges3"): edges3, ("B", "values3"): values3,
                          ("B", "store"): store})


_INS = ["x", "adj", "L0_gnn_Wq", "L0_gnn_Wk", "L0_gnn_Wv", "L0_gnn_Wo", "L1_gnn_W", "L1_gnn_b", "L1_gnn_attn",
        "L2_gnn_W", "L2_gnn_a", "L3_gnn_W", "L3_gnn_a"]


def kernel(**inputs):
    import numpy as _np
    import concourse.bacc as _bacc
    from concourse import mybir as _mybir
    from concourse.bass_utils import run_bass_kernel_spmd as _run

    nc = _bacc.Bacc("TRN2", target_bir_lowering=False, num_devices=1)
    arrays, args = {}, []
    for name in _INS:
        a = _np.ascontiguousarray(inputs[name])
        arrays[f"in_{name}"] = a
        args.append(nc.dram_tensor(f"in_{name}", a.shape, _mybir.dt.from_np(a.dtype), kind="ExternalInput").ap())
    args.append(nc.dram_tensor("out_x", (BATCH, N, D), F32, kind="ExternalOutput").ap())
    build(nc, *args)
    r = _run(nc, [arrays], core_ids=[0])
    return r.results[0]["out_x"]
```
